# Optimizing a Trainium2 kernel written in Bass

```python
import numpy as np
import jax
import jax.numpy as jnp

def _softmax(x, axis=-1):
    return jax.nn.softmax(x, axis=axis)

def _gelu(x):
    return jax.nn.gelu(x, approximate=True)

def _silu(x):
    return jax.nn.silu(x)

def _sigmoid(x):
    return jax.nn.sigmoid(x)

def _layernorm(x, axis=-1, eps=1e-05):
    m = jnp.mean(x, axis=axis, keepdims=True)
    v = jnp.var(x, axis=axis, keepdims=True)
    return (x - m) / jnp.sqrt(v + eps)

def _scatter_add(tgt, idx, src, axis=0):
    return tgt.at[idx].add(src)

def _segment_sum(src, seg, n):
    return jax.ops.segment_sum(src, seg, n)
kernel_name = 'mk_perceiver_d1_seqx_r4_945a0f'

def setup_inputs(seed: int=0):
    np.random.seed(seed)
    _w = jnp.asarray

    def _rec_inputs():
        import jax
        import jax.numpy as jnp
        _rk = jax.random.key(seed)
        x = 7.22e-05 + 1 * jax.random.normal(jax.random.fold_in(_rk, 1), (32, 32, 256), jnp.float32)
        _lenS = 32 - jax.random.randint(jax.random.fold_in(_rk, 7), (32,), 0, max(1, 32 // 4) + 1, jnp.int32)
        _lenS2 = 257 - jax.random.randint(jax.random.fold_in(_rk, 8), (32,), 0, max(1, 257 // 4) + 1, jnp.int32)
        _ctx_1024P = jax.random.normal(jax.random.fold_in(_rk, 11), (32, 16, 256), jnp.float32)
        _ctx_1024c = jax.random.dirichlet(jax.random.fold_in(_rk, 511), 0.3 * jnp.ones((16,), jnp.float32), (32, 257))
        _ctx_1024t = jnp.einsum('bsk,bkd->bsd', _ctx_1024c, _ctx_1024P)
        _ctx_1024t = _ctx_1024t * jax.lax.rsqrt(jnp.mean(jnp.square(_ctx_1024t)) + 1e-12) * 0.953939
        ctx_1024 = 4.13588e-05 + 0.999923 * (_ctx_1024t + 0.3 * jax.random.normal(jax.random.fold_in(_rk, 611), (32, 257, 256), jnp.float32))
        return (x, ctx_1024)
    x, ctx_1024 = _rec_inputs()

    def _L0_xattn_setup():
        import jax, jax.numpy as jnp
        import numpy as np
        D_MODEL = 256
        N_HEADS = 16
        HEAD_DIM = 64
        key = jax.random.key(seed)
        ks = jax.random.split(key, 11)
        B, S = (4, 512)
        scale = 1.0 / np.sqrt(D_MODEL)
        return {'query': jax.random.normal(ks[0], (B, S, D_MODEL), jnp.float32), 'key': jax.random.normal(ks[1], (B, S, D_MODEL), jnp.float32), 'value': jax.random.normal(ks[2], (B, S, D_MODEL), jnp.float32), 'Wq': jax.random.normal(ks[3], (D_MODEL, N_HEADS * HEAD_DIM), jnp.float32) * scale, 'bq': jnp.zeros((N_HEADS * HEAD_DIM,), jnp.float32), 'Wk': jax.random.normal(ks[4], (D_MODEL, N_HEADS * HEAD_DIM), jnp.float32) * scale, 'bk': jnp.zeros((N_HEADS * HEAD_DIM,), jnp.float32), 'Wv': jax.random.normal(ks[5], (D_MODEL, N_HEADS * HEAD_DIM), jnp.float32) * scale, 'bv': jnp.zeros((N_HEADS * HEAD_DIM,), jnp.float32), 'Wo': jax.random.normal(ks[6], (N_HEADS * HEAD_DIM, D_MODEL), jnp.float32) * scale, 'bo': jnp.zeros((D_MODEL,), jnp.float32)}
    _L0_xattn_all = _L0_xattn_setup()
    _L0_xattn_in = {k: v for k, v in _L0_xattn_all.items() if k in ('Wq', 'bq', 'Wk', 'bk', 'Wv', 'bv', 'Wo', 'bo')}
    del _L0_xattn_all

    def _L0_attn_setup():
        import jax, jax.numpy as jnp
        import numpy as np
        DT_RANK = 64
        N_STATES = 16

        def selective_scan(u, delta, A, B, C, D):
            dA = jnp.einsum('bld,dn->bldn', delta, A)
            dB_u = jnp.einsum('bld,bld,bln->bldn', delta, u, B)
            dA_shift = jnp.concatenate([dA[:, 1:], jnp.zeros_like(dA[:, :1])], axis=1)
            dA_cumsum = jnp.exp(jnp.flip(jnp.cumsum(jnp.flip(dA_shift, axis=1), axis=1), axis=1))
            xs = jnp.cumsum(dB_u * dA_cumsum, axis=1) / (dA_cumsum + 1e-12)
            y = jnp.einsum('bldn,bln->bld', xs, C)
            return y + u * D
        key = jax.random.key(seed)
        ks = jax.random.split(key, 6)
        b, l, d = (2, 256, 256)
        dt_rank, n = (DT_RANK, N_STATES)
        x = jax.random.normal(ks[0], (b, l, d), dtype=jnp.float32)
        W_x = jax.random.normal(ks[1], (d, dt_rank + 2 * n), dtype=jnp.float32) * (1.0 / np.sqrt(d))
        W_dt = jax.random.normal(ks[2], (dt_rank, d), dtype=jnp.float32) * (1.0 / np.sqrt(dt_rank))
        b_dt = jnp.zeros((d,), dtype=jnp.float32)
        A_log = jnp.log(jnp.tile(jnp.arange(1, n + 1, dtype=jnp.float32)[None, :], (d, 1)))
        D = jnp.ones((d,), dtype=jnp.float32)
        W_out = jax.random.normal(ks[3], (d, d), dtype=jnp.float32) * (1.0 / np.sqrt(d))
        b_out = jnp.zeros((d,), dtype=jnp.float32)
        return {'x': x, 'W_x': W_x, 'W_dt': W_dt, 'b_dt': b_dt, 'A_log': A_log, 'D': D, 'W_out': W_out, 'b_out': b_out}
    _L0_attn_all = _L0_attn_setup()
    _L0_attn_in = {k: v for k, v in _L0_attn_all.items() if k in ('W_x', 'W_dt', 'b_dt', 'A_log', 'D', 'W_out', 'b_out')}
    del _L0_attn_all

    def _L0_ffn_setup():
        import jax, jax.numpy as jnp
        import numpy as np
        import math
        D_IN = 256
        FEATURES = (1024, 1024, 256)
        BATCH, SEQ = (8, 512)

        def _conn_dense(kernel_bool, x):
            w = jnp.where(kernel_bool, jnp.float32(1.0), jnp.float32(-1.0))
            return x @ w
        key = jax.random.key(seed)
        kx, kk0, kk1, kk2 = jax.random.split(key, 4)
        x = jax.random.normal(kx, (BATCH, SEQ, D_IN), dtype=jnp.float32)
        k0 = jax.random.randint(kk0, (2 * D_IN, FEATURES[0]), 0, 2).astype(jnp.bool_)
        k1 = jax.random.randint(kk1, (FEATURES[0], FEATURES[1]), 0, 2).astype(jnp.bool_)
        k2 = jax.random.randint(kk2, (FEATURES[1], FEATURES[2]), 0, 2).astype(jnp.bool_)
        s0 = jnp.asarray(1.0 / math.sqrt(2 * D_IN), dtype=jnp.float32)
        s1 = jnp.asarray(1.0 / math.sqrt(FEATURES[0]), dtype=jnp.float32)
        s2 = jnp.asarray(1.0 / math.sqrt(FEATURES[1]), dtype=jnp.float32)
        return {'x': x, 'k0': k0, 'k1': k1, 'k2': k2, 's0': s0, 's1': s1, 's2': s2}
    _L0_ffn_all = _L0_ffn_setup()
    _L0_ffn_in = {k: v for k, v in _L0_ffn_all.items() if k in ('k0', 'k1', 'k2', 's0', 's1', 's2')}
    del _L0_ffn_all
    return {'x': x, 'ctx_1024': ctx_1024, 'L0_xattn_Wq': _L0_xattn_in['Wq'], 'L0_xattn_bq': _L0_xattn_in['bq'], 'L0_xattn_Wk': _L0_xattn_in['Wk'], 'L0_xattn_bk': _L0_xattn_in['bk'], 'L0_xattn_Wv': _L0_xattn_in['Wv'], 'L0_xattn_bv': _L0_xattn_in['bv'], 'L0_xattn_Wo': _L0_xattn_in['Wo'], 'L0_xattn_bo': _L0_xattn_in['bo'], 'L0_attn_W_x': _L0_attn_in['W_x'], 'L0_attn_W_dt': _L0_attn_in['W_dt'], 'L0_attn_b_dt': _L0_attn_in['b_dt'], 'L0_attn_A_log': _L0_attn_in['A_log'], 'L0_attn_D': _L0_attn_in['D'], 'L0_attn_W_out': _L0_attn_in['W_out'], 'L0_attn_b_out': _L0_attn_in['b_out'], 'L0_ffn_k0': _L0_ffn_in['k0'], 'L0_ffn_k1': _L0_ffn_in['k1'], 'L0_ffn_k2': _L0_ffn_in['k2'], 'L0_ffn_s0': _L0_ffn_in['s0'], 'L0_ffn_s1': _L0_ffn_in['s1'], 'L0_ffn_s2': _L0_ffn_in['s2']}

def reference(x, ctx_1024, L0_xattn_Wq, L0_xattn_bq, L0_xattn_Wk, L0_xattn_bk, L0_xattn_Wv, L0_xattn_bv, L0_xattn_Wo, L0_xattn_bo, L0_attn_W_x, L0_attn_W_dt, L0_attn_b_dt, L0_attn_A_log, L0_attn_D, L0_attn_W_out, L0_attn_b_out, L0_ffn_k0, L0_ffn_k1, L0_ffn_k2, L0_ffn_s0, L0_ffn_s1, L0_ffn_s2):
    import jax
    import jax.numpy as jnp

    def _L0_xattn_ref(query, key, value, Wq, bq, Wk, bk, Wv, bv, Wo, bo):
        import jax, jax.numpy as jnp
        import numpy as np
        D_MODEL = 256
        N_HEADS = 16
        HEAD_DIM = 64
        B, Sq, _ = query.shape
        Sk = key.shape[1]
        q = (query @ Wq + bq).reshape(B, Sq, N_HEADS, HEAD_DIM).transpose(0, 2, 1, 3)
        k = (key @ Wk + bk).reshape(B, Sk, N_HEADS, HEAD_DIM).transpose(0, 2, 1, 3)
        v = (value @ Wv + bv).reshape(B, Sk, N_HEADS, HEAD_DIM).transpose(0, 2, 1, 3)
        scores = jnp.einsum('bhqd,bhkd->bhqk', q, k) / np.sqrt(HEAD_DIM).astype(np.float32)
        probs = jax.nn.softmax(scores, axis=-1)
        z = jnp.einsum('bhqk,bhkd->bhqd', probs, v)
        z = z.transpose(0, 2, 1, 3).reshape(B, Sq, N_HEADS * HEAD_DIM)
        return z @ Wo + bo

    def _L0_attn_ref(x, W_x, W_dt, b_dt, A_log, D, W_out, b_out):
        import jax, jax.numpy as jnp
        import numpy as np
        DT_RANK = 64
        N_STATES = 16

        def selective_scan(u, delta, A, B, C, D):
            dA = jnp.einsum('bld,dn->bldn', delta, A)
            dB_u = jnp.einsum('bld,bld,bln->bldn', delta, u, B)
            dA_shift = jnp.concatenate([dA[:, 1:], jnp.zeros_like(dA[:, :1])], axis=1)
            dA_cumsum = jnp.exp(jnp.flip(jnp.cumsum(jnp.flip(dA_shift, axis=1), axis=1), axis=1))
            xs = jnp.cumsum(dB_u * dA_cumsum, axis=1) / (dA_cumsum + 1e-12)
            y = jnp.einsum('bldn,bln->bld', xs, C)
            return y + u * D
        n = A_log.shape[1]
        A = -jnp.exp(A_log)
        x_dbl = jnp.einsum('bld,de->ble', x, W_x)
        delta = x_dbl[..., :DT_RANK]
        B = x_dbl[..., DT_RANK:DT_RANK + n]
        C = x_dbl[..., DT_RANK + n:]
        delta = jax.nn.softplus(jnp.einsum('blr,rd->bld', delta, W_dt) + b_dt)
        y = selective_scan(x, delta, A, B, C, D)
        return jnp.einsum('bld,de->ble', y, W_out) + b_out

    def _L0_ffn_ref(x, k0, k1, k2, s0, s1, s2):
        import jax, jax.numpy as jnp
        import numpy as np
        import math
        D_IN = 256
        FEATURES = (1024, 1024, 256)
        BATCH, SEQ = (8, 512)

        def _conn_dense(kernel_bool, x):
            w = jnp.where(kernel_bool, jnp.float32(1.0), jnp.float32(-1.0))
            return x @ w
        h = jnp.concatenate([x, -x], axis=-1)
        h = s0 * _conn_dense(k0, h)
        h = jax.nn.relu(h) * 2
        h = s1 * _conn_dense(k1, h)
        h = jax.nn.relu(h) * 2
        h = s2 * _conn_dense(k2, h)
        return h
    x = x + _L0_xattn_ref(_layernorm(x, axis=-1), ctx_1024, ctx_1024, L0_xattn_Wq, L0_xattn_bq, L0_xattn_Wk, L0_xattn_bk, L0_xattn_Wv, L0_xattn_bv, L0_xattn_Wo, L0_xattn_bo)
    x = x + _L0_attn_ref(_layernorm(x, axis=-1), L0_attn_W_x, L0_attn_W_dt, L0_attn_b_dt, L0_attn_A_log, L0_attn_D, L0_attn_W_out, L0_attn_b_out)
    x = x + _L0_ffn_ref(_layernorm(x, axis=-1), L0_ffn_k0, L0_ffn_k1, L0_ffn_k2, L0_ffn_s0, L0_ffn_s1, L0_ffn_s2)
    return x

_drawn_inputs = setup_inputs


def setup_inputs(seed=0):
    import zlib

    import numpy as np

    out = dict(_drawn_inputs(seed))
    spreads = {'L0_xattn_bq': (0.0, 0.1),
     'L0_xattn_bk': (0.0, 0.1),
     'L0_xattn_bv': (0.0, 0.1),
     'L0_xattn_bo': (0.0, 0.1),
     'L0_attn_b_dt': (0.0, 0.1),
     'L0_attn_D': (1.0, 0.2),
     'L0_attn_b_out': (0.0, 0.1)}
    factors = {}
    for name, (base, spread) in spreads.items():
        noise = np.random.default_rng([zlib.crc32(name.encode()), seed]).standard_normal(out[name].shape)
        drawn = base * np.exp(spread * noise) if base else spread * noise
        out[name] = jnp.asarray(drawn.astype(out[name].dtype))
    for name, factor in factors.items():
        out[name] = (out[name] * factor).astype(out[name].dtype)
    return out
```

```python
from contextlib import ExitStack

import numpy as np

import concourse.bass as bass
from concourse import mybir

ALU = mybir.AluOpType
ACT = mybir.ActivationFunctionType
AX = mybir.AxisListType
F32 = mybir.dt.float32
F32R = mybir.dt.float32r
U8 = mybir.dt.uint8

P = 128
B, L, D = 32, 32, 256
SK = 257
H, E = 16, 64
NS, RANK = 16, 64
TB = P // L
T = B // TB
DC = D // P
IC = H * E // P
UNITS = 2 * TB
HU = H // 2
F = 1024
FC = F // P
EPS = 1e-5
SCAN_EPS = 1e-12

ATTN_HEAD = ["ctxT0", "q0", "q1", "qk0", "qk1", "qk2", "qk3"]
LAG_HEAD = ["oT0", "oT1", "last", "wo"]
STEPS = {
    0: ([], ["xnT"]), 1: (["ctxT1"], ["dTBC"]), 2: (["dt"], ["R"]), 3: (["ctxT2"], ["num0"]),
    4: (["num1"], ["num2"]), 5: (["ctxT3", "num3"], ["num4"]), 6: (["num5"], ["num6"]),
    7: (["num7"], ["yT", "out"]),
}
LAGGED = {"xnT", "dTBC", "dt", "R", "yT", "out"} | {f"num{i}" for i in range(8)}


def slot_order(attn, lag):
    names = (["ctxT0", "q0", "q1"] if attn else [])
    names += (["qk0", "qk1", "qk2", "qk3"] if attn else []) + (LAG_HEAD if lag else [])
    names += (["qk4", "qk5", "qk6", "qk7"] if attn else [])
    for s in range(UNITS):
        for part in STEPS[s]:
            names += [n for n in part if (lag if n in LAGGED else attn)]
    return names


SETUP = (["wk0", "wk1", "wk2", "wk3", "x0", "x1", "x2", "x3", "lastc", "vl"] + [f"vo{i}" for i in range(8)]
         + ["bias", "alog"] + [f"a{i}" for i in range(8)])
FIRST, BODY, LAST = slot_order(True, False), slot_order(True, True), slot_order(False, True)
assert len(BODY) % 2 == 0


class Slots:

    def __init__(self, section, t=0):
        self.names = {"setup": SETUP, "first": FIRST, "body": BODY, "last": LAST}[section]
        self.base = {"setup": 0, "first": len(SETUP), "body": len(SETUP) + len(FIRST),
                     "last": len(SETUP) + len(FIRST) + (T - 1) * len(BODY)}[section]
        self.more = (t - 1) * (len(BODY) // 2) if section == "body" else 0

    def at(self, name):
        g = self.base + self.names.index(name)
        return g % 2, g // 2 + self.more


class Chain:

    def __init__(self, sem, eng):
        self.sem, self.eng, self.base, self.k, self.more = sem, eng, 0, 0, 0

    def __call__(self, ins):
        ins.then_inc(self.sem, 1)
        self.k += 1
        self.eng.wait_ge(self.sem, self.base + self.k + self.more)

    def enter(self, t, per):
        self.base, self.k, self.per = self.base + self.k, 0, per
        self.more = (t - 1) * per

    def leave(self, times):
        assert self.k == self.per, f"the loop has {self.k} links"
        self.base, self.k, self.more = self.base + self.per * times, 0, 0


CONSTS = {"ident": P, "tri_incl": P, "tri_after": P, "head_sel": TB * H, "lat_sel": L, "own": UNITS * 2}


def host_constants():
    i = np.arange(P)
    same = i[:, None] // L == i[None, :] // L
    ident = np.eye(P)
    incl = same & (i[:, None] <= i[None, :])
    after = same & (i[:, None] > i[None, :])
    bh = np.arange(TB * H)
    head_sel = (i[:, None] // L) == (bh[None, :] % H) % 4
    lat_sel = (i[:, None] % L) == np.arange(L)[None, :]
    bg = np.arange(UNITS * 2)
    own = np.zeros((P, UNITS * 2))
    own[:TB * H] = (bh[:, None] // H == bg[None, :] // 4) & ((bh[:, None] % H) // 4 == bg[None, :] % 4)
    return np.concatenate([ident, incl, after, head_sel, lat_sel, own], axis=1).astype(np.float32)


def perceiver_block(nc, consts, x, ctx_1024, L0_xattn_Wq, L0_xattn_bq, L0_xattn_Wk, L0_xattn_bk, L0_xattn_Wv,
                    L0_xattn_bv, L0_xattn_Wo, L0_xattn_bo, L0_attn_W_x, L0_attn_W_dt, L0_attn_b_dt,
                    L0_attn_A_log, L0_attn_D, L0_attn_W_out, L0_attn_b_out, L0_ffn_k0, L0_ffn_k1,
                    L0_ffn_k2, L0_ffn_s0, L0_ffn_s1, L0_ffn_s2, out):
    with ExitStack() as stack:
        x_all = stack.enter_context(nc.sbuf_tensor("x_all", [P, T, D], F32))
        k0 = stack.enter_context(nc.sbuf_tensor("k0", [P, 2 * DC, F], U8))
        k1 = stack.enter_context(nc.sbuf_tensor("k1", [P, FC, F], U8))
        k2 = stack.enter_context(nc.sbuf_tensor("k2", [P, FC, D], U8))
        s_cols = stack.enter_context(nc.sbuf_tensor("s_cols", [P, 3], F32))
        cst = stack.enter_context(nc.sbuf_tensor("cst", [P, sum(CONSTS.values())], F32))
        s_mlp_in = stack.enter_context(nc.semaphore("mlp_in"))
        mlp = (k0, k1, k2, s_cols, s_mlp_in)
        attention_and_scan(nc, cst, consts, x, ctx_1024, L0_xattn_Wq, L0_xattn_bq, L0_xattn_Wk, L0_xattn_Wv,
                           L0_xattn_bv, L0_xattn_Wo, L0_xattn_bo, L0_attn_W_x, L0_attn_W_dt, L0_attn_b_dt,
                           L0_attn_A_log, L0_attn_D, L0_attn_W_out, L0_attn_b_out, x_all, mlp,
                           (L0_ffn_k0, L0_ffn_k1, L0_ffn_k2, L0_ffn_s0, L0_ffn_s1, L0_ffn_s2))
        sign_mlp(nc, cst, x_all, mlp, out)


def row(vector):
    return vector.rearrange("(a d) -> a d", a=1)


def spread(ap, axis, n):
    wide = ap.unsqueeze(axis)
    shape = list(wide.shape)
    shape[axis] = n
    return wide.to_broadcast(shape)


def chunks(matrix):
    return matrix.rearrange("(c p) n -> p c n", p=P)


def attention_and_scan(nc, cst, consts, x, ctx, Wq, bq, Wk, Wv, bv, Wo, bo, W_x, W_dt, b_dt, A_log, D_skip, W_out,
                       b_out, x_all, mlp, mlp_dram):
    x_rows = x.rearrange("(t b) l d -> (b l) t d", b=TB)

    with ExitStack() as stack:
        def sb(name, shape, dt=F32):
            return stack.enter_context(nc.sbuf_tensor(name, shape, dt))

        def sem(name):
            return stack.enter_context(nc.semaphore(name))

        masks, c = {}, 0
        for name, n in CONSTS.items():
            masks[name], c = cst[:, c:c + n], c + n
        ident, tri_incl, tri_after = masks["ident"], masks["tri_incl"], masks["tri_after"]
        head_sel, lat_sel, own = masks["head_sel"], masks["lat_sel"], masks["own"]

        xn1T = sb("xn1T", [P, DC, T, P])
        wq = sb("wq", [P, DC, H * E])
        wkT = sb("wkT", [P, H, D])
        wv = sb("wv", [P, DC, H * E])
        wo = sb("wo", [P, IC, D])
        bqT = sb("bqT", [P, IC])
        last_vo = sb("last_vo", [TB * H, T, D])
        last_ctxT = sb("last_ctxT", [P, DC, B])
        wx = sb("wx", [P, DC, RANK + 2 * NS])
        wdt = sb("wdt", [RANK + 1, D])
        wout = sb("wout", [P, DC, D])
        bout = sb("bout", [P, D])
        dskip = sb("dskip", [P, D])
        a_all = sb("a_all", [P, NS, D])
        eps_col = sb("eps_col", [P, 2])
        bvT = sb("bvT", [P, IC])
        bo_row = sb("bo_row", [1, D])
        ones_row = sb("ones_row", [1, P])
        a_log = sb("a_log", [P, DC, NS])
        stats1 = sb("stats1", [P, T, 6])
        mv1 = sb("mv1", [P, T, 2])
        lnv1 = sb("lnv1", [P, T])
        rstd1 = sb("rstd1", [P, T])

        ctx_t = [sb(f"ctx{i}", [P, DC, D]) for i in range(TB)]
        ctxT = [sb(f"ctxT{i}", [P, DC, SK]) for i in range(2)]
        qT = sb("qT", [P, IC, P])
        qkT = sb("qkT", [P, DC, H // 4, TB, 4 * L])
        probs = [sb(f"probs{i}", [P, 2, SK]) for i in range(2)]
        pT = [sb(f"pT{i}", [P, DC, 2 * P]) for i in range(2)]
        zT = sb("zT", [P, DC, H, P])
        oT = sb("oT", [P, IC, P])
        neg_max = sb("neg_max", [P, 2, 2])
        row_sum = sb("row_sum", [P, 2, 2])
        inv_sum = sb("inv_sum", [P, 2, 2])
        last_p = sb("last_p", [P, 4 * TB, L])
        last_pm = sb("last_pm", [TB * H, TB, 4, L])
        last_pT = sb("last_pT", [TB * H, TB, L])

        x1 = sb("x1", [P, D])
        x1b = sb("x1b", [P, D])
        stats2 = sb("stats2", [P, 6])
        mv2 = sb("mv2", [P, 2])
        lnv2 = sb("lnv2", [P, 1])
        rstd2 = sb("rstd2", [P, 1])
        xn2 = sb("xn2", [P, D])
        xn2T = sb("xn2T", [P, DC, P])
        dT = sb("dT", [RANK + 1, P])
        bc = sb("bc", [P, 2 * NS])
        sp_x = sb("sp_x", [P, D])
        sp_e = sb("sp_e", [P, D])
        delta = sb("delta", [P, D])
        du = sb("du", [P, D])
        later = sb("later", [P, D])
        tri_b = sb("tri_b", [P, 2, 4, P])
        scan_buf = sb("scan_buf", [P, 3, 2, 4, D])
        decay, inv_decay, driven = (scan_buf[:, i] for i in range(3))
        y = sb("y", [P, D])
        y_part = sp_e
        yT = xn2T

        flat = lambda a: a[:].rearrange("p a b c -> p (a b c)")
        wk_raw = qkT[:].rearrange("p c g b n -> p (c g b n)")[:, 0:DC * H * E].rearrange("p (c n) -> p c n", c=DC)
        spare = qkT[:].rearrange("p c g b n -> p (c g b n)")[:, DC * H * E:]
        last_rows = spare[0:B, 0:D]
        a_T = spare[0:NS, D:2 * D]
        last_vT = spare[:, 2 * D:2 * D + 2 * IC * B].rearrange("p (c e b) -> p c e b", c=IC, e=2)
        xn1 = flat(zT)[:, 0:T * D].rearrange("p (t d) -> p t d", t=T)
        state_sel = flat(zT)[0:NS, T * D:T * D + NS * P].rearrange("p (n m) -> p n m", n=NS)
        vo_rows = scan_buf[0:B].rearrange("p a b c d -> p (a b c d)")[:, 0:H * D].rearrange("p (h d) -> p h d", h=H)
        bv_rep = tri_b[:].rearrange("p a b m -> p (a b) m")

        ps_s = stack.enter_context(nc.psum_tensor("ps_s", [P, 2, 2, 512], F32))
        ps_t = stack.enter_context(nc.psum_tensor("ps_t", [P, DC, 256], F32))
        ps_z = stack.enter_context(nc.psum_tensor("ps_z", [P, DC, 256], F32))
        ps_m = [stack.enter_context(nc.psum_tensor(f"ps_m{i}", [P, 512], F32)) for i in range(2)]

        s_cst, s_x, s_wq, s_wk, s_wv, s_wo = (sem(n) for n in ("consts_in", "x_in", "wq_in", "wk_in", "wv_in", "wo_in"))
        s_small, s_lastc, s_alog, s_scanw, s_rows, s_vo = (
            sem(n) for n in ("small_in", "last_ctx_in", "a_log_in", "scan_weights_in", "scan_rows_in", "last_vo_placed"))
        s_ctx = [sem(f"ctx{i}_in") for i in range(TB)]
        s_sel, s_zero, s_bvrep, s_mv1, s_rstd1, s_xn1 = (
            sem(n) for n in ("state_sel_ready", "zeros_ready", "bv_rep_ready", "variance1_ready", "rstd1_ready",
                             "xn1_ready"))
        filled = [sem("bank0_filled"), sem("bank1_filled")]
        emptied = [sem("bank0_emptied"), sem("bank1_emptied")]
        s_scores, s_negmax, s_exp, s_inv, s_probs = (
            sem(n) for n in ("scores_ready", "neg_max_ready", "exp_done", "inv_sum_ready", "probs_ready"))
        s_tp, s_pT, s_z, s_zT, s_lastT = (
            sem(n) for n in ("probs_transposed", "pT_ready", "z_summed", "zT_ready", "last_pT_ready"))
        s_mv2, s_rstd2, s_xn2, s_negabs, s_spl, s_delta, s_du, s_y0, s_x1b = (
            sem(n) for n in ("variance2_ready", "rstd2_ready", "xn2_ready", "neg_abs_ready", "softplus_ln_ready",
                             "delta_ready", "du_ready", "skip_ready", "x1b_ready"))
        s_trib, s_arg, s_decay, s_inv_decay, s_driven, s_scanned = (
            sem(n) for n in ("tri_b_ready", "decay_log_ready", "decay_ready", "inv_decay_ready", "driven_ready",
                             "chunk_scanned"))
        s_dve, s_act, s_pool = sem("vector_chain"), sem("scalar_chain"), sem("gpsimd_chain")

        def wait_filled(eng, sl, name):
            bank, before = sl.at(name)
            eng.wait_ge(filled[bank], before + 1)
            return ps_m[bank], emptied[bank]

        def wait_copied(eng, sl, *names):
            for name in names:
                bank, before = sl.at(name)
                eng.wait_ge(emptied[bank], before + 1)

        def unit(t, u):
            return t * UNITS + u

        block = stack.enter_context(nc.Block())

        @block.sync
        def _(sp):
            k0, k1, k2, s_cols, s_mlp_in = mlp
            sp.dma_start(cst[:], consts).then_inc(s_cst, 16)
            sp.dma_start(wk_raw, chunks(Wk)).then_inc(s_wk, 16)
            sp.dma_start(x_all[:], x_rows).then_inc(s_x, 16)
            sp.dma_start(wv[:], chunks(Wv)).then_inc(s_wv, 16)
            sp.dma_start(wo[:], chunks(Wo)).then_inc(s_wo, 16)
            sp.dma_start(wq[:], chunks(Wq)).then_inc(s_wq, 16)
            for b in range(TB):
                sp.dma_start(ctx_t[b][:], ctx[b, 0:2 * P, :].rearrange("(k p) d -> p k d", p=P)).then_inc(s_ctx[b], 16)
            sp.dma_start(wx[:], chunks(W_x)).then_inc(s_scanw, 16)
            sp.dma_start(wdt[0:RANK, :], W_dt).then_inc(s_scanw, 16)
            sp.dma_start(wdt[RANK:RANK + 1, :], row(b_dt)).then_inc(s_scanw, 16)
            sp.dma_start(wout[:], chunks(W_out)).then_inc(s_scanw, 16)
            for dst, src in ((k0, mlp_dram[0]), (k1, mlp_dram[1]), (k2, mlp_dram[2])):
                sp.dma_start(dst[:], chunks(src)).then_inc(s_mlp_in, 16)
            for i in range(3):
                sp.dma_start(s_cols[:, i:i + 1], row(mlp_dram[3 + i]).partition_broadcast(P)).then_inc(s_mlp_in, 16)
            wait_copied(sp, Slots("setup"), "vo6", "vo7")
            for t in range(T):
                sp.dma_start(last_vo[:, t, :], vo_rows[TB * t:TB * t + TB]).then_inc(s_vo, 16)
            with sp.Fori(1, T) as t:
                for b in range(TB):
                    sp.wait_ge(s_z, unit(t - 1, 2 * b) + 2)
                    sp.dma_start(ctx_t[b][:], ctx[t * TB + b, 0:2 * P, :].rearrange("(k p) d -> p k d", p=P)) \
                        .then_inc(s_ctx[b], 16)

        @block.gpsimd
        def _(pool):
            pool.dma_start(last_rows, ctx[:, SK - 1, :]).then_inc(s_lastc, 16)
            pool.dma_start(a_log[:], chunks(A_log)).then_inc(s_alog, 16)
            pool.dma_start(bqT[:], bq.rearrange("(c p) -> p c", p=P), allow_slow_non_contiguous=True).then_inc(s_small, 16)
            pool.dma_start(bvT[:], bv.rearrange("(c p) -> p c", p=P), allow_slow_non_contiguous=True).then_inc(s_small, 16)
            pool.dma_start(bo_row[:], row(bo)).then_inc(s_small, 16)
            pool.dma_start(bout[:], row(b_out).partition_broadcast(P)).then_inc(s_rows, 16)
            pool.dma_start(dskip[:], row(D_skip).partition_broadcast(P)).then_inc(s_rows, 16)
            pool.memset(wkT[:], 0.0)
            pool.memset(last_vT, 0.0)
            pool.memset(dT[:], 1.0)
            pool.memset(eps_col[:, 0:1], EPS)
            pool.memset(eps_col[:, 1:2], SCAN_EPS)
            pool.memset(ones_row[:], 1.0).then_inc(s_zero, 1)
            pool.wait_ge(s_cst, 16)
            pool.tensor_copy(state_sel, spread(ident[0:NS, 0:NS], 2, P)).then_inc(s_sel, 1)
            pool.wait_ge(s_small, 48)
            pool.tensor_copy(bv_rep, spread(bvT[:], 2, P)).then_inc(s_bvrep, 1)

            def normalise(t, u, last_slot):
                g = unit(t, u)
                pr = probs[u % 2]
                pool.wait_ge(s_inv, g + 1)
                pool.tensor_tensor(pr[:], pr[:], spread(inv_sum[:, u % 2, :], 2, SK), ALU.mult) \
                    .then_inc(s_pool, 1)
                if last_slot is not None:
                    bank, fills = last_slot
                    pool.wait_ge(filled[bank], fills + 1)
                pool.wait_ge(s_pool, g + 1)
                pool.tensor_tensor(last_p[:, 2 * u:2 * u + 2, :], pr[:, :, SK - 1:SK].to_broadcast([P, 2, L]),
                                   spread(lat_sel, 1, 2), ALU.mult).then_inc(s_probs, 1)

            def prepare_chunk(sl, v, c):
                if c >= 2:
                    pool.wait_ge(s_scanned, v * 4 + c - 1)
                if c == 0:
                    wait_copied(pool, sl, "dTBC")
                pool.tensor_tensor(tri_b[:, c % 2], spread(tri_incl, 1, 4),
                                   spread(bc[:, 4 * c:4 * c + 4], 2, P), ALU.mult).then_inc(s_trib, 1)
                if c == 0:
                    wait_copied(pool, sl, "R")
                pool.tensor_tensor(decay[:, c % 2], a_all[:, 4 * c:4 * c + 4, :],
                                   spread(later[:], 1, 4), ALU.mult).then_inc(s_arg, 1)

            def tile(section, t, v):
                sl = Slots(section, t)
                if v is not None:
                    pool.wait_ge(s_xn2, v + 1)
                    pool.tensor_tensor(y[:], xn2[:], dskip[:], ALU.mult).then_inc(s_y0, 1)
                for u in range(UNITS):
                    if t is not None:
                        normalise(t, u, sl.at("last") if v is not None and u == 0 else None)
                    if v is not None and u == 1:
                        pool.wait_ge(s_delta, v + 1)
                        pool.tensor_tensor(du[:], delta[:], xn2[:], ALU.mult).then_inc(s_du, 1)
                    if v is not None and 2 <= u < 6:
                        prepare_chunk(sl, v, u - 2)

            tile("first", 0, None)
            wait_copied(pool, Slots("setup"), "a6", "a7")
            pool.wait_ge(s_rows, 32)
            with pool.Fori(1, T) as t:
                tile("body", t, t - 1)
            tile("last", None, T - 1)

        @block.tensor
        def _(pe):
            def fill(sl, name):
                bank, before = sl.at(name)
                if not (isinstance(before, int) and before == 0):
                    pe.wait_ge(emptied[bank], before)
                return ps_m[bank], filled[bank]

            def two(dst, lhs, rhs):
                pe.matmul(dst, lhs(0), rhs(0), start=True, stop=False)
                return pe.matmul(dst, lhs(1), rhs(1), start=False, stop=True)

            def setup():
                sl = Slots("setup")
                pe.wait_ge(s_cst, 16)
                pe.wait_ge(s_wk, 16)
                for i in range(4):
                    ps, done = fill(sl, f"wk{i}")
                    for j in range(2):
                        for c in range(DC):
                            last = pe.transpose(ps[:, (2 * j + c) * P:(2 * j + c + 1) * P],
                                                wk_raw[:, c, (2 * i + j) * P:(2 * i + j + 1) * P], ident)
                    last.then_inc(done, 1)
                for i in range(4):
                    pe.wait_ge(s_xn1, 2 * i + 2)
                    ps, done = fill(sl, f"x{i}")
                    for j in range(2):
                        for c in range(DC):
                            last = pe.transpose(ps[:, (2 * c + j) * P:(2 * c + j + 1) * P],
                                                xn1[:, 2 * i + j, c * P:(c + 1) * P], ident)
                    last.then_inc(done, 1)
                pe.wait_ge(s_lastc, 16)
                ps, done = fill(sl, "lastc")
                for c in range(DC):
                    last = pe.transpose(ps[:, c * B:(c + 1) * B], last_rows[:, c * P:(c + 1) * P], ident[0:B, 0:B])
                last.then_inc(done, 1)
                pe.wait_ge(s_wv, 16)
                wait_copied(pe, sl, "lastc")
                ps, done = fill(sl, "vl")
                for c in range(IC):
                    last = two(ps[:, c * B:(c + 1) * B], lambda k: wv[:, k, c * P:(c + 1) * P],
                               lambda k: last_ctxT[:, k, :])
                last.then_inc(done, 1)
                pe.wait_ge(s_wo, 16)
                wait_copied(pe, sl, "vl")
                for c in range(IC):
                    ps, done = fill(sl, f"vo{c}")
                    for j in range(2):
                        last = pe.matmul(ps[0:B, j * D:(j + 1) * D], last_vT[:, c, j, :], wo[:, c, :], start=True, stop=True)
                    last.then_inc(done, 1)
                pe.wait_ge(s_bvrep, 1)
                ps, done = fill(sl, "bias")
                for c in range(IC):
                    pe.matmul(ps[:, 0:D], bv_rep[:, c, :], wo[:, c, :], start=(c == 0), stop=False)
                pe.matmul(ps[:, 0:D], ones_row[:], bo_row[:], start=False, stop=True).then_inc(done, 1)
                pe.wait_ge(s_alog, 16)
                ps, done = fill(sl, "alog")
                for c in range(DC):
                    last = pe.transpose(ps[0:NS, c * P:(c + 1) * P], a_log[:, c, :], ident)
                last.then_inc(done, 1)
                pe.wait_ge(s_sel, 1)
                wait_copied(pe, sl, "alog")
                for i in range(8):
                    ps, done = fill(sl, f"a{i}")
                    for j in range(2):
                        last = pe.matmul(ps[:, j * D:(j + 1) * D], state_sel[:, 2 * i + j, :], a_T,
                                         start=True, stop=True)
                    last.then_inc(done, 1)

            def context_transposes(sl, t, b):
                pe.wait_ge(s_ctx[b], (t + 1) * 16)
                ps, done = fill(sl, f"ctxT{b}")
                for k in range(DC):
                    for c in range(DC):
                        last = pe.transpose(ps[:, (2 * c + k) * P:(2 * c + k + 1) * P],
                                            ctx_t[b][:, k, c * P:(c + 1) * P], ident)
                last.then_inc(done, 1)

            def queries(sl, t):
                for i in range(2):
                    ps, done = fill(sl, f"q{i}")
                    for j in range(4):
                        c = 4 * i + j
                        last = two(ps[:, j * P:(j + 1) * P], lambda k: wq[:, k, c * P:(c + 1) * P],
                                   lambda k: xn1T[:, k, t, :])
                    last.then_inc(done, 1)

            def query_keys(sl, t, i):
                if i % 4 == 0:
                    wait_copied(pe, sl, f"q{i // 4}")
                ps, done = fill(sl, f"qk{i}")
                for j in range(2):
                    for c in range(DC):
                        dst = ps[:, 2 * c * P:2 * (c + 1) * P].rearrange("p (b j q) -> p b j q", b=TB, j=2)[:, :, j, :]
                        last = pe.matmul(dst, wkT[:, 2 * i + j, c * P:(c + 1) * P],
                                         qT[:, i, :].rearrange("p (b q) -> p b q", b=TB), start=True, stop=True)
                last.then_inc(done, 1)

            def scores(sl, t, u):
                g, b = unit(t, u), u // 2
                if u == 0:
                    wait_copied(pe, sl, "qk6", "qk7")
                if u % 2 == 0:
                    wait_copied(pe, sl, f"ctxT{b}")
                if not isinstance(g, int) or g >= 2:
                    pe.wait_ge(s_exp, g - 1)
                for gi in range(2):
                    last = two(ps_s[:, u % 2, gi, 0:SK], lambda k: qkT[:, k, 2 * (u % 2) + gi, b, :],
                               lambda k: ctxT[b % 2][:, k, :])
                last.then_inc(s_scores, 1)

            def probs_transposes(t, u):
                g = unit(t, u)
                pe.wait_ge(s_probs, g + 1)
                if not isinstance(g, int) or g >= 1:
                    pe.wait_ge(s_pT, g)
                for k in range(DC):
                    for gi in range(2):
                        last = pe.transpose(ps_t[:, k, gi * P:(gi + 1) * P],
                                            probs[u % 2][:, gi, k * P:(k + 1) * P], ident)
                last.then_inc(s_tp, 1)

            def weighted_context(t, u):
                g, b = unit(t, u), u // 2
                pe.wait_ge(s_pT, g + 1)
                if not isinstance(g, int) or g >= 1:
                    pe.wait_ge(s_zT, g)
                for c in range(DC):
                    last = two(ps_z[:, c, :], lambda k: ctx_t[b][:, k, c * P:(c + 1) * P], lambda k: pT[u % 2][:, k, :])
                last.then_inc(s_z, 1)

            def outputs(sl, v):
                pe.wait_ge(s_zT, (v + 1) * UNITS)
                for i in range(2):
                    ps, done = fill(sl, f"oT{i}")
                    for j in range(4):
                        c = 4 * i + j
                        for e in range(2):
                            h = 2 * c + e
                            last = two(ps[e * E:(e + 1) * E, j * P:(j + 1) * P],
                                       lambda k: wv[:, k, h * E:(h + 1) * E], lambda k: zT[:, k, h, :])
                    last.then_inc(done, 1)
                ps, done = fill(sl, "last")
                pe.matmul(ps[0:TB * H, :], head_sel, last_p[:], start=True, stop=True).then_inc(done, 1)
                ps, done = fill(sl, "wo")
                for c in range(IC):
                    if c % 4 == 0:
                        wait_copied(pe, sl, f"oT{c // 4}")
                    pe.matmul(ps[:, 0:D], oT[:, c, :], wo[:, c, :], start=(c == 0), stop=False)
                pe.wait_ge(s_lastT, v + 1)
                pe.matmul(ps[:, 0:D], last_pT[:], last_vo[:, v, :], start=False, stop=True).then_inc(done, 1)

            def scan_slot(sl, v, name):
                if name == "xnT":
                    pe.wait_ge(s_xn2, v + 1)
                    ps, done = fill(sl, name)
                    for c in range(DC):
                        last = pe.transpose(ps[:, c * P:(c + 1) * P], xn2[:, c * P:(c + 1) * P], ident)
                elif name == "dTBC":
                    wait_copied(pe, sl, "xnT")
                    ps, done = fill(sl, name)
                    two(ps[0:RANK, 0:P], lambda k: wx[:, k, 0:RANK], lambda k: xn2T[:, k, :])
                    last = two(ps[:, P:P + 2 * NS], lambda k: xn2T[:, k, :], lambda k: wx[:, k, RANK:RANK + 2 * NS])
                elif name == "dt":
                    wait_copied(pe, sl, "dTBC")
                    ps, done = fill(sl, name)
                    last = pe.matmul(ps[:, 0:D], dT[:], wdt[:], start=True, stop=True)
                elif name == "R":
                    pe.wait_ge(s_delta, v + 1)
                    ps, done = fill(sl, name)
                    last = pe.matmul(ps[:, 0:D], tri_after, delta[:], start=True, stop=True)
                elif name.startswith("num"):
                    i = int(name[3:])
                    c = i // 2
                    if i % 2 == 0:
                        pe.wait_ge(s_trib, v * 4 + c + 1)
                        pe.wait_ge(s_driven, v * 4 + c + 1)
                    ps, done = fill(sl, name)
                    for j in range(2):
                        n = 2 * (i % 2) + j
                        last = pe.matmul(ps[:, j * D:(j + 1) * D], tri_b[:, c % 2, n, :], driven[:, c % 2, n, :],
                                         start=True, stop=True)
                elif name == "yT":
                    pe.wait_ge(s_scanned, v * 4 + 4)
                    ps, done = fill(sl, name)
                    for c in range(DC):
                        last = pe.transpose(ps[:, c * P:(c + 1) * P], y[:, c * P:(c + 1) * P], ident)
                elif name == "out":
                    wait_copied(pe, sl, "yT")
                    ps, done = fill(sl, name)
                    last = two(ps[:, 0:D], lambda k: yT[:, k, :], lambda k: wout[:, k, :])
                last.then_inc(done, 1)

            def tile(section, t, v):
                sl = Slots(section, t)
                if t is not None:
                    context_transposes(sl, t, 0)
                if v is not None:
                    probs_transposes(v, UNITS - 1)
                if t is not None:
                    queries(sl, t)
                if v is not None:
                    weighted_context(v, UNITS - 1)
                if t is not None:
                    for i in range(4):
                        query_keys(sl, t, i)
                if v is not None:
                    outputs(sl, v)
                if t is not None:
                    for i in range(4, 8):
                        query_keys(sl, t, i)
                for u in range(UNITS):
                    if t is not None:
                        scores(sl, t, u)
                    for part, names in enumerate(STEPS[u]):
                        for name in names:
                            if name in LAGGED:
                                if v is not None:
                                    scan_slot(sl, v, name)
                            elif t is not None:
                                context_transposes(sl, t, int(name[4:]))
                        if t is not None and u >= 1:
                            if part == 0:
                                probs_transposes(t, u - 1)
                            else:
                                weighted_context(t, u - 1)

            setup()
            wait_copied(pe, Slots("setup"), "wk2", "wk3", "x2", "x3")
            pe.wait_ge(s_wq, 16)
            tile("first", 0, None)
            pe.wait_ge(s_vo, 16 * T)
            pe.wait_ge(s_scanw, 64)
            with pe.Fori(1, T) as t:
                tile("body", t, t - 1)
            tile("last", None, T - 1)

        @block.scalar
        def _(act):
            link = Chain(s_act, act)

            def setup():
                sl = Slots("setup")
                act.wait_ge(s_zero, 1)
                for i in range(4):
                    ps, done = wait_filled(act, sl, f"wk{i}")
                    for e in range(2):
                        dst = wkT[e * E:(e + 1) * E, 4 * i:4 * i + 4, :].rearrange("p (j e) d -> p j e d", e=2)[:, :, e, :]
                        last = act.activation(dst, ps[e * E:(e + 1) * E, :].rearrange("p (j d) -> p j d", j=2),
                                              ACT.Copy, scale=float(E) ** -0.5)
                    last.then_inc(done, 1)
                act.wait_ge(s_mv1, 1)
                link(act.activation(lnv1[:], mv1[:, :, 1], ACT.Ln, bias=eps_col[:, 0:1]))
                act.activation(rstd1[:], lnv1[:], ACT.Exp, scale=-0.5).then_inc(s_rstd1, 1)
                ps, done = wait_filled(act, sl, "alog")
                act.activation(a_T, ps[0:NS, 0:D], ACT.Exp).then_inc(done, 1)
                for i in range(8):
                    ps, done = wait_filled(act, sl, f"a{i}")
                    act.copy(a_all[:, 2 * i:2 * i + 2, :], ps[:].rearrange("p (j d) -> p j d", j=2)).then_inc(done, 1)

            def context_copy(sl, t, b):
                ps, done = wait_filled(act, sl, f"ctxT{b}")
                act.copy(ctxT[b % 2][:, :, SK - 1], last_ctxT[:, :, t * TB + b])
                act.copy(ctxT[b % 2][:, :, 0:2 * P], ps[:].rearrange("p (c n) -> p c n", c=DC)).then_inc(done, 1)

            def query_keys_copy(sl, i):
                ps, done = wait_filled(act, sl, f"qk{i}")
                act.copy(qkT[:, :, i // 2, :, 2 * (i % 2) * L:2 * (i % 2 + 1) * L],
                         ps[:].rearrange("p (c b n) -> p c b n", c=DC, b=TB)) \
                    .then_inc(done, 1)

            def exponentials(t, u):
                g = unit(t, u)
                act.wait_ge(s_negmax, g + 1)
                if not isinstance(g, int) or g >= 2:
                    act.wait_ge(s_tp, g - 1)
                for gi in range(2):
                    last = act.activation(probs[u % 2][:, gi, :], ps_s[:, u % 2, gi, 0:SK], ACT.Exp,
                                          bias=neg_max[:, u % 2, gi:gi + 1], accum_out=row_sum[:, u % 2, gi:gi + 1])
                last.then_inc(s_exp, 1)

            def sums_copy(t, u):
                g, b, h0 = unit(t, u), u // 2, HU * (u % 2)
                act.wait_ge(s_z, g + 1)
                act.copy(zT[:, :, h0:h0 + HU, b * L:(b + 1) * L],
                         ps_z[:].rearrange("p c (h q) -> p c h q", h=HU)).then_inc(s_zT, 1)

            def chunk_decay(v, c):
                act.wait_ge(s_arg, v * 4 + c + 1)
                act.activation(decay[:, c % 2], decay[:, c % 2], ACT.Exp, scale=-1.0).then_inc(s_decay, 1)
                act.wait_ge(s_decay, v * 4 + c + 1)
                link(act.activation(inv_decay[:, c % 2], decay[:, c % 2], ACT.Ln, bias=eps_col[:, 1:2]))
                act.activation(inv_decay[:, c % 2], inv_decay[:, c % 2], ACT.Exp, scale=-1.0).then_inc(s_inv_decay, 1)

            def tile(section, t, v):
                sl = Slots(section, t)
                if t is not None:
                    context_copy(sl, t, 0)
                if v is not None:
                    sums_copy(v, UNITS - 1)
                if t is not None:
                    for i in range(6):
                        query_keys_copy(sl, i)
                if v is not None:
                    act.wait_ge(s_mv2, v + 1)
                    link(act.activation(lnv2[:], mv2[:, 1:2], ACT.Ln, bias=eps_col[:, 0:1]))
                    act.activation(rstd2[:], lnv2[:], ACT.Exp, scale=-0.5).then_inc(s_rstd2, 1)
                if t is not None:
                    for i in range(6, 8):
                        query_keys_copy(sl, i)
                for u in range(UNITS):
                    if t is not None:
                        exponentials(t, u)
                        if u in (1, 3, 5):
                            context_copy(sl, t, (u + 1) // 2)
                    if v is not None:
                        if u == 2:
                            act.wait_ge(s_negabs, v + 1)
                            link(act.activation(sp_e[:], sp_e[:], ACT.Exp))
                            act.activation(sp_e[:], sp_e[:], ACT.Ln, bias=1.0).then_inc(s_spl, 1)
                            ps, done = wait_filled(act, sl, "R")
                            act.copy(later[:], ps[:, 0:D]).then_inc(done, 1)
                        if 3 <= u < 7:
                            chunk_decay(v, u - 3)
                        if u == 7:
                            ps, done = wait_filled(act, sl, "yT")
                            act.copy(yT[:].rearrange("p c n -> p (c n)"), ps[:, 0:D]).then_inc(done, 1)
                    if t is not None and u >= 1:
                        sums_copy(t, u - 1)

            setup()
            tile("first", 0, None)
            with act.Fori(1, T) as t:
                link.enter(t, 6)
                tile("body", t, t - 1)
            link.leave(T - 1)
            tile("last", None, T - 1)

        @block.vector
        def _(dve):
            link = Chain(s_dve, dve)

            def setup():
                sl = Slots("setup")
                dve.wait_ge(s_x, 16)
                for t in range(T):
                    last = dve.bn_stats(stats1[:, t, :], x_all[:, t, :])
                link(last)
                for t in range(T):
                    last = dve.bn_aggr(mv1[:, t, :], stats1[:, t, :])
                last.then_inc(s_mv1, 1)
                dve.wait_ge(s_rstd1, 1)
                for t in range(T):
                    dve.tensor_scalar(xn1[:, t, :], x_all[:, t, :], mv1[:, t, 0:1], rstd1[:, t:t + 1],
                                      ALU.subtract, ALU.mult).then_inc(s_xn1, 1)
                for i in range(4):
                    ps, done = wait_filled(dve, sl, f"x{i}")
                    dve.tensor_copy(xn1T[:, :, 2 * i:2 * i + 2, :],
                                    ps[:].rearrange("p (c t n) -> p c t n", c=DC, t=2)).then_inc(done, 1)
                ps, done = wait_filled(dve, sl, "lastc")
                dve.tensor_copy(last_ctxT[:], ps[:, 0:DC * B].rearrange("p (c n) -> p c n", c=DC)).then_inc(done, 1)
                ps, done = wait_filled(dve, sl, "vl")
                dve.wait_ge(s_zero, 1)
                for e in range(2):
                    half = slice(e * E, (e + 1) * E)
                    last = dve.tensor_copy(last_vT[half, :, e, :],
                                           ps[half, 0:IC * B].rearrange("p (c n) -> p c n", c=IC))
                last.then_inc(done, 1)
                for i in range(IC):
                    ps, done = wait_filled(dve, sl, f"vo{i}")
                    dve.tensor_copy(vo_rows[:, 2 * i:2 * i + 2, :],
                                    ps[0:B, :].rearrange("p (j d) -> p j d", j=2)).then_inc(done, 1)
                ps, done = wait_filled(dve, sl, "bias")
                dve.tensor_tensor(x_all[:], x_all[:], spread(ps[:, 0:D], 1, T), ALU.add).then_inc(done, 1)
                wait_copied(dve, sl, "bias")

            def queries_copy(sl, i):
                ps, done = wait_filled(dve, sl, f"q{i}")
                dve.tensor_tensor(qT[:, 4 * i:4 * i + 4, :], ps[:].rearrange("p (j n) -> p j n", j=4),
                                  spread(bqT[:, 4 * i:4 * i + 4], 2, P), ALU.add).then_inc(done, 1)

            def maxima(t, u):
                g = unit(t, u)
                dve.wait_ge(s_scores, g + 1)
                dve.tensor_reduce(neg_max[:, u % 2, :], ps_s[:, u % 2, :, 0:SK], AX.X, ALU.max, negate=True) \
                    .then_inc(s_negmax, 1)

            def inverse_sums(t, u):
                dve.wait_ge(s_exp, unit(t, u) + 1)
                dve.reciprocal(inv_sum[:, u % 2, :], row_sum[:, u % 2, :]).then_inc(s_inv, 1)

            def probs_copy(t, u):
                dve.wait_ge(s_tp, unit(t, u) + 1)
                dve.tensor_copy(pT[u % 2][:], ps_t[:]).then_inc(s_pT, 1)

            def outputs(sl, v):
                for i in range(2):
                    ps, done = wait_filled(dve, sl, f"oT{i}")
                    dve.tensor_copy(oT[:, 4 * i:4 * i + 4, :], ps[:].rearrange("p (j n) -> p j n", j=4)) \
                        .then_inc(done, 1)
                ps, done = wait_filled(dve, sl, "last")
                ins = dve.tensor_tensor(last_pm[:].rearrange("p b g q -> p (b g) q"),
                                        ps[0:TB * H, :].rearrange("p (k q) -> p k q", q=L),
                                        spread(own[0:TB * H, :], 2, L), ALU.mult)
                ins.then_inc(done, 1)
                wait_copied(dve, sl, "last")
                dve.tensor_reduce(last_pT[:], last_pm[:].rearrange("p b g q -> p b q g"), AX.X, ALU.add) \
                    .then_inc(s_lastT, 1)
                if isinstance(v, int) or True:
                    dve.wait_ge(s_lastT, v + 1)
                ps, done = wait_filled(dve, sl, "wo")
                dve.tensor_tensor(x1[:], ps[:, 0:D], x_all[:, v, :], ALU.add).then_inc(done, 1)
                wait_copied(dve, sl, "wo")
                link(dve.bn_stats(stats2[:], x1[:]))
                dve.tensor_tensor(x1b[:], x1[:], bout[:], ALU.add).then_inc(s_x1b, 1)
                dve.bn_aggr(mv2[:], stats2[:]).then_inc(s_mv2, 1)
                dve.wait_ge(s_rstd2, v + 1)
                dve.wait_ge(s_mv2, v + 1)
                dve.tensor_scalar(xn2[:], x1[:], mv2[:, 0:1], rstd2[:, 0:1], ALU.subtract, ALU.mult) \
                    .then_inc(s_xn2, 1)

            def scan_slot(sl, v, name):
                ps, done = wait_filled(dve, sl, name)
                if name == "xnT":
                    dve.tensor_copy(xn2T[:].rearrange("p c n -> p (c n)"), ps[:, 0:D]).then_inc(done, 1)
                elif name == "dTBC":
                    dve.tensor_copy(dT[0:RANK, :], ps[0:RANK, 0:P])
                    dve.tensor_copy(bc[:], ps[:, P:P + 2 * NS]).then_inc(done, 1)
                elif name == "dt":
                    dve.tensor_copy(sp_x[:], ps[:, 0:D]).then_inc(done, 1)
                    wait_copied(dve, sl, "dt")
                    dve.scalar_tensor_tensor(sp_e[:], sp_x[:], -1.0, sp_x[:], ALU.mult, ALU.min).then_inc(s_negabs, 1)
                    dve.wait_ge(s_spl, v + 1)
                    dve.scalar_tensor_tensor(delta[:], sp_x[:], 0.0, sp_e[:], ALU.max, ALU.add).then_inc(s_delta, 1)
                elif name.startswith("num"):
                    i = int(name[3:])
                    c = i // 2
                    if i % 2 == 0:
                        dve.wait_ge(s_inv_decay, v * 4 + c + 1)
                    for j in range(2):
                        n = 2 * (i % 2) + j
                        last = dve.scalar_tensor_tensor(inv_decay[:, c % 2, n, :], ps[:, j * D:(j + 1) * D],
                                                        bc[:, NS + 4 * c + n:NS + 4 * c + n + 1],
                                                        inv_decay[:, c % 2, n, :], ALU.mult, ALU.mult)
                    last.then_inc(done, 1)
                    if i % 2 == 1:
                        wait_copied(dve, sl, name)
                        link(dve.tensor_reduce(y_part[:], inv_decay[:, c % 2].rearrange("p n d -> p d n"), AX.X,
                                               ALU.add))
                        if c == 0:
                            dve.wait_ge(s_y0, v + 1)
                        else:
                            dve.wait_ge(s_scanned, v * 4 + c)
                        dve.tensor_tensor(y[:], y[:], y_part[:], ALU.add).then_inc(s_scanned, 1)
                elif name == "out":
                    dve.wait_ge(s_x1b, v + 1)
                    dve.tensor_tensor(x_all[:, v, :], ps[:, 0:D], x1b[:], ALU.add).then_inc(done, 1)

            def drive(v, c):
                dve.wait_ge(s_decay, v * 4 + c + 1)
                if c == 0:
                    dve.wait_ge(s_du, v + 1)
                dve.tensor_tensor(driven[:, c % 2], decay[:, c % 2], spread(du[:], 1, 4), ALU.mult) \
                    .then_inc(s_driven, 1)

            def tile(section, t, v):
                sl = Slots(section, t)
                if v is not None:
                    probs_copy(v, UNITS - 1)
                if t is not None:
                    queries_copy(sl, 0)
                    queries_copy(sl, 1)
                if v is not None:
                    outputs(sl, v)
                for u in range(UNITS):
                    if t is not None:
                        maxima(t, u)
                    if v is not None and 3 <= u < 7:
                        drive(v, u - 3)
                    for part, names in enumerate(STEPS[u]):
                        for name in names:
                            if v is not None and name in LAGGED and name not in ("R", "yT"):
                                scan_slot(sl, v, name)
                        if t is not None and u >= 1 and part == 0:
                            probs_copy(t, u - 1)
                    if t is not None:
                        inverse_sums(t, u)

            setup()
            tile("first", 0, None)
            dve.wait_ge(s_rows, 32)
            with dve.Fori(1, T) as t:
                link.enter(t, 5)
                tile("body", t, t - 1)
            link.leave(T - 1)
            tile("last", None, T - 1)


def sign_mlp(nc, cst, x_all, mlp, out):
    k0, k1, k2, s_cols, s_mlp_in = mlp
    ident = cst[:, 0:P]
    out_rows = out.rearrange("(t b) l d -> (b l) t d", b=TB)
    NB = 2 * P
    BLOCKS = T // 2
    with ExitStack() as stack:
        def sb(name, shape, dt=F32):
            return stack.enter_context(nc.sbuf_tensor(name, shape, dt))

        def sem(name):
            return stack.enter_context(nc.semaphore(name))

        w0 = sb("w0", [P, DC, F], F32R)
        w1 = sb("w1", [P, FC, F], F32R)
        w2 = sb("w2", [P, FC, D], F32R)
        k0_diff = sb("k0_diff", [P, DC, F])
        eps_m = sb("eps_m", [P, 1])
        s_two = sb("s_two", [P, 2])
        stats3 = sb("stats3", [P, T, 6])
        mv3 = sb("mv3", [P, T, 2])
        lnv3 = sb("lnv3", [P, T])
        rstd3 = sb("rstd3", [P, T])
        xn3 = sb("xn3", [P, T, D])
        xT_hi = sb("xT_hi", [P, DC, T, P], F32R)
        xT_lo = sb("xT_lo", [P, DC, T, P], F32R)
        whole = [sb(f"whole{i}", [P, 2, NB]) for i in range(3)]
        h1_hi = sb("h1_hi", [P, FC, NB], F32R)
        h1_lo = sb("h1_lo", [P, FC, NB], F32R)
        h2_hi = sb("h2_hi", [P, FC, NB], F32R)
        h2_lo = sb("h2_lo", [P, FC, NB], F32R)
        y_out = sb("y_out", [P, 2, D])

        HB = 4
        HS = FC
        ps_h = [stack.enter_context(nc.psum_tensor(f"ps_h{i}", [P, 2, NB], F32)) for i in range(HB)]
        ps_x = [stack.enter_context(nc.psum_tensor(f"ps_x{i}", [P, 2, DC, P], F32)) for i in range(2)]
        ps_o = [stack.enter_context(nc.psum_tensor(f"ps_o{i}", [P, D], F32)) for i in range(2)]

        s_eps, s_diff, s_w0, s_w1, s_w2, s_two_r = (
            sem(n) for n in ("mlp_eps_ready", "k0_diff_ready", "w0_ready", "w1_ready", "w2_ready", "scales_ready"))
        s_st3, s_mv3, s_ln3, s_rstd3, s_xn3, s_xT, s_xThi, s_xTlo = (
            sem(n) for n in ("stats3_ready", "variance3_ready", "ln3_ready", "rstd3_ready", "xn3_ready",
                             "x3_transposed", "xT_hi_ready", "xT_lo_ready"))
        s_h, s_whole, s_hi, s_lo = (
            sem(n) for n in ("hidden_summed", "hidden_whole", "hidden_hi_ready", "hidden_lo_ready"))
        s_o, s_yout = sem("outputs_summed"), [sem("outputs0_ready"), sem("outputs1_ready")]
        s_stored = [sem("stored0"), sem("stored1")]

        block = stack.enter_context(nc.Block())

        @block.gpsimd
        def _(pool):
            pool.memset(eps_m[:], EPS).then_inc(s_eps, 1)
            pool.wait_ge(s_mlp_in, 96)
            pool.tensor_scalar(w2[:], k2[:], 2.0, -1.0, ALU.mult, ALU.add).then_inc(s_w2, 1)
            pool.wait_ge(s_xT, 4)

            def low_parts(i, k):
                hi, lo = (h1_hi, h1_lo) if k < HS // 2 else (h2_hi, h2_lo)
                j = 2 * (k % (HS // 2))
                pool.wait_ge(s_hi, i * HS + k + 1)
                pool.tensor_tensor(lo[:, j:j + 2, :], whole[k % 2][:], hi[:, j:j + 2, :].bitcast(F32), ALU.subtract) \
                    .then_inc(s_lo, 1)

            with pool.Fori(0, BLOCKS) as i:
                for k in range(HS):
                    low_parts(i, k)

        @block.scalar
        def _(act):
            act.wait_ge(s_eps, 1)
            act.wait_ge(s_mv3, T)
            act.activation(lnv3[:], mv3[:, :, 1], ACT.Ln, bias=eps_m[:, 0:1]).then_inc(s_ln3, 1)
            act.wait_ge(s_ln3, 1)
            act.activation(rstd3[:], lnv3[:], ACT.Exp, scale=-0.5).then_inc(s_rstd3, 1)
            for j in range(4):
                act.wait_ge(s_xT, j + 1)
                act.copy(xT_hi[:, :, 2 * j:2 * j + 2, :],
                         ps_x[j % 2][:].rearrange("p t c n -> p c t n")).then_inc(s_xThi, 1)
            act.activation(w1[:, 4:8, :], k1[:, 4:8, :], ACT.Copy, scale=2.0, bias=-1.0).then_inc(s_w1, 1)
            with act.Fori(0, BLOCKS) as i:
                for k in range(HS):
                    hi = h1_hi if k < HS // 2 else h2_hi
                    j = 2 * (k % (HS // 2))
                    act.wait_ge(s_whole, i * HS + k + 1)
                    act.copy(hi[:, j:j + 2, :], whole[k % 2][:]).then_inc(s_hi, 1)

        @block.vector
        def _(dve):
            for t in range(T):
                dve.bn_stats(stats3[:, t, :], x_all[:, t, :]).then_inc(s_st3, 1)
            dve.wait_ge(s_st3, T)
            for t in range(T):
                dve.bn_aggr(mv3[:, t, :], stats3[:, t, :]).then_inc(s_mv3, 1)
            dve.wait_ge(s_mlp_in, 96)
            dve.tensor_tensor(k0_diff[:], k0[:, 0:DC, :], k0[:, DC:2 * DC, :], ALU.subtract).then_inc(s_diff, 1)
            dve.tensor_scalar(s_two[:], s_cols[:, 0:2], 2.0, None, ALU.mult).then_inc(s_two_r, 1)
            dve.wait_ge(s_rstd3, 1)
            dve.wait_ge(s_mv3, T)
            for t in range(T):
                dve.tensor_scalar(xn3[:, t, :], x_all[:, t, :], mv3[:, t, 0:1], rstd3[:, t:t + 1],
                                  ALU.subtract, ALU.mult).then_inc(s_xn3, 1)
            dve.wait_ge(s_diff, 1)
            dve.tensor_scalar(w0[:], k0_diff[:], 2.0, None, ALU.mult).then_inc(s_w0, 1)
            for j in range(4):
                dve.wait_ge(s_xThi, j + 1)
                hi = xT_hi[:, :, 2 * j:2 * j + 2, :].bitcast(F32)
                dve.tensor_tensor(xT_lo[:, :, 2 * j:2 * j + 2, :], ps_x[j % 2][:].rearrange("p t c n -> p c t n"), hi,
                                  ALU.subtract).then_inc(s_xTlo, 1)
            dve.tensor_scalar(w1[:, 0:4, :], k1[:, 0:4, :], 2.0, -1.0, ALU.mult, ALU.add).then_inc(s_w1, 1)
            dve.wait_ge(s_two_r, 1)

            def hidden(i, k):
                dve.wait_ge(s_h, i * HS + k + 1)
                if k >= 2 or not isinstance(i, int):
                    dve.wait_ge(s_lo, i * HS + k - 1)
                layer = 0 if k < HS // 2 else 1
                dve.tensor_scalar(whole[k % 2][:], ps_h[k % HB][:], s_two[:, layer:layer + 1], 0.0,
                                  ALU.mult, ALU.max).then_inc(s_whole, 1)

            def results(i):
                for j in range(2):
                    dve.wait_ge(s_o, 2 * i + j + 1)
                    if not isinstance(i, int) or i >= 1:
                        dve.wait_ge(s_stored[j], 16 * i)
                    dve.scalar_tensor_tensor(y_out[:, j, :], ps_o[j][:], s_cols[:, 2:3], x_all[:, 2 * i + j, :],
                                             ALU.mult, ALU.add).then_inc(s_yout[j], 1)

            def block_of(i, first=False, last=False):
                if not last:
                    for k in range(HS // 2):
                        hidden(i, k)
                if not first:
                    results(i - 1)
                if not last:
                    for k in range(HS // 2, HS):
                        hidden(i, k)

            block_of(0, first=True)
            with dve.Fori(1, BLOCKS) as i:
                block_of(i)
            block_of(BLOCKS, last=True)

        @block.tensor
        def _(pe):
            for j in range(4):
                pe.wait_ge(s_xn3, 2 * j + 2)
                if j >= 2:
                    pe.wait_ge(s_xTlo, j - 1)
                for t in range(2):
                    for c in range(DC):
                        last = pe.transpose(ps_x[j % 2][:, t, c, :], xn3[:, 2 * j + t, c * P:(c + 1) * P], ident)
                last.then_inc(s_xT, 1)

            def free_bank(i, k):
                if k >= HB or not isinstance(i, int):
                    pe.wait_ge(s_whole, i * HS + k - HB + 1)

            def layer1(i):
                for k in range(HS // 2):
                    free_bank(i, k)
                    for j in range(2):
                        f = 2 * k + j
                        n = 0
                        for part in (xT_hi, xT_lo):
                            for c in range(DC):
                                last = pe.matmul(ps_h[k % HB][:, j, :], w0[:, c, f * P:(f + 1) * P],
                                                 part[:, c, bass.ds(2 * i, 2), :].rearrange("p t n -> p (t n)"),
                                                 start=(n == 0), stop=(n == 2 * DC - 1))
                                n += 1
                    last.then_inc(s_h, 1)

            def layer2(i):
                for k in range(HS // 2, HS):
                    free_bank(i, k)
                    for j in range(2):
                        f = 2 * (k - HS // 2) + j
                        n = 0
                        for c in range(FC):
                            if c % 2 == 0 and k == HS // 2 and j == 0:
                                pe.wait_ge(s_lo, i * HS + c // 2 + 1)
                            for part in (h1_hi, h1_lo):
                                last = pe.matmul(ps_h[k % HB][:, j, :], w1[:, c, f * P:(f + 1) * P], part[:, c, :],
                                                 start=(n == 0), stop=(n == 2 * FC - 1))
                                n += 1
                    last.then_inc(s_h, 1)

            def layer3(i):
                pe.wait_ge(s_lo, (i + 1) * HS)
                for j in range(2):
                    if not isinstance(i, int) or i >= 1:
                        pe.wait_ge(s_yout[j], i)
                    n = 0
                    for c in range(FC):
                        for part in (h2_hi, h2_lo):
                            last = pe.matmul(ps_o[j][:], part[:, c, j * P:(j + 1) * P], w2[:, c, :],
                                             start=(n == 0), stop=(n == 2 * FC - 1))
                            n += 1
                    last.then_inc(s_o, 1)

            pe.wait_ge(s_xTlo, 4)
            pe.wait_ge(s_w0, 1)
            layer1(0)
            pe.wait_ge(s_w1, 2)
            layer2(0)
            pe.wait_ge(s_w2, 1)
            with pe.Fori(1, BLOCKS) as i:
                layer1(i)
                layer3(i - 1)
                layer2(i)
            layer3(BLOCKS - 1)

        @block.sync
        def _(sp):
            with sp.Fori(0, BLOCKS) as i:
                for j in range(2):
                    sp.wait_ge(s_yout[j], i + 1)
                    sp.dma_start(out_rows[:, 2 * i + j, :], y_out[:, j, :]).then_inc(s_stored[j], 16)
            for j in range(2):
                sp.wait_ge(s_stored[j], 16 * BLOCKS)


_INS = ["x", "ctx_1024", "L0_xattn_Wq", "L0_xattn_bq", "L0_xattn_Wk", "L0_xattn_bk", "L0_xattn_Wv", "L0_xattn_bv",
        "L0_xattn_Wo", "L0_xattn_bo", "L0_attn_W_x", "L0_attn_W_dt", "L0_attn_b_dt", "L0_attn_A_log", "L0_attn_D",
        "L0_attn_W_out", "L0_attn_b_out", "L0_ffn_k0", "L0_ffn_k1", "L0_ffn_k2", "L0_ffn_s0", "L0_ffn_s1",
        "L0_ffn_s2"]


def kernel(**inputs):
    import numpy as _np
    import concourse.bacc as _bacc
    from concourse import mybir as _mybir
    from concourse.bass_utils import run_bass_kernel_spmd as _run

    nc = _bacc.Bacc("TRN2", target_bir_lowering=False, num_devices=1)
    arrays = {"in_masks": host_constants()}
    for name in _INS:
        a = _np.ascontiguousarray(inputs[name])
        arrays[f"in_{name}"] = a.reshape(1) if a.ndim == 0 else a
    args = [nc.dram_tensor(n, a.shape, _mybir.dt.from_np(a.dtype), kind="ExternalInput").ap()
            for n, a in arrays.items()]
    args.append(nc.dram_tensor("out_x", (B, L, D), F32, kind="ExternalOutput").ap())
    perceiver_block(nc, *args)
    r = _run(nc, [arrays], core_ids=[0])
    return r.results[0]["out_x"]
```

```python
from contextlib import ExitStack

import numpy as np

import concourse.bass as bass
from concourse import mybir

ALU = mybir.AluOpType
ACT = mybir.ActivationFunctionType
AX = mybir.AxisListType
F32 = mybir.dt.float32
F32R = mybir.dt.float32r
U8 = mybir.dt.uint8

P = 128
B, L, D = 32, 32, 256
SK = 257
H, E = 16, 64
NS, RANK = 16, 64
TB = P // L
T = B // TB
DC = D // P
IC = H * E // P
UNITS = 2 * TB
HU = H // 2
F = 1024
FC = F // P
EPS = 1e-5
SCAN_EPS = 1e-12

FIRST_ORDER = [
    "ctxT0", "q0", "q1", "qk0", "qk1", "qk2", "qk3", "qk4", "qk5", "qk6", "max0", "qk7", "norm0", "scores0",
    "exp0", "inv0", "scores1", "max1", "exp1", "ctxT1", "norm1", "turn0", "copyP0", "inv1", "scores2", "max2",
    "exp2", "turn1", "copyP1", "sum0", "copyZ0", "ctxT2", "turn2", "scores3", "inv2", "norm2", "max3", "exp3",
    "copyP2", "inv3", "norm3", "max4", "sum1", "copyZ1", "scores4", "exp4", "copyP3", "turn3", "inv4", "norm4",
    "sum2", "copyZ2", "scores5", "max5", "turn4", "copyP4", "ctxT3", "norm5", "sum3", "exp5", "inv5", "copyZ3",
    "max6", "scores6", "exp6", "turn5", "norm6", "sum4", "inv6", "copyZ4", "copyP5", "scores7", "max7", "exp7",
    "turn6", "copyP6", "inv7", "norm7", "copyZ5", "sum5"]
BODY_ORDER = [
    "copyP7", "ctxT0", "sum6", "turn7", "q0", "q1", "copyZ6", "sum7", "last", "qk0", "copyZ7", "oT0", "oT1",
    "qk1", "wo", "qk2", "layernorm", "qk4", "qk3", "xnT", "qk5", "qk6", "qk7", "dT", "dt", "BC", "exp0", "max0",
    "scores0", "inv0", "norm0", "R", "prep0", "max1", "exp1", "ctxT1", "copyP0", "scores1", "inv1", "prep1",
    "decay0", "drive0", "norm1", "turn0", "invert0", "scores2", "sum0", "newton0", "max2", "num0", "turn1",
    "copyP1", "exp2", "inv2", "norm2", "decay1", "max3", "num1", "drive1", "invert1", "prep2", "copyP2",
    "newton1", "copyZ0", "scores3", "exp3", "ctxT2", "turn2", "inv3", "part0", "decay2", "num2", "sum1",
    "norm3", "copyZ1", "drive2", "num3", "prep3", "invert2", "max4", "scores4", "newton2", "turn3", "exp4",
    "part1", "copyP3", "inv4", "norm4", "num4", "decay3", "max5", "sum2", "copyZ2", "copyP4", "norm5", "inv5",
    "scores5", "drive3", "exp5", "num5", "invert3", "copyZ3", "ctxT3", "turn4", "sum3", "newton3", "part2",
    "exp6", "num6", "copyP5", "norm6", "max6", "scores6", "num7", "turn5", "max7", "inv6", "copyZ4", "scores7",
    "sum4", "part3", "exp7", "yT", "inv7", "turn6", "copyP6", "out", "mlpnorm", "sum5", "norm7", "x3T", "copyZ5"]
LAST_ORDER = [
    "turn7", "copyP7", "w0", "mlpx", "sum6", "copyZ6", "high0", "w1_0", "sum7", "hidden0", "relu0", "low0",
    "copyZ7", "low1", "oT0", "w1_1", "high1", "hidden1", "relu1", "last", "oT1", "hidden2", "relu2", "high2",
    "wo", "relu3", "w1_2", "hidden3", "layernorm", "low2", "low3", "xnT", "w1_5", "w1_6", "w1_3", "dT", "w1_7",
    "w1_4", "dt", "BC", "R", "prep0", "high3", "relu4", "decay0", "drive0", "high4", "hidden4", "hidden5",
    "relu5", "invert0", "newton0", "high5", "prep1", "low4", "num0", "decay1", "low5", "num1", "invert1",
    "drive1", "part0", "prep2", "newton1", "hidden6", "num2", "num3", "decay2", "relu6", "low6", "drive2",
    "part1", "invert2", "newton2", "hidden7", "num4", "high6", "prep3", "num5", "decay3", "invert3", "drive3",
    "relu7", "high7", "part2", "newton3", "w2_0", "num6", "num7", "low7", "mlpout0", "part3", "yT", "mlpsum0",
    "out", "mlpnorm", "x3T"]
ORDER = {"first": FIRST_ORDER, "body": BODY_ORDER, "last": LAST_ORDER}
LATE = set(LAST_ORDER)


SLOTS = ({f"ctxT{i}" for i in range(TB)} | {f"q{i}" for i in range(2)} | {f"qk{i}" for i in range(8)}
         | {"oT0", "oT1", "last", "wo", "xnT", "dT", "BC", "dt", "R", "yT", "out", "x3T"} | {f"num{i}" for i in range(8)})


def slot_order(section):
    return [name for name in ORDER[section] if name in SLOTS]


SETUP = ([f"wk{i}" for i in range(4)] + [f"x{i}" for i in range(T // 2)] + ["lastc", "vl"]
         + [f"vo{i}" for i in range(8)] + ["bias", "alog"] + [f"a{i}" for i in range(8)])
FIRST, BODY, LAST = slot_order("first"), slot_order("body"), slot_order("last")
assert len(BODY) % 2 == 0


class Slots:

    def __init__(self, section, t=0):
        self.names = {"setup": SETUP, "first": FIRST, "body": BODY, "last": LAST}[section]
        self.base = {"setup": 0, "first": len(SETUP), "body": len(SETUP) + len(FIRST),
                     "last": len(SETUP) + len(FIRST) + (T - 1) * len(BODY)}[section]
        self.more = (t - 1) * (len(BODY) // 2) if section == "body" else 0

    def at(self, name):
        g = self.base + self.names.index(name)
        return g % 2, g // 2 + self.more


class Chain:

    def __init__(self, sem, eng):
        self.sem, self.eng, self.base, self.k, self.more = sem, eng, 0, 0, 0

    def __call__(self, ins):
        ins.then_inc(self.sem, 1)
        self.k += 1
        self.eng.wait_ge(self.sem, self.base + self.k + self.more)

    def enter(self, t, per):
        self.base, self.k, self.per = self.base + self.k, 0, per
        self.more = (t - 1) * per

    def leave(self, times):
        assert self.k == self.per, f"the loop has {self.k} links"
        self.base, self.k, self.more = self.base + self.per * times, 0, 0


class Mlp:

    def __init__(self, nc, stack, w0, w1, w2):
        def sem(name):
            return stack.enter_context(nc.semaphore(name))

        self.w0, self.w1, self.w2 = w0, w1, w2
        self.s_two = stack.enter_context(nc.sbuf_tensor("s_two", [P, 2], F32))
        self.scales_ready, self.weights_ready, self.w2_ready = (
            sem("scales_ready"), sem("weights_ready"), sem("w2_ready"))
        self.xT_hi_ready, self.xT_lo_ready = sem("xT_hi_ready"), sem("xT_lo_ready")
        self.hidden_summed, self.hidden_whole = sem("hidden_summed"), sem("hidden_whole")
        self.hidden_hi_ready, self.hidden_lo_ready = sem("hidden_hi_ready"), sem("hidden_lo_ready")
        self.outputs_summed = sem("outputs_summed")
        self.outputs0_ready, self.outputs1_ready = sem("outputs0_ready"), sem("outputs1_ready")
        self.stored0, self.stored1 = sem("stored0"), sem("stored1")


CONSTS = {"ident": P, "tri_incl": P, "tri_after": P, "head_sel": TB * H, "lat_sel": L, "own": UNITS * 2}


def host_constants():
    i = np.arange(P)
    same = i[:, None] // L == i[None, :] // L
    ident = np.eye(P)
    incl = same & (i[:, None] <= i[None, :])
    after = same & (i[:, None] > i[None, :])
    bh = np.arange(TB * H)
    head_sel = (i[:, None] // L) == (bh[None, :] % H) % 4
    lat_sel = (i[:, None] % L) == np.arange(L)[None, :]
    bg = np.arange(UNITS * 2)
    own = np.zeros((P, UNITS * 2))
    own[:TB * H] = (bh[:, None] // H == bg[None, :] // 4) & ((bh[:, None] % H) // 4 == bg[None, :] % 4)
    return np.concatenate([ident, incl, after, head_sel, lat_sel, own], axis=1).astype(np.float32)


def perceiver_block(nc, consts, x, ctx_1024, L0_xattn_Wq, L0_xattn_bq, L0_xattn_Wk, L0_xattn_bk, L0_xattn_Wv,
                    L0_xattn_bv, L0_xattn_Wo, L0_xattn_bo, L0_attn_W_x, L0_attn_W_dt, L0_attn_b_dt,
                    L0_attn_A_log, L0_attn_D, L0_attn_W_out, L0_attn_b_out, L0_ffn_k0, L0_ffn_k1,
                    L0_ffn_k2, L0_ffn_s0, L0_ffn_s1, L0_ffn_s2, out):
    with ExitStack() as stack:
        x_all = stack.enter_context(nc.sbuf_tensor("x_all", [P, T, D], F32))
        k0 = stack.enter_context(nc.sbuf_tensor("k0", [P, 2 * DC, F], U8))
        k1 = stack.enter_context(nc.sbuf_tensor("k1", [P, FC, F], U8))
        k2 = stack.enter_context(nc.sbuf_tensor("k2", [P, FC, D], U8))
        s_cols = stack.enter_context(nc.sbuf_tensor("s_cols", [P, 3], F32))
        cst = stack.enter_context(nc.sbuf_tensor("cst", [P, sum(CONSTS.values())], F32))
        proj = stack.enter_context(nc.sbuf_tensor("proj", [P, (FC + DC) * F], F32))
        proj_at = nc.sbuf_base - 4 * (FC + DC) * F
        rowsT = stack.enter_context(nc.sbuf_tensor("rowsT", [P, DC, T, P], F32))
        s_mlp_in = stack.enter_context(nc.semaphore("mlp_in"))
        ctx_rows = stack.enter_context(nc.sbuf_tensor("ctx_rows", [P, TB * DC * D], F32))
        ctx_rows_at = nc.sbuf_base - 4 * TB * DC * D
        mlp = Mlp(nc, stack, overlay(nc, "w0", [P, DC, F], proj_at + 4 * FC * F),
                  overlay(nc, "w1", [P, FC, F], proj_at), overlay(nc, "w2", [P, FC, D], ctx_rows_at))
        mlp.k0, mlp.k1, mlp.k2, mlp.s_cols, mlp.loaded = k0, k1, k2, s_cols, s_mlp_in
        mlp.x_all, mlp.rowsT = x_all, rowsT
        attention_and_scan(nc, cst, consts, x, ctx_1024, L0_xattn_Wq, L0_xattn_bq, L0_xattn_Wk, L0_xattn_Wv,
                           L0_xattn_bv, L0_xattn_Wo, L0_xattn_bo, L0_attn_W_x, L0_attn_W_dt, L0_attn_b_dt,
                           L0_attn_A_log, L0_attn_D, L0_attn_W_out, L0_attn_b_out, x_all, proj, rowsT, ctx_rows, mlp,
                           (L0_ffn_k0, L0_ffn_k1, L0_ffn_k2, L0_ffn_s0, L0_ffn_s1, L0_ffn_s2), out)
        sign_mlp(nc, mlp, out)


def overlay(nc, name, shape, start):
    return nc.alloc_sbuf_tensor_at(name, shape, F32R, offset=start)


def row(vector):
    return vector.rearrange("(a d) -> a d", a=1)


def spread(ap, axis, n):
    wide = ap.unsqueeze(axis)
    shape = list(wide.shape)
    shape[axis] = n
    return wide.to_broadcast(shape)


def chunks(matrix):
    return matrix.rearrange("(c p) n -> p c n", p=P)


def attention_and_scan(nc, cst, consts, x, ctx, Wq, bq, Wk, Wv, bv, Wo, bo, W_x, W_dt, b_dt, A_log, D_skip, W_out,
                       b_out, x_all, proj, rowsT, ctx_rows, mlp, mlp_dram, out):
    x_rows = x.rearrange("(t b) l d -> (b l) t d", b=TB)

    with ExitStack() as stack:
        starts = {}

        def sb(name, shape, dt=F32):
            tensor = stack.enter_context(nc.sbuf_tensor(name, shape, dt))
            starts[name] = nc.sbuf_base - 4 * int(np.prod(shape[1:]))
            return tensor

        def sem(name):
            return stack.enter_context(nc.semaphore(name))

        masks, c = {}, 0
        for name, n in CONSTS.items():
            masks[name], c = cst[:, c:c + n], c + n
        ident, tri_incl, tri_after = masks["ident"], masks["tri_incl"], masks["tri_after"]
        head_sel, lat_sel, own = masks["head_sel"], masks["lat_sel"], masks["own"]

        xn1T, xn3T = rowsT, rowsT
        view = lambda a, n, c: proj[:, a:a + n].rearrange("p (c n) -> p c n", c=c)
        wkT = view(0, H * D, H)
        wv = view(H * D, DC * H * E, DC)
        wo = view(H * D + DC * H * E, IC * D, IC)
        wq = view(H * D + DC * H * E + IC * D, DC * H * E, DC)
        bqT = sb("bqT", [P, IC])
        last_vo = sb("last_vo", [TB * H, T, D])
        last_ctxT = sb("last_ctxT", [P, DC, B])
        wx = sb("wx", [P, DC, RANK + 2 * NS])
        wdt = sb("wdt", [RANK + 1, D])
        wout = sb("wout", [P, DC, D])
        bout = sb("bout", [P, D])
        dskip = sb("dskip", [P, D])
        a_all = sb("a_all", [P, NS, D])
        eps_col = sb("eps_col", [P, 2])
        bvT = sb("bvT", [P, IC])
        bo_row = sb("bo_row", [1, D])
        ones_row = sb("ones_row", [1, P])
        a_log = sb("a_log", [P, DC, NS])
        stats1 = sb("stats1", [P, T, 6])
        mv1 = sb("mv1", [P, T, 2])
        lnv1 = sb("lnv1", [P, T])
        rstd1 = sb("rstd1", [P, T])

        ctx_t = [ctx_rows[:, i * DC * D:(i + 1) * DC * D].rearrange("p (c d) -> p c d", c=DC) for i in range(TB)]
        ctxT = [sb(f"ctxT{i}", [P, DC, SK]) for i in range(2)]
        qT = sb("qT", [P, IC, P])
        qkT = sb("qkT", [P, DC, H // 4, TB, 4 * L])
        probs = [sb(f"probs{i}", [P, 2, SK]) for i in range(2)]
        pT = [sb(f"pT{i}", [P, DC, 2 * P]) for i in range(2)]
        zT = sb("zT", [P, DC, H, P])
        oT = sb("oT", [P, IC, P])
        neg_max = sb("neg_max", [P, 2, 2])
        row_sum = sb("row_sum", [P, 2, 2])
        inv_sum = sb("inv_sum", [P, 2, 2])
        last_p = sb("last_p", [P, 4 * TB, L])
        last_pm = sb("last_pm", [TB * H, TB, 4, L])
        last_pT = sb("last_pT", [TB * H, TB, L])

        x1 = sb("x1", [P, D])
        x1b = sb("x1b", [P, D])
        x2 = x1
        stats2 = sb("stats2", [P, 6])
        mv2 = sb("mv2", [P, 2])
        lnv2 = sb("lnv2", [P, 1])
        rstd2 = sb("rstd2", [P, 1])
        xn2 = sb("xn2", [P, D])
        xn2T = sb("xn2T", [P, DC, P])
        dT = sb("dT", [RANK + 1, P])
        bc = sb("bc", [P, 2 * NS])
        sp_x = sb("sp_x", [P, D])
        sp_e = sb("sp_e", [P, D])
        delta = sb("delta", [P, D])
        du = sb("du", [P, D])
        later = sb("later", [P, D])
        tri_b = sb("tri_b", [P, 2, 4, P])
        scan_buf = sb("scan_buf", [P, 3, 2, 4, D])
        decay, inv_decay = scan_buf[:, 0], scan_buf[:, 1]
        error, driven = scan_buf[:, 2, 0], scan_buf[:, 2, 1]
        y = sb("y", [P, D])
        y_part = sp_e
        yT = xn2T

        flat = lambda a: a[:].rearrange("p a b c -> p (a b c)")
        wk_raw = qkT[:].rearrange("p c g b n -> p (c g b n)")[:, 0:DC * H * E].rearrange("p (c n) -> p c n", c=DC)
        spare = qkT[:].rearrange("p c g b n -> p (c g b n)")[:, DC * H * E:]
        last_rows = spare[0:B, 0:D]
        a_T = spare[0:NS, D:2 * D]
        last_vT = spare[:, 2 * D:2 * D + 2 * IC * B].rearrange("p (c e b) -> p c e b", c=IC, e=2)
        xn1 = flat(zT)[:, 0:T * D].rearrange("p (t d) -> p t d", t=T)
        state_sel = flat(zT)[0:NS, T * D:T * D + NS * P].rearrange("p (n m) -> p n m", n=NS)
        vo_rows = scan_buf[0:B].rearrange("p a b c d -> p (a b c d)")[:, 0:H * D].rearrange("p (h d) -> p h d", h=H)
        bv_rep = tri_b[:].rearrange("p a b m -> p (a b) m")

        half = 4 * FC * NB
        mlp.h1_hi, mlp.h1_lo, mlp.h2_hi, mlp.h2_lo = (
            overlay(nc, f"first_{name}", [P, FC, NB], start)
            for name, start in (("h1_hi", starts["qkT"]), ("h1_lo", starts["qkT"] + half),
                                ("h2_hi", starts["zT"]), ("h2_lo", starts["zT"] + half)))
        mlp.whole = [a[:].rearrange("p a n -> p (a n)")[:, 0:4 * P].rearrange("p (a n) -> p a n", a=2) for a in probs]
        x_parts = [overlay(nc, f"first_x{i}", [P, DC, 2, P], starts[f"ctxT{i}"]) for i in range(2)]
        mlp.x_rows = lambda lo, c, i: x_parts[lo][:, c].rearrange("p t n -> p (t n)")
        mlp.y_out = qT[:].rearrange("p c n -> p (c n)")[:, 0:2 * D].rearrange("p (j d) -> p j d", j=2)

        ps_s = stack.enter_context(nc.psum_tensor("ps_s", [P, 2, 2, 512], F32))
        ps_t = stack.enter_context(nc.psum_tensor("ps_t", [P, DC, 256], F32))
        ps_z = stack.enter_context(nc.psum_tensor("ps_z", [P, DC, 256], F32))
        ps_m = [stack.enter_context(nc.psum_tensor(f"ps_m{i}", [P, 512], F32)) for i in range(2)]

        mlp.banks = [ps_s[:, k // 2, k % 2, :].rearrange("p (j n) -> p j n", j=2) for k in range(4)]
        mlp.out_banks = [ps_t[:, 0, :], ps_z[:, 0, :]]

        s_cst, s_x, s_wq, s_wk, s_wv, s_wo = (sem(n) for n in ("consts_in", "x_in", "wq_in", "wk_in", "wv_in", "wo_in"))
        s_small, s_lastc, s_alog, s_scanw, s_rows, s_vo = (
            sem(n) for n in ("small_in", "last_ctx_in", "a_log_in", "scan_weights_in", "scan_rows_in", "last_vo_placed"))
        s_ctx = [sem(f"ctx{i}_in") for i in range(TB)]
        s_eps, s_zero_wk, s_sel, s_zero, s_bvrep, s_mv1, s_rstd1, s_xn1 = (
            sem(n) for n in ("eps_ready", "wkT_zeros_ready", "state_sel_ready", "zeros_ready", "bv_rep_ready", "variance1_ready", "rstd1_ready",
                             "xn1_ready"))
        filled = [sem("bank0_filled"), sem("bank1_filled")]
        emptied = [sem("bank0_emptied"), sem("bank1_emptied")]
        s_scores, s_negmax, s_exp, s_inv, s_probs = (
            sem(n) for n in ("scores_ready", "neg_max_ready", "exp_done", "inv_sum_ready", "probs_ready"))
        s_tp, s_pT, s_z, s_zT, s_lastT = (
            sem(n) for n in ("probs_transposed", "pT_ready", "z_summed", "zT_ready", "last_pT_ready"))
        s_mv3, s_rstd3, s_xn3 = (sem(n) for n in ("variance3_ready", "rstd3_ready", "xn3_ready"))
        s_mv2, s_rstd2, s_xn2, s_negabs, s_spl, s_delta, s_du, s_y0, s_x1b = (
            sem(n) for n in ("variance2_ready", "rstd2_ready", "xn2_ready", "neg_abs_ready", "softplus_ln_ready",
                             "delta_ready", "du_ready", "skip_ready", "x1b_ready"))
        s_trib, s_arg, s_decay, s_inv_decay, s_driven, s_error, s_scanned = (
            sem(n) for n in ("tri_b_ready", "decay_log_ready", "decay_ready", "inv_decay_ready", "driven_ready",
                             "decay_error_ready", "chunk_scanned"))
        s_dve, s_act, s_pool = sem("vector_chain"), sem("scalar_chain"), sem("gpsimd_chain")

        def walk(parts, section, t, v):
            sl = Slots(section, t)
            for name in ORDER[section]:
                late = section == "last" or (section == "body" and name in LATE)
                kind = name.rstrip("0123456789")
                if kind in parts:
                    parts[kind](sl, v if late else t, int(name[len(kind):] or 0))

        def wait_filled(eng, sl, name):
            bank, before = sl.at(name)
            eng.wait_ge(filled[bank], before + 1)
            return ps_m[bank], emptied[bank]

        def wait_copied(eng, sl, *names):
            for name in names:
                bank, before = sl.at(name)
                eng.wait_ge(emptied[bank], before + 1)

        def unit(t, u):
            return t * UNITS + u

        k0, k1, k2, s_cols, s_mlp_in = mlp.k0, mlp.k1, mlp.k2, mlp.s_cols, mlp.loaded
        w0, w1 = mlp.w0, mlp.w1

        block = stack.enter_context(nc.Block())

        @block.sync
        def _(sp):
            sp.dma_start(cst[:], consts).then_inc(s_cst, 16)
            sp.dma_start(x_all[:], x_rows).then_inc(s_x, 16)
            sp.dma_start(wk_raw, chunks(Wk)).then_inc(s_wk, 16)
            sp.dma_start(wv[:], chunks(Wv)).then_inc(s_wv, 16)
            sp.dma_start(wo[:], chunks(Wo)).then_inc(s_wo, 16)
            sp.dma_start(wq[:], chunks(Wq)).then_inc(s_wq, 16)
            for b in range(TB):
                sp.dma_start(ctx_t[b][:], ctx[b, 0:2 * P, :].rearrange("(k p) d -> p k d", p=P)).then_inc(s_ctx[b], 16)
            sp.dma_start(wx[:], chunks(W_x)).then_inc(s_scanw, 16)
            sp.dma_start(wdt[0:RANK, :], W_dt).then_inc(s_scanw, 16)
            sp.dma_start(wdt[RANK:RANK + 1, :], row(b_dt)).then_inc(s_scanw, 16)
            sp.dma_start(wout[:], chunks(W_out)).then_inc(s_scanw, 16)
            for dst, src in ((k0, mlp_dram[0]), (k1, mlp_dram[1]), (k2, mlp_dram[2])):
                sp.dma_start(dst[:], chunks(src)).then_inc(s_mlp_in, 16)
            for i in range(3):
                sp.dma_start(s_cols[:, i:i + 1], row(mlp_dram[3 + i]).partition_broadcast(P)).then_inc(s_mlp_in, 16)
            wait_copied(sp, Slots("setup"), "vo6", "vo7")
            for t in range(T):
                sp.dma_start(last_vo[:, t, :], vo_rows[TB * t:TB * t + TB]).then_inc(s_vo, 16)
            with sp.Fori(1, T) as t:
                for b in range(TB):
                    sp.wait_ge(s_z, unit(t - 1, 2 * b) + 2)
                    sp.dma_start(ctx_t[b][:], ctx[t * TB + b, 0:2 * P, :].rearrange("(k p) d -> p k d", p=P)) \
                        .then_inc(s_ctx[b], 16)
            mlp_stores(sp, mlp, out, 0)
            for j in range(2):
                sp.wait_ge(mlp.stored0 if j == 0 else mlp.stored1, 16)

        @block.gpsimd
        def _(pool):
            pool.memset(eps_col[:, 0:1], EPS)
            pool.memset(eps_col[:, 1:2], SCAN_EPS).then_inc(s_eps, 1)
            pool.memset(wkT[:, H // 2:H, :], 0.0).then_inc(s_zero_wk, 1)
            pool.dma_start(last_rows, ctx[:, SK - 1, :]).then_inc(s_lastc, 16)
            pool.dma_start(a_log[:], chunks(A_log)).then_inc(s_alog, 16)
            pool.dma_start(bqT[:], bq.rearrange("(c p) -> p c", p=P), allow_slow_non_contiguous=True).then_inc(s_small, 16)
            pool.dma_start(bvT[:], bv.rearrange("(c p) -> p c", p=P), allow_slow_non_contiguous=True).then_inc(s_small, 16)
            pool.dma_start(bo_row[:], row(bo)).then_inc(s_small, 16)
            pool.dma_start(bout[:], row(b_out).partition_broadcast(P)).then_inc(s_rows, 16)
            pool.dma_start(dskip[:], row(D_skip).partition_broadcast(P)).then_inc(s_rows, 16)
            pool.memset(last_vT, 0.0)
            pool.memset(dT[:], 1.0)
            pool.memset(ones_row[:], 1.0).then_inc(s_zero, 1)
            pool.wait_ge(s_cst, 16)
            pool.tensor_copy(state_sel, spread(ident[0:NS, 0:NS], 2, P)).then_inc(s_sel, 1)
            pool.wait_ge(s_small, 48)
            pool.tensor_copy(bv_rep, spread(bvT[:], 2, P)).then_inc(s_bvrep, 1)

            def normalise(sl, t, u):
                g = unit(t, u)
                pr = probs[u % 2]
                pool.wait_ge(s_inv, g + 1)
                pool.tensor_tensor(pr[:], pr[:], spread(inv_sum[:, u % 2, :], 2, SK), ALU.mult) \
                    .then_inc(s_pool, 1)
                if u == 0 and "last" in sl.names:
                    wait_filled(pool, sl, "last")
                pool.wait_ge(s_pool, g + 1)
                pool.tensor_tensor(last_p[:, 2 * u:2 * u + 2, :], pr[:, :, SK - 1:SK].to_broadcast([P, 2, L]),
                                   spread(lat_sel, 1, 2), ALU.mult).then_inc(s_probs, 1)

            def prepare_chunk(sl, v, c):
                if c >= 2:
                    wait_filled(pool, sl, f"num{2 * c - 3}")
                    pool.wait_ge(s_error, v * 4 + c - 1)
                if c == 0:
                    wait_copied(pool, sl, "BC")
                pool.tensor_tensor(tri_b[:, c % 2], spread(tri_incl, 1, 4),
                                   spread(bc[:, 4 * c:4 * c + 4], 2, P), ALU.mult).then_inc(s_trib, 1)
                if c == 0:
                    wait_copied(pool, sl, "R")
                pool.tensor_tensor(decay[:, c % 2], a_all[:, 4 * c:4 * c + 4, :],
                                   spread(later[:], 1, 4), ALU.mult).then_inc(s_arg, 1)

            def skip_path(sl, v, _):
                pool.wait_ge(s_xn2, v + 1)
                pool.tensor_tensor(y[:], xn2[:], dskip[:], ALU.mult).then_inc(s_y0, 1)

            def delta_u(sl, v, _):
                pool.wait_ge(s_delta, v + 1)
                pool.tensor_tensor(du[:], delta[:], xn2[:], ALU.mult).then_inc(s_du, 1)

            def convert_w2(sl, v, _):
                pool.wait_ge(s_z, T * UNITS)
                pool.wait_ge(s_mlp_in, 96)
                pool.tensor_scalar(mlp.w2[:], k2[:], 2.0, -1.0, ALU.mult, ALU.add).then_inc(mlp.w2_ready, 1)

            parts = {"low": lambda sl, v, k: mlp_low(pool, mlp, 0, k), "w2_": convert_w2, "norm": normalise, "prep": prepare_chunk, "layernorm": skip_path, "dt": delta_u}
            walk(parts, "first", 0, None)
            wait_copied(pool, Slots("setup"), "a6", "a7")
            pool.wait_ge(s_rows, 32)
            with pool.Fori(1, T) as t:
                walk(parts, "body", t, t - 1)
            walk(parts, "last", None, T - 1)

        @block.tensor
        def _(pe):
            def fill(sl, name):
                bank, before = sl.at(name)
                if not (isinstance(before, int) and before == 0):
                    pe.wait_ge(emptied[bank], before)
                return ps_m[bank], filled[bank]

            def two(dst, lhs, rhs):
                pe.matmul(dst, lhs(0), rhs(0), start=True, stop=False)
                return pe.matmul(dst, lhs(1), rhs(1), start=False, stop=True)

            def setup():
                sl = Slots("setup")
                pe.wait_ge(s_cst, 16)
                pe.wait_ge(s_wk, 16)
                for i in range(4):
                    ps, done = fill(sl, f"wk{i}")
                    for j in range(2):
                        for c in range(DC):
                            last = pe.transpose(ps[:, (2 * j + c) * P:(2 * j + c + 1) * P],
                                                wk_raw[:, c, (2 * i + j) * P:(2 * i + j + 1) * P], ident)
                    last.then_inc(done, 1)
                for i in range(T // 2):
                    pe.wait_ge(s_xn1, 2 * i + 2)
                    ps, done = fill(sl, f"x{i}")
                    for j in range(2):
                        for c in range(DC):
                            last = pe.transpose(ps[:, (2 * c + j) * P:(2 * c + j + 1) * P],
                                                xn1[:, 2 * i + j, c * P:(c + 1) * P], ident)
                    last.then_inc(done, 1)
                pe.wait_ge(s_lastc, 16)
                ps, done = fill(sl, "lastc")
                for c in range(DC):
                    last = pe.transpose(ps[:, c * B:(c + 1) * B], last_rows[:, c * P:(c + 1) * P], ident[0:B, 0:B])
                last.then_inc(done, 1)
                pe.wait_ge(s_wv, 16)
                wait_copied(pe, sl, "lastc")
                ps, done = fill(sl, "vl")
                for c in range(IC):
                    last = two(ps[:, c * B:(c + 1) * B], lambda k: wv[:, k, c * P:(c + 1) * P],
                               lambda k: last_ctxT[:, k, :])
                last.then_inc(done, 1)
                pe.wait_ge(s_wo, 16)
                wait_copied(pe, sl, "vl")
                for c in range(IC):
                    ps, done = fill(sl, f"vo{c}")
                    for j in range(2):
                        last = pe.matmul(ps[0:B, j * D:(j + 1) * D], last_vT[:, c, j, :], wo[:, c, :], start=True, stop=True)
                    last.then_inc(done, 1)
                pe.wait_ge(s_bvrep, 1)
                ps, done = fill(sl, "bias")
                for c in range(IC):
                    pe.matmul(ps[:, 0:D], bv_rep[:, c, :], wo[:, c, :], start=(c == 0), stop=False)
                pe.matmul(ps[:, 0:D], ones_row[:], bo_row[:], start=False, stop=True).then_inc(done, 1)
                pe.wait_ge(s_alog, 16)
                ps, done = fill(sl, "alog")
                for c in range(DC):
                    last = pe.transpose(ps[0:NS, c * P:(c + 1) * P], a_log[:, c, :], ident)
                last.then_inc(done, 1)
                pe.wait_ge(s_sel, 1)
                wait_copied(pe, sl, "alog")
                for i in range(8):
                    ps, done = fill(sl, f"a{i}")
                    for j in range(2):
                        last = pe.matmul(ps[:, j * D:(j + 1) * D], state_sel[:, 2 * i + j, :], a_T,
                                         start=True, stop=True)
                    last.then_inc(done, 1)

            def context_transposes(sl, t, b):
                pe.wait_ge(s_ctx[b], (t + 1) * 16)
                ps, done = fill(sl, f"ctxT{b}")
                for k in range(DC):
                    for c in range(DC):
                        last = pe.transpose(ps[:, (2 * c + k) * P:(2 * c + k + 1) * P],
                                            ctx_t[b][:, k, c * P:(c + 1) * P], ident)
                last.then_inc(done, 1)

            def queries(sl, t, i):
                ps, done = fill(sl, f"q{i}")
                for j in range(4):
                    c = 4 * i + j
                    last = two(ps[:, j * P:(j + 1) * P], lambda k: wq[:, k, c * P:(c + 1) * P],
                               lambda k: xn1T[:, k, t, :])
                last.then_inc(done, 1)

            def query_keys(sl, t, i):
                if i % 4 == 0:
                    wait_copied(pe, sl, f"q{i // 4}")
                ps, done = fill(sl, f"qk{i}")
                for j in range(2):
                    for c in range(DC):
                        dst = ps[:, 2 * c * P:2 * (c + 1) * P].rearrange("p (b j q) -> p b j q", b=TB, j=2)[:, :, j, :]
                        last = pe.matmul(dst, wkT[:, 2 * i + j, c * P:(c + 1) * P],
                                         qT[:, i, :].rearrange("p (b q) -> p b q", b=TB), start=True, stop=True)
                last.then_inc(done, 1)

            def scores(sl, t, u):
                g, b = unit(t, u), u // 2
                if u == 0:
                    wait_copied(pe, sl, "qk6", "qk7")
                if u % 2 == 0:
                    wait_copied(pe, sl, f"ctxT{b}")
                if not isinstance(g, int) or g >= 2:
                    pe.wait_ge(s_exp, g - 1)
                for gi in range(2):
                    last = two(ps_s[:, u % 2, gi, 0:SK], lambda k: qkT[:, k, 2 * (u % 2) + gi, b, :],
                               lambda k: ctxT[b % 2][:, k, :])
                last.then_inc(s_scores, 1)

            def probs_transposes(sl, t, u):
                g = unit(t, u)
                pe.wait_ge(s_probs, g + 1)
                if not isinstance(g, int) or g >= 1:
                    pe.wait_ge(s_pT, g)
                for k in range(DC):
                    for gi in range(2):
                        last = pe.transpose(ps_t[:, k, gi * P:(gi + 1) * P],
                                            probs[u % 2][:, gi, k * P:(k + 1) * P], ident)
                last.then_inc(s_tp, 1)

            def weighted_context(sl, t, u):
                g, b = unit(t, u), u // 2
                pe.wait_ge(s_pT, g + 1)
                if not isinstance(g, int) or g >= 1:
                    pe.wait_ge(s_zT, g)
                for c in range(DC):
                    last = two(ps_z[:, c, :], lambda k: ctx_t[b][:, k, c * P:(c + 1) * P], lambda k: pT[u % 2][:, k, :])
                last.then_inc(s_z, 1)

            def heads_outputs(sl, v, i):
                pe.wait_ge(s_zT, unit(v, UNITS - 2) + 1 + i)
                ps, done = fill(sl, f"oT{i}")
                for j in range(4):
                    for e in range(2):
                        h = 2 * (4 * i + j) + e
                        last = two(ps[e * E:(e + 1) * E, j * P:(j + 1) * P],
                                   lambda k: wv[:, k, h * E:(h + 1) * E], lambda k: zT[:, k, h, :])
                last.then_inc(done, 1)

            def last_rows_part(sl, v, _):
                ps, done = fill(sl, "last")
                pe.matmul(ps[0:TB * H, :], head_sel, last_p[:], start=True, stop=True).then_inc(done, 1)

            def output_projection(sl, v, _):
                ps, done = fill(sl, "wo")
                for c in range(IC):
                    if c % 4 == 0:
                        wait_copied(pe, sl, f"oT{c // 4}")
                    pe.matmul(ps[:, 0:D], oT[:, c, :], wo[:, c, :], start=(c == 0), stop=False)
                pe.wait_ge(s_lastT, v + 1)
                pe.matmul(ps[:, 0:D], last_pT[:], last_vo[:, v, :], start=False, stop=True).then_inc(done, 1)

            def xn2_transposes(sl, v, _):
                pe.wait_ge(s_xn2, v + 1)
                ps, done = fill(sl, "xnT")
                for c in range(DC):
                    last = pe.transpose(ps[:, c * P:(c + 1) * P], xn2[:, c * P:(c + 1) * P], ident)
                last.then_inc(done, 1)

            def delta_rows(sl, v, _):
                wait_copied(pe, sl, "xnT")
                ps, done = fill(sl, "dT")
                two(ps[0:RANK, 0:P], lambda k: wx[:, k, 0:RANK], lambda k: xn2T[:, k, :]).then_inc(done, 1)

            def b_and_c(sl, v, _):
                ps, done = fill(sl, "BC")
                two(ps[:, 0:2 * NS], lambda k: xn2T[:, k, :], lambda k: wx[:, k, RANK:RANK + 2 * NS]) \
                    .then_inc(done, 1)

            def delta_product(sl, v, _):
                wait_copied(pe, sl, "dT")
                ps, done = fill(sl, "dt")
                pe.matmul(ps[:, 0:D], dT[:], wdt[:], start=True, stop=True).then_inc(done, 1)

            def later_deltas(sl, v, _):
                pe.wait_ge(s_delta, v + 1)
                ps, done = fill(sl, "R")
                pe.matmul(ps[:, 0:D], tri_after, delta[:], start=True, stop=True).then_inc(done, 1)

            def numerators(sl, v, i):
                c = i // 2
                if i % 2 == 0:
                    pe.wait_ge(s_trib, v * 4 + c + 1)
                    pe.wait_ge(s_driven, v * 4 + c + 1)
                ps, done = fill(sl, f"num{i}")
                for j in range(2):
                    n = 2 * (i % 2) + j
                    last = pe.matmul(ps[:, j * D:(j + 1) * D], tri_b[:, c % 2, n, :], driven[:, n, :],
                                     start=True, stop=True)
                last.then_inc(done, 1)

            def y_transposes(sl, v, _):
                pe.wait_ge(s_scanned, v * 4 + 4)
                ps, done = fill(sl, "yT")
                for c in range(DC):
                    last = pe.transpose(ps[:, c * P:(c + 1) * P], y[:, c * P:(c + 1) * P], ident)
                last.then_inc(done, 1)

            def scan_output(sl, v, _):
                wait_copied(pe, sl, "yT")
                ps, done = fill(sl, "out")
                two(ps[:, 0:D], lambda k: yT[:, k, :], lambda k: wout[:, k, :]).then_inc(done, 1)

            def xn3_transposes(sl, v, _):
                pe.wait_ge(s_xn3, v + 1)
                ps, done = fill(sl, "x3T")
                for c in range(DC):
                    last = pe.transpose(ps[:, c * P:(c + 1) * P], xn2[:, c * P:(c + 1) * P], ident)
                last.then_inc(done, 1)

            def mlp_hidden(sl, v, k):
                if k == 0:
                    pe.wait_ge(mlp.weights_ready, 1)
                    pe.wait_ge(mlp.xT_lo_ready, 1)
                if k == FC // 2:
                    pe.wait_ge(mlp.weights_ready, 1 + FC)
                mlp_layer(pe, mlp, 0, k)

            def mlp_outputs(sl, v, _):
                pe.wait_ge(mlp.w2_ready, 1)
                mlp_last_layer(pe, mlp, 0)

            parts = {"hidden": mlp_hidden, "mlpout": mlp_outputs, "x3T": xn3_transposes, "ctxT": context_transposes, "q": queries, "qk": query_keys, "scores": scores,
                     "turn": probs_transposes, "sum": weighted_context, "oT": heads_outputs, "last": last_rows_part,
                     "wo": output_projection, "xnT": xn2_transposes, "dT": delta_rows, "BC": b_and_c, "dt": delta_product,
                     "R": later_deltas, "num": numerators, "yT": y_transposes, "out": scan_output}
            setup()
            wait_copied(pe, Slots("setup"), "wk2", "wk3", f"x{T // 2 - 2}", f"x{T // 2 - 1}")
            pe.wait_ge(s_wq, 16)
            walk(parts, "first", 0, None)
            pe.wait_ge(s_vo, 16 * T)
            pe.wait_ge(s_scanw, 64)
            with pe.Fori(1, T) as t:
                walk(parts, "body", t, t - 1)
            walk(parts, "last", None, T - 1)

        @block.scalar
        def _(act):
            link = Chain(s_act, act)

            act.preload_act_table_set("natural_log_exp_and_others")

            def setup():
                sl = Slots("setup")
                act.wait_ge(s_eps, 1)
                act.wait_ge(s_mv1, 1)
                link(act.activation(lnv1[:], mv1[:, :, 1], ACT.Ln, bias=eps_col[:, 0:1]))
                act.activation(rstd1[:], lnv1[:], ACT.Exp, scale=-0.5).then_inc(s_rstd1, 1)
                act.wait_ge(s_zero_wk, 2)
                for i in range(4):
                    ps, done = wait_filled(act, sl, f"wk{i}")
                    for e in range(2):
                        dst = wkT[e * E:(e + 1) * E, 4 * i:4 * i + 4, :].rearrange("p (j e) d -> p j e d", e=2)[:, :, e, :]
                        last = act.activation(dst, ps[e * E:(e + 1) * E, :].rearrange("p (j d) -> p j d", j=2),
                                              ACT.Copy, scale=float(E) ** -0.5)
                    last.then_inc(done, 1)
                ps, done = wait_filled(act, sl, "alog")
                act.activation(a_T, ps[0:NS, 0:D], ACT.Exp).then_inc(done, 1)
                for i in range(8):
                    ps, done = wait_filled(act, sl, f"a{i}")
                    act.copy(a_all[:, 2 * i:2 * i + 2, :], ps[:].rearrange("p (j d) -> p j d", j=2)).then_inc(done, 1)

            def context_copy(sl, t, b):
                ps, done = wait_filled(act, sl, f"ctxT{b}")
                act.copy(ctxT[b % 2][:, :, SK - 1], last_ctxT[:, :, t * TB + b])
                act.copy(ctxT[b % 2][:, :, 0:2 * P], ps[:].rearrange("p (c n) -> p c n", c=DC)).then_inc(done, 1)

            def query_keys_copy(sl, t, i):
                ps, done = wait_filled(act, sl, f"qk{i}")
                act.copy(qkT[:, :, i // 2, :, 2 * (i % 2) * L:2 * (i % 2 + 1) * L],
                         ps[:].rearrange("p (c b n) -> p c b n", c=DC, b=TB)) \
                    .then_inc(done, 1)

            def exponentials(sl, t, u):
                g = unit(t, u)
                act.wait_ge(s_negmax, g + 1)
                if not isinstance(g, int) or g >= 2:
                    act.wait_ge(s_tp, g - 1)
                for gi in range(2):
                    last = act.activation(probs[u % 2][:, gi, :], ps_s[:, u % 2, gi, 0:SK], ACT.Exp,
                                          bias=neg_max[:, u % 2, gi:gi + 1], accum_out=row_sum[:, u % 2, gi:gi + 1])
                last.then_inc(s_exp, 1)

            def sums_copy(sl, t, u):
                g, b, h0 = unit(t, u), u // 2, HU * (u % 2)
                act.wait_ge(s_z, g + 1)
                act.copy(zT[:, :, h0:h0 + HU, b * L:(b + 1) * L],
                         ps_z[:].rearrange("p c (h q) -> p c h q", h=HU)).then_inc(s_zT, 1)

            def chunk_decay(sl, v, c):
                act.wait_ge(s_arg, v * 4 + c + 1)
                act.activation(decay[:, c % 2], decay[:, c % 2], ACT.Exp, scale=-1.0).then_inc(s_decay, 1)

            def chunk_inverse(sl, v, c):
                act.wait_ge(s_decay, v * 4 + c + 1)
                if c >= 2:
                    act.wait_ge(s_scanned, v * 4 + c - 1)
                link(act.activation(inv_decay[:, c % 2], decay[:, c % 2], ACT.Ln, bias=eps_col[:, 1:2]))
                act.activation(inv_decay[:, c % 2], inv_decay[:, c % 2], ACT.Exp, scale=-1.0).then_inc(s_inv_decay, 1)

            def inverse_deviation(sl, v, _):
                act.wait_ge(s_mv2, v + 1)
                link(act.activation(lnv2[:], mv2[:, 1:2], ACT.Ln, bias=eps_col[:, 0:1]))
                act.activation(rstd2[:], lnv2[:], ACT.Exp, scale=-0.5).then_inc(s_rstd2, 1)

            def softplus(sl, v, _):
                act.wait_ge(s_negabs, v + 1)
                link(act.activation(sp_e[:], sp_e[:], ACT.Exp))
                act.activation(sp_e[:], sp_e[:], ACT.Ln, bias=1.0).then_inc(s_spl, 1)

            def later_copy(sl, v, _):
                ps, done = wait_filled(act, sl, "R")
                act.copy(later[:], ps[:, 0:D]).then_inc(done, 1)

            def y_copy(sl, v, _):
                ps, done = wait_filled(act, sl, "yT")
                act.copy(yT[:].rearrange("p c n -> p (c n)"), ps[:, 0:D]).then_inc(done, 1)

            def inverse_deviation3(sl, v, _):
                act.wait_ge(s_mv3, v + 1)
                link(act.activation(lnv2[:], mv2[:, 1:2], ACT.Ln, bias=eps_col[:, 0:1]))
                act.activation(rstd2[:], lnv2[:], ACT.Exp, scale=-0.5).then_inc(s_rstd3, 1)

            def convert_w1(sl, v, c):
                if c == 0:
                    act.wait_ge(s_mlp_in, 96)
                if c == FC // 2:
                    wait_copied(act, sl, "wo")
                act.activation(w1[:, c, :], k1[:, c, :], ACT.Copy, scale=2.0, bias=-1.0).then_inc(mlp.weights_ready, 1)

            def mlp_rows_hi(sl, v, _):
                act.copy(x_parts[0][:], rowsT[:, :, 0:2, :]).then_inc(mlp.xT_hi_ready, 1)

            parts = {"mlpx": mlp_rows_hi, "high": lambda sl, v, k: mlp_high(act, mlp, 0, k),
                     "mlpnorm": inverse_deviation3, "w1_": convert_w1, "ctxT": context_copy, "qk": query_keys_copy, "exp": exponentials, "copyZ": sums_copy,
                     "layernorm": inverse_deviation, "dt": softplus, "R": later_copy, "decay": chunk_decay,
                     "invert": chunk_inverse,
                     "yT": y_copy}
            setup()
            walk(parts, "first", 0, None)
            with act.Fori(1, T) as t:
                link.enter(t, 7)
                walk(parts, "body", t, t - 1)
            link.leave(T - 1)
            walk(parts, "last", None, T - 1)

        @block.vector
        def _(dve):
            link = Chain(s_dve, dve)

            def setup():
                sl = Slots("setup")
                dve.memset(wkT[:, 0:H // 2, :], 0.0).then_inc(s_zero_wk, 1)
                dve.wait_ge(s_x, 16)
                for t in range(T):
                    last = dve.bn_stats(stats1[:, t, :], x_all[:, t, :])
                link(last)
                for t in range(T):
                    last = dve.bn_aggr(mv1[:, t, :], stats1[:, t, :])
                last.then_inc(s_mv1, 1)
                dve.wait_ge(s_rstd1, 1)
                for t in range(T):
                    dve.tensor_scalar(xn1[:, t, :], x_all[:, t, :], mv1[:, t, 0:1], rstd1[:, t:t + 1],
                                      ALU.subtract, ALU.mult).then_inc(s_xn1, 1)
                for i in range(T // 2):
                    ps, done = wait_filled(dve, sl, f"x{i}")
                    dve.tensor_copy(xn1T[:, :, 2 * i:2 * i + 2, :],
                                    ps[:].rearrange("p (c t n) -> p c t n", c=DC, t=2)).then_inc(done, 1)
                ps, done = wait_filled(dve, sl, "lastc")
                dve.tensor_copy(last_ctxT[:], ps[:, 0:DC * B].rearrange("p (c n) -> p c n", c=DC)).then_inc(done, 1)
                ps, done = wait_filled(dve, sl, "vl")
                dve.wait_ge(s_zero, 1)
                for e in range(2):
                    half = slice(e * E, (e + 1) * E)
                    last = dve.tensor_copy(last_vT[half, :, e, :],
                                           ps[half, 0:IC * B].rearrange("p (c n) -> p c n", c=IC))
                last.then_inc(done, 1)
                for i in range(IC):
                    ps, done = wait_filled(dve, sl, f"vo{i}")
                    dve.tensor_copy(vo_rows[:, 2 * i:2 * i + 2, :],
                                    ps[0:B, :].rearrange("p (j d) -> p j d", j=2)).then_inc(done, 1)
                ps, done = wait_filled(dve, sl, "bias")
                dve.tensor_tensor(x_all[:], x_all[:], spread(ps[:, 0:D], 1, T), ALU.add).then_inc(done, 1)
                wait_copied(dve, sl, "bias")

            def queries_copy(sl, t, i):
                ps, done = wait_filled(dve, sl, f"q{i}")
                dve.tensor_tensor(qT[:, 4 * i:4 * i + 4, :], ps[:].rearrange("p (j n) -> p j n", j=4),
                                  spread(bqT[:, 4 * i:4 * i + 4], 2, P), ALU.add).then_inc(done, 1)

            def maxima(sl, t, u):
                g = unit(t, u)
                dve.wait_ge(s_scores, g + 1)
                dve.tensor_reduce(neg_max[:, u % 2, :], ps_s[:, u % 2, :, 0:SK], AX.X, ALU.max, negate=True) \
                    .then_inc(s_negmax, 1)

            def inverse_sums(sl, t, u):
                dve.wait_ge(s_exp, unit(t, u) + 1)
                dve.reciprocal(inv_sum[:, u % 2, :], row_sum[:, u % 2, :]).then_inc(s_inv, 1)

            def probs_copy(sl, t, u):
                dve.wait_ge(s_tp, unit(t, u) + 1)
                dve.tensor_copy(pT[u % 2][:], ps_t[:]).then_inc(s_pT, 1)

            def heads_copy(sl, v, i):
                ps, done = wait_filled(dve, sl, f"oT{i}")
                dve.tensor_copy(oT[:, 4 * i:4 * i + 4, :], ps[:].rearrange("p (j n) -> p j n", j=4)) \
                    .then_inc(done, 1)

            def last_rows_own(sl, v, _):
                ps, done = wait_filled(dve, sl, "last")
                dve.tensor_tensor(last_pm[:].rearrange("p b g q -> p (b g) q"),
                                  ps[0:TB * H, :].rearrange("p (k q) -> p k q", q=L),
                                  spread(own[0:TB * H, :], 2, L), ALU.mult).then_inc(done, 1)
                wait_copied(dve, sl, "last")
                dve.tensor_reduce(last_pT[:], last_pm[:].rearrange("p b g q -> p b q g"), AX.X, ALU.add) \
                    .then_inc(s_lastT, 1)

            def attended(sl, v, _):
                ps, done = wait_filled(dve, sl, "wo")
                dve.tensor_tensor(x1[:], ps[:, 0:D], x_all[:, v, :], ALU.add).then_inc(done, 1)

            def layernorm(sl, v, _):
                wait_copied(dve, sl, "wo")
                link(dve.bn_stats(stats2[:], x1[:]))
                dve.tensor_tensor(x1b[:], x1[:], bout[:], ALU.add).then_inc(s_x1b, 1)
                dve.bn_aggr(mv2[:], stats2[:]).then_inc(s_mv2, 1)
                dve.wait_ge(s_mv2, v + 1)
                dve.wait_ge(s_rstd2, v + 1)
                dve.tensor_scalar(xn2[:], x1[:], mv2[:, 0:1], rstd2[:, 0:1], ALU.subtract, ALU.mult) \
                    .then_inc(s_xn2, 1)

            def xn2_copy(sl, v, _):
                ps, done = wait_filled(dve, sl, "xnT")
                dve.tensor_copy(xn2T[:].rearrange("p c n -> p (c n)"), ps[:, 0:D]).then_inc(done, 1)

            def delta_rows_copy(sl, v, _):
                ps, done = wait_filled(dve, sl, "dT")
                dve.tensor_copy(dT[0:RANK, :], ps[0:RANK, 0:P]).then_inc(done, 1)

            def b_and_c_copy(sl, v, _):
                ps, done = wait_filled(dve, sl, "BC")
                dve.tensor_copy(bc[:], ps[:, 0:2 * NS]).then_inc(done, 1)

            def softplus(sl, v, _):
                ps, done = wait_filled(dve, sl, "dt")
                dve.tensor_copy(sp_x[:], ps[:, 0:D]).then_inc(done, 1)
                wait_copied(dve, sl, "dt")
                dve.scalar_tensor_tensor(sp_e[:], sp_x[:], -1.0, sp_x[:], ALU.mult, ALU.min).then_inc(s_negabs, 1)
                dve.wait_ge(s_spl, v + 1)
                dve.scalar_tensor_tensor(delta[:], sp_x[:], 0.0, sp_e[:], ALU.max, ALU.add).then_inc(s_delta, 1)

            def drive(sl, v, c):
                if c == 0:
                    dve.wait_ge(s_du, v + 1)
                else:
                    wait_filled(dve, sl, f"num{2 * c - 1}")
                dve.wait_ge(s_decay, v * 4 + c + 1)
                dve.tensor_tensor(driven, decay[:, c % 2], spread(du[:], 1, 4), ALU.mult).then_inc(s_driven, 1)

            def newton(sl, v, c):
                dve.wait_ge(s_inv_decay, v * 4 + c + 1)
                dve.scalar_tensor_tensor(error, decay[:, c % 2], SCAN_EPS, inv_decay[:, c % 2],
                                         ALU.add, ALU.mult).then_inc(s_error, 1)
                dve.wait_ge(s_error, v * 4 + c + 1)
                link(dve.scalar_tensor_tensor(inv_decay[:, c % 2], error, 2.0, inv_decay[:, c % 2],
                                              ALU.subtract, ALU.mult))

            def numerators(sl, v, i):
                ps, done = wait_filled(dve, sl, f"num{i}")
                c = i // 2
                for j in range(2):
                    n = 2 * (i % 2) + j
                    last = dve.scalar_tensor_tensor(inv_decay[:, c % 2, n, :], ps[:, j * D:(j + 1) * D],
                                                    bc[:, NS + 4 * c + n:NS + 4 * c + n + 1],
                                                    inv_decay[:, c % 2, n, :], ALU.mult, ALU.mult)
                last.then_inc(done, 1)

            def part_of_y(sl, v, c):
                wait_copied(dve, sl, f"num{2 * c + 1}")
                link(dve.tensor_reduce(y_part[:], inv_decay[:, c % 2].rearrange("p n d -> p d n"), AX.X, ALU.add))
                if c == 0:
                    dve.wait_ge(s_y0, v + 1)
                else:
                    dve.wait_ge(s_scanned, v * 4 + c)
                dve.tensor_tensor(y[:], y[:], y_part[:], ALU.subtract).then_inc(s_scanned, 1)

            def scanned(sl, v, _):
                ps, done = wait_filled(dve, sl, "out")
                dve.wait_ge(s_x1b, v + 1)
                link(dve.tensor_tensor(x2[:], ps[:, 0:D], x1b[:], ALU.add))
                link(dve.bn_stats(stats2[:], x2[:]))
                dve.tensor_tensor(x_all[:, v, :], ps[:, 0:D], x1b[:], ALU.add).then_inc(done, 1)

            def layernorm3(sl, v, _):
                dve.bn_aggr(mv2[:], stats2[:]).then_inc(s_mv3, 1)
                dve.wait_ge(s_mv3, v + 1)
                dve.wait_ge(s_rstd3, v + 1)
                dve.tensor_scalar(xn2[:], x2[:], mv2[:, 0:1], rstd2[:, 0:1], ALU.subtract, ALU.mult) \
                    .then_inc(s_xn3, 1)

            def xn3_copy(sl, v, _):
                ps, done = wait_filled(dve, sl, "x3T")
                dve.tensor_copy(xn3T[:, :, v, :], ps[:, 0:D].rearrange("p (c n) -> p c n", c=DC)).then_inc(done, 1)

            def convert_w0(sl, v, _):
                dve.wait_ge(s_mlp_in, 96)
                dve.tensor_tensor(w0[:], k0[:, 0:DC, :], k0[:, DC:2 * DC, :], ALU.subtract) \
                    .then_inc(mlp.weights_ready, 1)
                dve.tensor_scalar(mlp.s_two[:, 0:1], s_cols[:, 0:1], 4.0, None, ALU.mult).then_inc(mlp.scales_ready, 1)
                dve.tensor_scalar(mlp.s_two[:, 1:2], s_cols[:, 1:2], 2.0, None, ALU.mult).then_inc(mlp.scales_ready, 1)
                dve.wait_ge(mlp.scales_ready, 2)

            def mlp_rows_lo(sl, v, _):
                dve.wait_ge(mlp.xT_hi_ready, 1)
                dve.tensor_tensor(x_parts[1][:], rowsT[:, :, 0:2, :], x_parts[0][:].bitcast(F32), ALU.subtract) \
                    .then_inc(mlp.xT_lo_ready, 1)

            parts = {"mlpx": mlp_rows_lo, "relu": lambda sl, v, k: mlp_relu(dve, mlp, 0, k),
                     "mlpsum": lambda sl, v, k: mlp_results(dve, mlp, 0), "mlpnorm": layernorm3, "x3T": xn3_copy,
                     "w": convert_w0, "q": queries_copy, "max": maxima, "copyP": probs_copy, "inv": inverse_sums, "oT": heads_copy,
                     "last": last_rows_own, "wo": attended, "layernorm": layernorm, "xnT": xn2_copy,
                     "dT": delta_rows_copy, "BC": b_and_c_copy, "dt": softplus, "drive": drive, "newton": newton, "num": numerators,
                     "part": part_of_y, "out": scanned}
            setup()
            walk(parts, "first", 0, None)
            dve.wait_ge(s_rows, 32)
            with dve.Fori(1, T) as t:
                link.enter(t, 11)
                walk(parts, "body", t, t - 1)
            link.leave(T - 1)
            walk(parts, "last", None, T - 1)


NB = 2 * P
BLOCKS = T // 2
HB = 4
HS = FC




def past_first(i):
    return not isinstance(i, int) or i >= 1


def mlp_layer(pe, m, i, k):
    if k >= HB or past_first(i):
        pe.wait_ge(m.hidden_whole, i * HS + k - HB + 1)
    first_layer = k < HS // 2
    for j in range(2):
        f = 2 * (k % (HS // 2)) + j
        n = 0
        if first_layer:
            for lo in range(2):
                for c in range(DC):
                    last = pe.matmul(m.banks[k % HB][:, j, :], m.w0[:, c, f * P:(f + 1) * P], m.x_rows(lo, c, i),
                                     start=(n == 0), stop=(n == 2 * DC - 1))
                    n += 1
        else:
            for c in range(FC):
                if c % 2 == 0 and k == HS // 2 and j == 0:
                    pe.wait_ge(m.hidden_lo_ready, i * HS + c // 2 + 1)
                for part in (m.h1_hi, m.h1_lo):
                    last = pe.matmul(m.banks[k % HB][:, j, :], m.w1[:, c, f * P:(f + 1) * P], part[:, c, :],
                                     start=(n == 0), stop=(n == 2 * FC - 1))
                    n += 1
    last.then_inc(m.hidden_summed, 1)


def mlp_last_layer(pe, m, i):
    for c in range(FC):
        if c % 2 == 0:
            pe.wait_ge(m.hidden_lo_ready, i * HS + HS // 2 + c // 2 + 1)
        for j in range(2):
            if c == 0 and past_first(i):
                pe.wait_ge(m.outputs0_ready if j == 0 else m.outputs1_ready, i)
            for part in (m.h2_hi, m.h2_lo):
                last = pe.matmul(m.out_banks[j], part[:, c, j * P:(j + 1) * P], m.w2[:, c, :],
                                 start=(c == 0 and part is m.h2_hi), stop=(c == FC - 1 and part is m.h2_lo))
            if c == FC - 1:
                last.then_inc(m.outputs_summed, 1)


def mlp_relu(dve, m, i, k):
    dve.wait_ge(m.hidden_summed, i * HS + k + 1)
    if k >= 2 or past_first(i):
        dve.wait_ge(m.hidden_lo_ready, i * HS + k - 1)
    layer = 0 if k < HS // 2 else 1
    dve.tensor_scalar(m.whole[k % 2], m.banks[k % HB], m.s_two[:, layer:layer + 1], 0.0,
                      ALU.mult, ALU.max).then_inc(m.hidden_whole, 1)


def hidden_halves(m, k):
    hi, lo = (m.h1_hi, m.h1_lo) if k < HS // 2 else (m.h2_hi, m.h2_lo)
    j = 2 * (k % (HS // 2))
    return hi[:, j:j + 2, :], lo[:, j:j + 2, :]


def mlp_high(act, m, i, k):
    act.wait_ge(m.hidden_whole, i * HS + k + 1)
    act.copy(hidden_halves(m, k)[0], m.whole[k % 2]).then_inc(m.hidden_hi_ready, 1)


def mlp_low(pool, m, i, k):
    pool.wait_ge(m.hidden_hi_ready, i * HS + k + 1)
    hi, lo = hidden_halves(m, k)
    pool.tensor_tensor(lo, m.whole[k % 2], hi.bitcast(F32), ALU.subtract).then_inc(m.hidden_lo_ready, 1)


def mlp_results(dve, m, i):
    for j in range(2):
        dve.wait_ge(m.outputs_summed, 2 * i + j + 1)
        if past_first(i):
            dve.wait_ge(m.stored0 if j == 0 else m.stored1, 16 * i)
        dve.scalar_tensor_tensor(m.y_out[:, j, :], m.out_banks[j], m.s_cols[:, 2:3], m.x_all[:, 2 * i + j, :],
                                 ALU.mult, ALU.add).then_inc(m.outputs0_ready if j == 0 else m.outputs1_ready, 1)


def mlp_stores(sp, m, out, i):
    out_rows = out.rearrange("(t b) l d -> (b l) t d", b=TB)
    for j in range(2):
        sp.wait_ge(m.outputs0_ready if j == 0 else m.outputs1_ready, i + 1)
        sp.dma_start(out_rows[:, 2 * i + j, :], m.y_out[:, j, :]).then_inc(m.stored0 if j == 0 else m.stored1, 16)


def sign_mlp(nc, mlp, out):
    with ExitStack() as stack:
        def sb(name, shape, dt=F32):
            return stack.enter_context(nc.sbuf_tensor(name, shape, dt))

        x_hi = sb("x_hi", [P, DC, T, P], F32R)
        x_lo = sb("x_lo", [P, DC, T, P], F32R)
        mlp.x_rows = lambda lo, c, i: (x_lo if lo else x_hi)[:, c, bass.ds(2 * i, 2), :].rearrange("p t n -> p (t n)")
        mlp.whole = [sb(f"whole{i}", [P, 2, NB])[:] for i in range(2)]
        mlp.h1_hi, mlp.h1_lo, mlp.h2_hi, mlp.h2_lo = (
            sb(name, [P, FC, NB], F32R) for name in ("h1_hi", "h1_lo", "h2_hi", "h2_lo"))
        mlp.y_out = sb("y_out", [P, 2, D])
        mlp.banks = [stack.enter_context(nc.psum_tensor(f"hidden{i}", [P, 2, NB], F32))[:] for i in range(HB)]
        mlp.out_banks = [stack.enter_context(nc.psum_tensor(f"outputs{i}", [P, D], F32))[:] for i in range(2)]

        block = stack.enter_context(nc.Block())

        @block.gpsimd
        def _(pool):
            with pool.Fori(1, BLOCKS) as i:
                for k in range(HS):
                    mlp_low(pool, mlp, i, k)

        @block.scalar
        def _(act):
            for j in range(1, BLOCKS):
                act.copy(x_hi[:, :, 2 * j:2 * j + 2, :], mlp.rowsT[:, :, 2 * j:2 * j + 2, :]) \
                    .then_inc(mlp.xT_hi_ready, 1)
            with act.Fori(1, BLOCKS) as i:
                for k in range(HS):
                    mlp_high(act, mlp, i, k)

        @block.vector
        def _(dve):
            for j in range(1, BLOCKS):
                dve.wait_ge(mlp.xT_hi_ready, j + 1)
                tiles = (slice(None), slice(None), slice(2 * j, 2 * j + 2))
                dve.tensor_tensor(x_lo[tiles], mlp.rowsT[tiles], x_hi[tiles].bitcast(F32), ALU.subtract) \
                    .then_inc(mlp.xT_lo_ready, 1)

            def block_of(i, first=False, last=False):
                if not last:
                    for k in range(HS // 2):
                        mlp_relu(dve, mlp, i, k)
                if not first:
                    mlp_results(dve, mlp, i - 1)
                if not last:
                    for k in range(HS // 2, HS):
                        mlp_relu(dve, mlp, i, k)

            block_of(1, first=True)
            with dve.Fori(2, BLOCKS) as i:
                block_of(i)
            block_of(BLOCKS, last=True)

        @block.tensor
        def _(pe):
            def layer(i, which):
                for k in range(which * HS // 2, (which + 1) * HS // 2):
                    mlp_layer(pe, mlp, i, k)

            pe.wait_ge(mlp.xT_lo_ready, 2)
            layer(1, 0)
            layer(1, 1)
            pe.wait_ge(mlp.xT_lo_ready, BLOCKS)
            with pe.Fori(2, BLOCKS) as i:
                layer(i, 0)
                mlp_last_layer(pe, mlp, i - 1)
                layer(i, 1)
            mlp_last_layer(pe, mlp, BLOCKS - 1)

        @block.sync
        def _(sp):
            with sp.Fori(1, BLOCKS) as i:
                mlp_stores(sp, mlp, out, i)
            for j in range(2):
                sp.wait_ge(mlp.stored0 if j == 0 else mlp.stored1, 16 * BLOCKS)


_INS = ["x", "ctx_1024", "L0_xattn_Wq", "L0_xattn_bq", "L0_xattn_Wk", "L0_xattn_bk", "L0_xattn_Wv", "L0_xattn_bv",
        "L0_xattn_Wo", "L0_xattn_bo", "L0_attn_W_x", "L0_attn_W_dt", "L0_attn_b_dt", "L0_attn_A_log", "L0_attn_D",
        "L0_attn_W_out", "L0_attn_b_out", "L0_ffn_k0", "L0_ffn_k1", "L0_ffn_k2", "L0_ffn_s0", "L0_ffn_s1",
        "L0_ffn_s2"]


def kernel(**inputs):
    import numpy as _np
    import concourse.bacc as _bacc
    from concourse import mybir as _mybir
    from concourse.bass_utils import run_bass_kernel_spmd as _run

    nc = _bacc.Bacc("TRN2", target_bir_lowering=False, num_devices=1)
    arrays = {"in_masks": host_constants()}
    for name in _INS:
        a = _np.ascontiguousarray(inputs[name])
        arrays[f"in_{name}"] = a.reshape(1) if a.ndim == 0 else a
    args = [nc.dram_tensor(n, a.shape, _mybir.dt.from_np(a.dtype), kind="ExternalInput").ap()
            for n, a in arrays.items()]
    args.append(nc.dram_tensor("out_x", (B, L, D), F32, kind="ExternalOutput").ap())
    perceiver_block(nc, *args)
    r = _run(nc, [arrays], core_ids=[0])
    return r.results[0]["out_x"]
```

```python
from contextlib import ExitStack

import numpy as np

import concourse.bass as bass
from concourse import mybir

ALU = mybir.AluOpType
ACT = mybir.ActivationFunctionType
AX = mybir.AxisListType
F32 = mybir.dt.float32
F32R = mybir.dt.float32r
U8 = mybir.dt.uint8

P = 128
B, L, D = 32, 32, 256
SK = 257
H, E = 16, 64
NS, RANK = 16, 64
TB = P // L
T = B // TB
DC = D // P
IC = H * E // P
UNITS = 2 * TB
HU = H // 2
F = 1024
FC = F // P
EPS = 1e-5
SCAN_EPS = 1e-12

FIRST_ORDER = [
    "ctxT0", "q0", "q1", "qk0", "qk1", "qk2", "norm0", "qk6", "qk3", "qk5", "qk4", "max0", "qk7", "scores0",
    "exp0", "inv0", "max1", "exp1", "ctxT1", "norm1", "copyP0", "inv1", "scores1", "turn0", "scores2", "max2",
    "exp2", "turn1", "sum0", "copyP1", "copyZ0", "ctxT2", "turn2", "inv2", "norm2", "norm3", "scores3", "max3",
    "exp3", "inv3", "copyP2", "max4", "sum1", "copyZ1", "exp4", "copyZ2", "copyP3", "scores4", "turn3", "inv4",
    "max5", "norm4", "sum2", "scores5", "ctxT3", "turn4", "copyP4", "norm5", "sum3", "exp5", "inv5", "copyZ3",
    "max6", "scores6", "exp6", "turn5", "norm6", "sum4", "inv6", "copyZ4", "copyP5", "scores7", "max7", "exp7",
    "turn6", "inv7", "norm7", "copyZ5", "copyP6", "sum5"]
BODY_ORDER = [
    "turn7", "ctxT0", "sum6", "copyP7", "q1", "copyZ6", "sum7", "copyZ7", "q0", "last", "oT0", "qk0", "oT1",
    "qk1", "wo", "qk2", "layernorm", "qk4", "qk3", "xnT", "qk6", "qk5", "qk7", "dT", "dt", "exp0", "BC", "max0",
    "inv0", "scores0", "norm0", "R", "prep0", "max1", "exp1", "ctxT1", "scores1", "inv1", "prep1", "decay0",
    "copyP0", "scores2", "norm1", "turn0", "invert0", "drive0", "sum0", "newton0", "norm2", "exp2", "max2",
    "copyP1", "turn1", "num0", "inv2", "num1", "decay1", "invert1", "max3", "drive1", "scores3", "ctxT2",
    "copyZ0", "prep2", "copyP2", "newton1", "turn2", "inv3", "exp3", "decay2", "part0", "num2", "norm3", "num3",
    "copyZ1", "drive2", "scores4", "sum1", "max4", "part1", "prep3", "turn3", "invert2", "inv4", "copyP3",
    "newton2", "norm4", "num4", "exp4", "scores5", "decay3", "max5", "num5", "copyP4", "invert3", "drive3",
    "sum2", "copyZ2", "norm5", "inv5", "exp5", "turn4", "copyZ3", "ctxT3", "newton3", "sum3", "part2", "num6",
    "exp6", "copyP5", "scores6", "max6", "num7", "max7", "turn5", "exp7", "scores7", "inv6", "sum4", "part3",
    "copyZ4", "norm6", "yT", "copyP6", "inv7", "turn6", "out", "mlpnorm", "norm7", "sum5", "x3T", "copyZ5"]
LAST_ORDER = [
    "mlpx0", "turn7", "copyZ6", "copyP7", "w0", "sum6", "high0", "low0", "last", "sum7", "w1_0", "hidden0",
    "copyZ7", "relu0", "oT0", "w1_2", "w1_1", "hidden1", "hidden2", "relu1", "oT1", "relu2", "high1", "high2",
    "low1", "wo", "layernorm", "low2", "w1_3", "w1_5", "xnT", "w1_7", "w1_4", "dT", "dt", "low3", "relu3",
    "w1_6", "hidden3", "R", "high3", "prep0", "BC", "hidden4", "relu4", "hidden5", "decay0", "low4", "drive0",
    "relu5", "high4", "prep1", "invert0", "newton0", "prep2", "low5", "w2_0", "high5", "num0", "decay1", "num1",
    "invert1", "drive1", "part0", "decay2", "newton1", "drive2", "mlpx1", "hidden6", "num2", "num3", "relu6",
    "part1", "invert2", "newton2", "hidden7", "prep3", "num4", "low6", "num5", "hidden8", "low7", "hidden9",
    "high6", "decay3", "invert3", "relu7", "drive3", "low8", "low9", "high7", "relu8", "hidden10", "part2",
    "high8", "low10", "high9", "relu9", "newton3", "num6", "num7", "relu10", "high10", "relu11", "low11",
    "high11", "mlpout0", "part3", "mlpx2", "hidden11", "mlpsum0", "hidden12", "yT", "relu12", "high12", "low12",
    "out", "hidden13", "low13", "relu13", "high13", "mlpnorm", "hidden14", "relu14", "high14", "low14", "x3T",
    "low15", "mlpx3", "relu15", "hidden15", "high15"]
ORDER = {"first": FIRST_ORDER, "body": BODY_ORDER, "last": LAST_ORDER}
LATE = set(LAST_ORDER)


SLOTS = ({f"ctxT{i}" for i in range(TB)} | {f"q{i}" for i in range(2)} | {f"qk{i}" for i in range(8)}
         | {"oT0", "oT1", "last", "wo", "xnT", "dT", "BC", "dt", "R", "yT", "out", "x3T"}
         | {f"num{i}" for i in range(8)})


def slot_order(section):
    return [name for name in ORDER[section] if name in SLOTS]


SETUP = ([f"wk{i}" for i in range(4)] + [f"x{i}" for i in range(T // 2)] + ["lastc", "vl"]
         + [f"vo{i}" for i in range(IC // 2)] + ["bias"])
FIRST, BODY, LAST = slot_order("first"), slot_order("body"), slot_order("last")
assert len(BODY) % 2 == 0


class Slots:

    def __init__(self, section, t=0):
        self.names = {"setup": SETUP, "first": FIRST, "body": BODY, "last": LAST}[section]
        self.base = {"setup": 0, "first": len(SETUP), "body": len(SETUP) + len(FIRST),
                     "last": len(SETUP) + len(FIRST) + (T - 1) * len(BODY)}[section]
        self.more = (t - 1) * (len(BODY) // 2) if section == "body" else 0

    def at(self, name):
        g = self.base + self.names.index(name)
        return g % 2, g // 2 + self.more


class Chain:

    def __init__(self, sem, eng):
        self.sem, self.eng, self.base, self.k, self.more = sem, eng, 0, 0, 0

    def __call__(self, ins):
        ins.then_inc(self.sem, 1)
        self.k += 1
        self.eng.wait_ge(self.sem, self.base + self.k + self.more)

    def enter(self, t, per):
        self.base, self.k, self.per = self.base + self.k, 0, per
        self.more = (t - 1) * per

    def leave(self, times):
        assert self.k == self.per, f"the loop has {self.k} links"
        self.base, self.k, self.more = self.base + self.per * times, 0, 0


class Mlp:

    def __init__(self, nc, stack, w0, w1, w2):
        def sem(name):
            return stack.enter_context(nc.semaphore(name))

        self.w0, self.w1, self.w2 = w0, w1, w2
        self.s_two = stack.enter_context(nc.sbuf_tensor("s_two", [P, 2], F32))
        self.scales_ready, self.weights_ready, self.w2_ready = (
            sem("scales_ready"), sem("weights_ready"), sem("w2_ready"))
        self.xT_hi_ready, self.xT_lo_ready = sem("xT_hi_ready"), sem("xT_lo_ready")
        self.hidden_summed, self.hidden_whole = sem("hidden_summed"), sem("hidden_whole")
        self.hidden_hi_ready, self.hidden_lo_ready = sem("hidden_hi_ready"), sem("hidden_lo_ready")
        self.outputs_summed = sem("outputs_summed")
        self.outputs0_ready, self.outputs1_ready = sem("outputs0_ready"), sem("outputs1_ready")
        self.stored0, self.stored1 = sem("stored0"), sem("stored1")


CONSTS = {"ident": P, "tri_incl": P, "tri_after": P, "head_sel": TB * H, "lat_sel": L, "own": UNITS * 2}


def host_constants():
    i = np.arange(P)
    same = i[:, None] // L == i[None, :] // L
    ident = np.eye(P)
    incl = same & (i[:, None] <= i[None, :])
    after = same & (i[:, None] > i[None, :])
    bh = np.arange(TB * H)
    head_sel = (i[:, None] // L) == (bh[None, :] % H) % 4
    lat_sel = (i[:, None] % L) == np.arange(L)[None, :]
    bg = np.arange(UNITS * 2)
    own = np.zeros((P, UNITS * 2))
    own[:TB * H] = (bh[:, None] // H == bg[None, :] // 4) & ((bh[:, None] % H) // 4 == bg[None, :] % 4)
    return np.concatenate([ident, incl, after, head_sel, lat_sel, own], axis=1).astype(np.float32)


def perceiver_block(nc, consts, x, ctx_1024, L0_xattn_Wq, L0_xattn_bq, L0_xattn_Wk, L0_xattn_bk, L0_xattn_Wv,
                    L0_xattn_bv, L0_xattn_Wo, L0_xattn_bo, L0_attn_W_x, L0_attn_W_dt, L0_attn_b_dt,
                    L0_attn_A_log, L0_attn_D, L0_attn_W_out, L0_attn_b_out, L0_ffn_k0, L0_ffn_k1,
                    L0_ffn_k2, L0_ffn_s0, L0_ffn_s1, L0_ffn_s2, out):
    with ExitStack() as stack:
        x_all = stack.enter_context(nc.sbuf_tensor("x_all", [P, T, D], F32))
        k0 = stack.enter_context(nc.sbuf_tensor("k0", [P, 2 * DC, F], U8))
        k1 = stack.enter_context(nc.sbuf_tensor("k1", [P, FC, F], U8))
        k2 = stack.enter_context(nc.sbuf_tensor("k2", [P, FC, D], U8))
        s_cols = stack.enter_context(nc.sbuf_tensor("s_cols", [P, 3], F32))
        cst = stack.enter_context(nc.sbuf_tensor("cst", [P, sum(CONSTS.values())], F32))
        proj = stack.enter_context(nc.sbuf_tensor("proj", [P, (FC + DC) * F], F32))
        proj_at = nc.sbuf_base - 4 * (FC + DC) * F
        rowsT = stack.enter_context(nc.sbuf_tensor("rowsT", [P, DC, T, P], F32))
        s_mlp_in = stack.enter_context(nc.semaphore("mlp_in"))
        ctx_rows = stack.enter_context(nc.sbuf_tensor("ctx_rows", [P, TB * DC * D], F32))
        ctx_rows_at = nc.sbuf_base - 4 * TB * DC * D
        mlp = Mlp(nc, stack, overlay(nc, "w0", [P, DC, F], proj_at + 4 * FC * F),
                  overlay(nc, "w1", [P, FC, F], proj_at), overlay(nc, "w2", [P, FC, D], ctx_rows_at))
        mlp.k0, mlp.k1, mlp.k2, mlp.s_cols, mlp.loaded = k0, k1, k2, s_cols, s_mlp_in
        mlp.x_all, mlp.rowsT = x_all, rowsT
        attention_and_scan(nc, cst, consts, x, ctx_1024, L0_xattn_Wq, L0_xattn_bq, L0_xattn_Wk, L0_xattn_Wv,
                           L0_xattn_bv, L0_xattn_Wo, L0_xattn_bo, L0_attn_W_x, L0_attn_W_dt, L0_attn_b_dt,
                           L0_attn_A_log, L0_attn_D, L0_attn_W_out, L0_attn_b_out, x_all, proj, rowsT, ctx_rows, mlp,
                           (L0_ffn_k0, L0_ffn_k1, L0_ffn_k2, L0_ffn_s0, L0_ffn_s1, L0_ffn_s2), out)


def overlay(nc, name, shape, start, dt=F32R):
    return nc.alloc_sbuf_tensor_at(name, shape, dt, offset=start)


def row(vector):
    return vector.rearrange("(a d) -> a d", a=1)


def spread(ap, axis, n):
    wide = ap.unsqueeze(axis)
    shape = list(wide.shape)
    shape[axis] = n
    return wide.to_broadcast(shape)


def chunks(matrix):
    return matrix.rearrange("(c p) n -> p c n", p=P)


def attention_and_scan(nc, cst, consts, x, ctx, Wq, bq, Wk, Wv, bv, Wo, bo, W_x, W_dt, b_dt, A_log, D_skip, W_out,
                       b_out, x_all, proj, rowsT, ctx_rows, mlp, mlp_dram, out):
    x_rows = x.rearrange("(t b) l d -> (b l) t d", b=TB)

    with ExitStack() as stack:
        starts = {}

        def sb(name, shape, dt=F32):
            tensor = stack.enter_context(nc.sbuf_tensor(name, shape, dt))
            starts[name] = nc.sbuf_base - 4 * int(np.prod(shape[1:]))
            return tensor

        def sem(name):
            return stack.enter_context(nc.semaphore(name))

        masks, c = {}, 0
        for name, n in CONSTS.items():
            masks[name], c = cst[:, c:c + n], c + n
        ident, tri_incl, tri_after = masks["ident"], masks["tri_incl"], masks["tri_after"]
        head_sel, lat_sel, own = masks["head_sel"], masks["lat_sel"], masks["own"]

        xn1T, xn3T = rowsT, rowsT
        view = lambda a, n, c: proj[:, a:a + n].rearrange("p (c n) -> p c n", c=c)
        wkT = view(0, H * D, H)
        wv = view(H * D, DC * H * E, DC)
        wo = view(H * D + DC * H * E, IC * D, IC)
        wq = view(H * D + DC * H * E + IC * D, DC * H * E, DC)
        bqT = sb("bqT", [P, IC])
        last_vo = sb("last_vo", [TB * H, T, D])
        last_ctxT = sb("last_ctxT", [P, DC, B])
        wx = sb("wx", [P, DC, RANK + 2 * NS])
        wdt = sb("wdt", [RANK + 1, D])
        wout = sb("wout", [P, DC, D])
        bout = sb("bout", [P, D])
        dskip = sb("dskip", [P, D])
        a_all = sb("a_all", [P, NS, D])
        eps_col = sb("eps_col", [P, 2])
        bvT = sb("bvT", [P, IC])
        bo_row = sb("bo_row", [1, D])
        ones_row = sb("ones_row", [1, P])
        stats1 = sb("stats1", [P, T, 6])
        mv1 = sb("mv1", [P, T, 2])
        lnv1 = sb("lnv1", [P, T])
        rstd1 = sb("rstd1", [P, T])

        ctx_t = [ctx_rows[:, i * DC * D:(i + 1) * DC * D].rearrange("p (c d) -> p c d", c=DC) for i in range(TB)]
        ctxT = [sb(f"ctxT{i}", [P, DC, SK]) for i in range(2)]
        qT = sb("qT", [P, IC, P])
        qkT = sb("qkT", [P, DC, H // 4, TB, 4 * L])
        probs = [sb(f"probs{i}", [P, 2, SK]) for i in range(2)]
        pT = [sb(f"pT{i}", [P, DC, 2 * P]) for i in range(2)]
        zT = sb("zT", [P, DC, H, P])
        oT = sb("oT", [P, IC, P])
        neg_max = sb("neg_max", [P, 2, 2])
        row_sum = sb("row_sum", [P, 2, 2])
        inv_sum = sb("inv_sum", [P, 2, 2])
        last_p = sb("last_p", [P, 4 * TB, L])
        last_pm = sb("last_pm", [TB * H, TB, 4, L])
        last_pT = sb("last_pT", [TB * H, TB, L])

        x1 = sb("x1", [P, D])
        x1b = sb("x1b", [P, D])
        x2 = x1
        stats2 = sb("stats2", [P, 6])
        mv2 = sb("mv2", [P, 2])
        lnv2 = sb("lnv2", [P, 1])
        rstd2 = sb("rstd2", [P, 1])
        xn2 = sb("xn2", [P, D])
        xn2T = sb("xn2T", [P, DC, P])
        dT = sb("dT", [RANK + 1, P])
        bc = sb("bc", [P, 2 * NS])
        sp_x = sb("sp_x", [P, D])
        sp_e = sb("sp_e", [P, D])
        delta = sb("delta", [P, D])
        du = sb("du", [P, D])
        later = sb("later", [P, D])
        tri_b = sb("tri_b", [P, 2, 4, P])
        scan_buf = sb("scan_buf", [P, 3, 2, 4, D])
        decay, inv_decay = scan_buf[:, 0], scan_buf[:, 1]
        error, driven = scan_buf[:, 2, 0], scan_buf[:, 2, 1]
        y = sb("y", [P, D])
        y_part = sp_e
        bias = y
        yT = xn2T

        flat = lambda a: a[:].rearrange("p a b c -> p (a b c)")
        wk_raw = qkT[:].rearrange("p c g b n -> p (c g b n)")[:, 0:DC * H * E].rearrange("p (c n) -> p c n", c=DC)
        spare = qkT[:].rearrange("p c g b n -> p (c g b n)")[:, DC * H * E:]
        last_rows = spare[0:B, 0:D]
        last_vT = spare[:, 2 * D:2 * D + 2 * IC * B].rearrange("p (c e b) -> p c e b", c=IC, e=2)
        xn1 = flat(zT)[:, 0:T * D].rearrange("p (t d) -> p t d", t=T)
        scan_flat = scan_buf[:].rearrange("p a b c d -> p (a b c d)")
        a_log = scan_flat[:, 0:D * NS].rearrange("p (d n) -> p n d", n=NS)
        vo_rows = scan_flat[0:2 * B, D * NS:D * NS + IC * D].rearrange("p (c d) -> p c d", c=IC)
        bv_rep = tri_b[:].rearrange("p a b m -> p (a b) m")

        half = 4 * FC * NB
        mlp.h1_hi, mlp.h1_lo, mlp.h2_hi, mlp.h2_lo = (
            overlay(nc, name, [P, FC, NB], start)
            for name, start in (("h1_hi", starts["qkT"]), ("h1_lo", starts["qkT"] + half),
                                ("h2_hi", starts["zT"]), ("h2_lo", starts["zT"] + half)))
        mlp.whole = [overlay(nc, f"whole{i}", [P, 2, NB], starts[f"probs{i}"], F32)[:] for i in range(2)]
        mlp.y_out = overlay(nc, "y_out", [P, 2, D], starts["qT"], F32)
        x_first = [overlay(nc, f"x_first{i}", [P, DC, 2, P], starts[f"ctxT{i}"]) for i in range(2)]
        x_parts = [overlay(nc, f"x_parts{i}", [P, DC, T, P], starts["a_all"] + i * 4 * T * D) for i in range(2)]

        def block_rows(lo, c, i):
            rows = x_first[lo][:, c] if isinstance(i, int) else x_parts[lo][:, c, bass.ds(2 * i, 2), :]
            return rows.rearrange("p t n -> p (t n)")

        def block_tiles(lo, j):
            return x_first[lo][:] if j < 2 else x_parts[lo][:, :, 2 * j:2 * j + 2, :]

        mlp.x_rows = block_rows

        ps_s = stack.enter_context(nc.psum_tensor("ps_s", [P, 2, 2, 512], F32))
        ps_t = stack.enter_context(nc.psum_tensor("ps_t", [P, DC, 256], F32))
        ps_z = stack.enter_context(nc.psum_tensor("ps_z", [P, DC, 256], F32))
        ps_m = [stack.enter_context(nc.psum_tensor(f"ps_m{i}", [P, 512], F32)) for i in range(2)]

        mlp.banks = [ps_s[:, k // 2, k % 2, :].rearrange("p (j n) -> p j n", j=2) for k in range(4)]
        mlp.out_banks = [ps_t[:, 0, :], ps_z[:, 0, :]]

        s_cst, s_x, s_wq, s_wk, s_wv, s_wo = (sem(n) for n in ("consts_in", "x_in", "wq_in", "wk_in", "wv_in", "wo_in"))
        s_small, s_lastc, s_alog, s_scanw, s_rows, s_vo = (
            sem(n) for n in ("small_in", "last_ctx_in", "a_log_in", "scan_weights_in", "scan_rows_in",
                             "last_vo_placed"))
        s_ctx = [sem(f"ctx{i}_in") for i in range(TB)]
        s_eps, s_zero_wk, s_a, s_zero, s_bvrep, s_mv1, s_rstd1, s_xn1 = (
            sem(n) for n in ("eps_ready", "wkT_zeros_ready", "a_ready", "zeros_ready", "bv_rep_ready",
                             "variance1_ready", "rstd1_ready", "xn1_ready"))
        filled = [sem("bank0_filled"), sem("bank1_filled")]
        emptied = [sem("bank0_emptied"), sem("bank1_emptied")]
        s_scores, s_negmax, s_exp, s_inv, s_probs = (
            sem(n) for n in ("scores_ready", "neg_max_ready", "exp_done", "inv_sum_ready", "probs_ready"))
        s_tp, s_pT, s_z, s_zT, s_lastT = (
            sem(n) for n in ("probs_transposed", "pT_ready", "z_summed", "zT_ready", "last_pT_ready"))
        s_mv3, s_rstd3, s_xn3 = (sem(n) for n in ("variance3_ready", "rstd3_ready", "xn3_ready"))
        s_mv2, s_rstd2, s_xn2, s_negabs, s_spl, s_delta, s_du, s_y0, s_x1b = (
            sem(n) for n in ("variance2_ready", "rstd2_ready", "xn2_ready", "neg_abs_ready", "softplus_ln_ready",
                             "delta_ready", "du_ready", "skip_ready", "x1b_ready"))
        s_trib, s_arg, s_decay, s_inv_decay, s_driven, s_error, s_scanned = (
            sem(n) for n in ("tri_b_ready", "decay_log_ready", "decay_ready", "inv_decay_ready", "driven_ready",
                             "decay_error_ready", "chunk_scanned"))
        s_dve, s_act, s_pool = sem("vector_chain"), sem("scalar_chain"), sem("gpsimd_chain")

        def walk(parts, section, t, v):
            sl = Slots(section, t)
            for name in ORDER[section]:
                late = section == "last" or (section == "body" and name in LATE)
                kind = name.rstrip("0123456789")
                if kind in parts:
                    parts[kind](sl, v if late else t, int(name[len(kind):] or 0))

        def wait_filled(eng, sl, name):
            bank, before = sl.at(name)
            eng.wait_ge(filled[bank], before + 1)
            return ps_m[bank], emptied[bank]

        def wait_copied(eng, sl, *names):
            for name in names:
                bank, before = sl.at(name)
                eng.wait_ge(emptied[bank], before + 1)

        def unit(t, u):
            return t * UNITS + u

        k0, k1, k2, s_cols, s_mlp_in = mlp.k0, mlp.k1, mlp.k2, mlp.s_cols, mlp.loaded
        w0, w1 = mlp.w0, mlp.w1

        block = stack.enter_context(nc.Block())

        @block.sync
        def _(sp):
            sp.dma_start(cst[:], consts).then_inc(s_cst, 16)
            sp.dma_start(x_all[:], x_rows).then_inc(s_x, 16)
            sp.dma_start(wk_raw, chunks(Wk)).then_inc(s_wk, 16)
            sp.dma_start(wv[:], chunks(Wv)).then_inc(s_wv, 16)
            sp.dma_start(wo[:], chunks(Wo)).then_inc(s_wo, 16)
            sp.dma_start(wq[:], chunks(Wq)).then_inc(s_wq, 16)
            for b in range(TB):
                sp.dma_start(ctx_t[b][:], ctx[b, 0:2 * P, :].rearrange("(k p) d -> p k d", p=P)).then_inc(s_ctx[b], 16)
            sp.dma_start(scan_flat[:, 0:D * NS], row(A_log.rearrange("d n -> (d n)")).partition_broadcast(P)) \
                .then_inc(s_alog, 16)
            sp.dma_start(wx[:], chunks(W_x)).then_inc(s_scanw, 16)
            sp.dma_start(wdt[0:RANK, :], W_dt).then_inc(s_scanw, 16)
            sp.dma_start(wdt[RANK:RANK + 1, :], row(b_dt)).then_inc(s_scanw, 16)
            sp.dma_start(wout[:], chunks(W_out)).then_inc(s_scanw, 16)
            for dst, src in ((k0, mlp_dram[0]), (k1, mlp_dram[1]), (k2, mlp_dram[2])):
                sp.dma_start(dst[:], chunks(src)).then_inc(s_mlp_in, 16)
            for i in range(3):
                sp.dma_start(s_cols[:, i:i + 1], row(mlp_dram[3 + i]).partition_broadcast(P)).then_inc(s_mlp_in, 16)
            wait_copied(sp, Slots("setup"), f"vo{IC // 2 - 2}", f"vo{IC // 2 - 1}")
            for t in range(T):
                for e in range(2):
                    sp.dma_start(last_vo[e:TB * H:2, t, :], vo_rows[e * B + TB * t:e * B + TB * t + TB]) \
                        .then_inc(s_vo, 16)
            with sp.Fori(1, T) as t:
                for b in range(TB):
                    sp.wait_ge(s_z, unit(t - 1, 2 * b) + 2)
                    sp.dma_start(ctx_t[b][:], ctx[t * TB + b, 0:2 * P, :].rearrange("(k p) d -> p k d", p=P)) \
                        .then_inc(s_ctx[b], 16)
            with sp.Fori(0, BLOCKS) as i:
                mlp_stores(sp, mlp, out, i)
            for j in range(2):
                sp.wait_ge(mlp.stored0 if j == 0 else mlp.stored1, 16 * BLOCKS)

        @block.gpsimd
        def _(pool):
            pool.memset(eps_col[:, 0:1], EPS)
            pool.memset(eps_col[:, 1:2], SCAN_EPS).then_inc(s_eps, 1)
            pool.memset(wkT[:, H // 2:H, :], 0.0).then_inc(s_zero_wk, 1)
            pool.dma_start(last_rows, ctx[:, SK - 1, :]).then_inc(s_lastc, 16)
            pool.dma_start(bqT[:], bq.rearrange("(c p) -> p c", p=P), allow_slow_non_contiguous=True) \
                .then_inc(s_small, 16)
            pool.dma_start(bvT[:], bv.rearrange("(c p) -> p c", p=P), allow_slow_non_contiguous=True) \
                .then_inc(s_small, 16)
            pool.dma_start(bo_row[:], row(bo)).then_inc(s_small, 16)
            pool.dma_start(bout[:], row(b_out).partition_broadcast(P)).then_inc(s_rows, 16)
            pool.dma_start(dskip[:], row(D_skip).partition_broadcast(P)).then_inc(s_rows, 16)
            pool.memset(last_vT, 0.0)
            pool.memset(dT[:], 1.0)
            pool.memset(ones_row[:], 1.0).then_inc(s_zero, 1)
            pool.wait_ge(s_cst, 16)
            pool.wait_ge(s_small, 48)
            pool.tensor_copy(bv_rep, spread(bvT[:], 2, P)).then_inc(s_bvrep, 1)

            def normalise(sl, t, u):
                g = unit(t, u)
                pr = probs[u % 2]
                pool.wait_ge(s_inv, g + 1)
                pool.tensor_tensor(pr[:], pr[:], spread(inv_sum[:, u % 2, :], 2, SK), ALU.mult) \
                    .then_inc(s_pool, 1)
                if u == 0 and "last" in sl.names:
                    wait_filled(pool, sl, "last")
                pool.wait_ge(s_pool, g + 1)
                pool.tensor_tensor(last_p[:, 2 * u:2 * u + 2, :], pr[:, :, SK - 1:SK].to_broadcast([P, 2, L]),
                                   spread(lat_sel, 1, 2), ALU.mult).then_inc(s_probs, 1)

            def prepare_chunk(sl, v, c):
                if c >= 2:
                    wait_filled(pool, sl, f"num{2 * c - 3}")
                    pool.wait_ge(s_error, v * 4 + c - 1)
                if c == 0:
                    wait_copied(pool, sl, "BC")
                pool.tensor_tensor(tri_b[:, c % 2], spread(tri_incl, 1, 4),
                                   spread(bc[:, 4 * c:4 * c + 4], 2, P), ALU.mult).then_inc(s_trib, 1)
                if c == 0:
                    wait_copied(pool, sl, "R")
                pool.tensor_tensor(decay[:, c % 2], a_all[:, 4 * c:4 * c + 4, :],
                                   spread(later[:], 1, 4), ALU.mult).then_inc(s_arg, 1)

            def skip_path(sl, v, _):
                pool.wait_ge(s_xn2, v + 1)
                pool.tensor_tensor(y[:], xn2[:], dskip[:], ALU.mult).then_inc(s_y0, 1)

            def delta_u(sl, v, _):
                pool.wait_ge(s_delta, v + 1)
                pool.tensor_tensor(du[:], delta[:], xn2[:], ALU.mult).then_inc(s_du, 1)

            def convert_w2(sl, v, _):
                pool.wait_ge(s_z, T * UNITS)
                pool.wait_ge(s_mlp_in, 96)
                pool.tensor_scalar(mlp.w2[:], k2[:], 2.0, -1.0, ALU.mult, ALU.add).then_inc(mlp.w2_ready, 1)

            parts = {"low": lambda sl, v, k: mlp_low(pool, mlp, k // HS, k % HS), "w2_": convert_w2,
                     "norm": normalise, "prep": prepare_chunk, "layernorm": skip_path, "dt": delta_u}
            walk(parts, "first", 0, None)
            pool.wait_ge(s_a, 1)
            pool.wait_ge(s_rows, 32)
            with pool.Fori(1, T) as t:
                walk(parts, "body", t, t - 1)
            walk(parts, "last", None, T - 1)
            with pool.Fori(2, BLOCKS) as i:
                for k in range(HS):
                    mlp_low(pool, mlp, i, k)

        @block.tensor
        def _(pe):
            def fill(sl, name):
                bank, before = sl.at(name)
                if not (isinstance(before, int) and before == 0):
                    pe.wait_ge(emptied[bank], before)
                return ps_m[bank], filled[bank]

            def two(dst, lhs, rhs):
                pe.matmul(dst, lhs(0), rhs(0), start=True, stop=False)
                return pe.matmul(dst, lhs(1), rhs(1), start=False, stop=True)

            def setup():
                sl = Slots("setup")
                pe.wait_ge(s_cst, 16)
                pe.wait_ge(s_wk, 16)
                for i in range(4):
                    ps, done = fill(sl, f"wk{i}")
                    for j in range(2):
                        for c in range(DC):
                            last = pe.transpose(ps[:, (2 * j + c) * P:(2 * j + c + 1) * P],
                                                wk_raw[:, c, (2 * i + j) * P:(2 * i + j + 1) * P], ident)
                    last.then_inc(done, 1)
                for i in range(T // 2):
                    pe.wait_ge(s_xn1, 2 * i + 2)
                    ps, done = fill(sl, f"x{i}")
                    for j in range(2):
                        for c in range(DC):
                            last = pe.transpose(ps[:, (2 * c + j) * P:(2 * c + j + 1) * P],
                                                xn1[:, 2 * i + j, c * P:(c + 1) * P], ident)
                    last.then_inc(done, 1)
                pe.wait_ge(s_lastc, 16)
                ps, done = fill(sl, "lastc")
                for c in range(DC):
                    last = pe.transpose(ps[:, c * B:(c + 1) * B], last_rows[:, c * P:(c + 1) * P], ident[0:B, 0:B])
                last.then_inc(done, 1)
                pe.wait_ge(s_wv, 16)
                wait_copied(pe, sl, "lastc")
                ps, done = fill(sl, "vl")
                for c in range(IC):
                    last = two(ps[:, c * B:(c + 1) * B], lambda k: wv[:, k, c * P:(c + 1) * P],
                               lambda k: last_ctxT[:, k, :])
                last.then_inc(done, 1)
                pe.wait_ge(s_wo, 16)
                wait_copied(pe, sl, "vl")
                for i in range(IC // 2):
                    ps, done = fill(sl, f"vo{i}")
                    for j in range(2):
                        c = 2 * i + j
                        last = pe.matmul(ps[0:2 * B, j * D:(j + 1) * D], last_vT[:, c].rearrange("p e b -> p (e b)"),
                                         wo[:, c, :], start=True, stop=True)
                    last.then_inc(done, 1)
                pe.wait_ge(s_bvrep, 1)
                ps, done = fill(sl, "bias")
                for c in range(IC):
                    pe.matmul(ps[:, 0:D], bv_rep[:, c, :], wo[:, c, :], start=(c == 0), stop=False)
                pe.matmul(ps[:, 0:D], ones_row[:], bo_row[:], start=False, stop=True).then_inc(done, 1)

            def context_transposes(sl, t, b):
                pe.wait_ge(s_ctx[b], (t + 1) * 16)
                ps, done = fill(sl, f"ctxT{b}")
                for k in range(DC):
                    for c in range(DC):
                        last = pe.transpose(ps[:, (2 * c + k) * P:(2 * c + k + 1) * P],
                                            ctx_t[b][:, k, c * P:(c + 1) * P], ident)
                last.then_inc(done, 1)

            def queries(sl, t, i):
                ps, done = fill(sl, f"q{i}")
                for j in range(4):
                    c = 4 * i + j
                    last = two(ps[:, j * P:(j + 1) * P], lambda k: wq[:, k, c * P:(c + 1) * P],
                               lambda k: xn1T[:, k, t, :])
                last.then_inc(done, 1)

            def query_keys(sl, t, i):
                if i % 4 == 0:
                    wait_copied(pe, sl, f"q{i // 4}")
                ps, done = fill(sl, f"qk{i}")
                for j in range(2):
                    for c in range(DC):
                        dst = ps[:, 2 * c * P:2 * (c + 1) * P].rearrange("p (b j q) -> p b j q", b=TB, j=2)[:, :, j, :]
                        last = pe.matmul(dst, wkT[:, 2 * i + j, c * P:(c + 1) * P],
                                         qT[:, i, :].rearrange("p (b q) -> p b q", b=TB), start=True, stop=True)
                last.then_inc(done, 1)

            def scores(sl, t, u):
                g, b = unit(t, u), u // 2
                if u == 0:
                    wait_copied(pe, sl, "qk6", "qk7")
                if u % 2 == 0:
                    wait_copied(pe, sl, f"ctxT{b}")
                if not isinstance(g, int) or g >= 2:
                    pe.wait_ge(s_exp, g - 1)
                for gi in range(2):
                    last = two(ps_s[:, u % 2, gi, 0:SK], lambda k: qkT[:, k, 2 * (u % 2) + gi, b, :],
                               lambda k: ctxT[b % 2][:, k, :])
                last.then_inc(s_scores, 1)

            def probs_transposes(sl, t, u):
                g = unit(t, u)
                pe.wait_ge(s_probs, g + 1)
                if not isinstance(g, int) or g >= 1:
                    pe.wait_ge(s_pT, g)
                for k in range(DC):
                    for gi in range(2):
                        last = pe.transpose(ps_t[:, k, gi * P:(gi + 1) * P],
                                            probs[u % 2][:, gi, k * P:(k + 1) * P], ident)
                last.then_inc(s_tp, 1)

            def weighted_context(sl, t, u):
                g, b = unit(t, u), u // 2
                pe.wait_ge(s_pT, g + 1)
                if not isinstance(g, int) or g >= 1:
                    pe.wait_ge(s_zT, g)
                for c in range(DC):
                    last = two(ps_z[:, c, :], lambda k: ctx_t[b][:, k, c * P:(c + 1) * P], lambda k: pT[u % 2][:, k, :])
                last.then_inc(s_z, 1)

            def heads_outputs(sl, v, i):
                pe.wait_ge(s_zT, unit(v, UNITS - 2) + 1 + i)
                ps, done = fill(sl, f"oT{i}")
                for j in range(4):
                    for e in range(2):
                        h = 2 * (4 * i + j) + e
                        last = two(ps[e * E:(e + 1) * E, j * P:(j + 1) * P],
                                   lambda k: wv[:, k, h * E:(h + 1) * E], lambda k: zT[:, k, h, :])
                last.then_inc(done, 1)

            def last_rows_part(sl, v, _):
                ps, done = fill(sl, "last")
                pe.matmul(ps[0:TB * H, :], head_sel, last_p[:], start=True, stop=True).then_inc(done, 1)

            def output_projection(sl, v, _):
                ps, done = fill(sl, "wo")
                for c in range(IC):
                    if c % 4 == 0:
                        wait_copied(pe, sl, f"oT{c // 4}")
                    pe.matmul(ps[:, 0:D], oT[:, c, :], wo[:, c, :], start=(c == 0), stop=False)
                pe.wait_ge(s_lastT, v + 1)
                pe.matmul(ps[:, 0:D], last_pT[:], last_vo[:, v, :], start=False, stop=True).then_inc(done, 1)

            def xn2_transposes(sl, v, _):
                pe.wait_ge(s_xn2, v + 1)
                ps, done = fill(sl, "xnT")
                for c in range(DC):
                    last = pe.transpose(ps[:, c * P:(c + 1) * P], xn2[:, c * P:(c + 1) * P], ident)
                last.then_inc(done, 1)

            def delta_rows(sl, v, _):
                wait_copied(pe, sl, "xnT")
                ps, done = fill(sl, "dT")
                two(ps[0:RANK, 0:P], lambda k: wx[:, k, 0:RANK], lambda k: xn2T[:, k, :]).then_inc(done, 1)

            def b_and_c(sl, v, _):
                ps, done = fill(sl, "BC")
                two(ps[:, 0:2 * NS], lambda k: xn2T[:, k, :], lambda k: wx[:, k, RANK:RANK + 2 * NS]) \
                    .then_inc(done, 1)

            def delta_product(sl, v, _):
                wait_copied(pe, sl, "dT")
                ps, done = fill(sl, "dt")
                pe.matmul(ps[:, 0:D], dT[:], wdt[:], start=True, stop=True).then_inc(done, 1)

            def later_deltas(sl, v, _):
                pe.wait_ge(s_delta, v + 1)
                ps, done = fill(sl, "R")
                pe.matmul(ps[:, 0:D], tri_after, delta[:], start=True, stop=True).then_inc(done, 1)

            def numerators(sl, v, i):
                c = i // 2
                if i % 2 == 0:
                    pe.wait_ge(s_trib, v * 4 + c + 1)
                    pe.wait_ge(s_driven, v * 4 + c + 1)
                ps, done = fill(sl, f"num{i}")
                for j in range(2):
                    n = 2 * (i % 2) + j
                    last = pe.matmul(ps[:, j * D:(j + 1) * D], tri_b[:, c % 2, n, :], driven[:, n, :],
                                     start=True, stop=True)
                last.then_inc(done, 1)

            def y_transposes(sl, v, _):
                pe.wait_ge(s_scanned, v * 4 + 4)
                ps, done = fill(sl, "yT")
                for c in range(DC):
                    last = pe.transpose(ps[:, c * P:(c + 1) * P], y[:, c * P:(c + 1) * P], ident)
                last.then_inc(done, 1)

            def scan_output(sl, v, _):
                wait_copied(pe, sl, "yT")
                ps, done = fill(sl, "out")
                two(ps[:, 0:D], lambda k: yT[:, k, :], lambda k: wout[:, k, :]).then_inc(done, 1)

            def xn3_transposes(sl, v, _):
                pe.wait_ge(s_xn3, v + 1)
                ps, done = fill(sl, "x3T")
                for c in range(DC):
                    last = pe.transpose(ps[:, c * P:(c + 1) * P], xn2[:, c * P:(c + 1) * P], ident)
                last.then_inc(done, 1)

            def mlp_hidden(sl, v, k):
                if k % HS == 0:
                    pe.wait_ge(mlp.weights_ready, 1)
                    pe.wait_ge(mlp.xT_lo_ready, k // HS + 1)
                if k == HS // 2:
                    pe.wait_ge(mlp.weights_ready, 1 + FC)
                mlp_layer(pe, mlp, k // HS, k % HS)

            def mlp_outputs(sl, v, _):
                pe.wait_ge(mlp.w2_ready, 1)
                mlp_last_layer(pe, mlp, 0)

            parts = {"hidden": mlp_hidden, "mlpout": mlp_outputs, "x3T": xn3_transposes,
                     "ctxT": context_transposes, "q": queries, "qk": query_keys, "scores": scores,
                     "turn": probs_transposes, "sum": weighted_context, "oT": heads_outputs, "last": last_rows_part,
                     "wo": output_projection, "xnT": xn2_transposes, "dT": delta_rows, "BC": b_and_c,
                     "dt": delta_product,
                     "R": later_deltas, "num": numerators, "yT": y_transposes, "out": scan_output}
            setup()
            wait_copied(pe, Slots("setup"), "wk2", "wk3", f"x{T // 2 - 2}", f"x{T // 2 - 1}")
            pe.wait_ge(s_wq, 16)
            walk(parts, "first", 0, None)
            pe.wait_ge(s_vo, 2 * 16 * T)
            pe.wait_ge(s_scanw, 64)
            with pe.Fori(1, T) as t:
                walk(parts, "body", t, t - 1)
            walk(parts, "last", None, T - 1)
            pe.wait_ge(mlp.xT_lo_ready, BLOCKS)
            with pe.Fori(2, BLOCKS) as i:
                for k in range(HS // 2):
                    mlp_layer(pe, mlp, i, k)
                mlp_last_layer(pe, mlp, i - 1)
                for k in range(HS // 2, HS):
                    mlp_layer(pe, mlp, i, k)
            mlp_last_layer(pe, mlp, BLOCKS - 1)

        @block.scalar
        def _(act):
            link = Chain(s_act, act)

            act.preload_act_table_set("natural_log_exp_and_others")

            def setup():
                sl = Slots("setup")
                act.wait_ge(s_eps, 1)
                act.wait_ge(s_mv1, 1)
                link(act.activation(lnv1[:], mv1[:, :, 1], ACT.Ln, bias=eps_col[:, 0:1]))
                act.activation(rstd1[:], lnv1[:], ACT.Exp, scale=-0.5).then_inc(s_rstd1, 1)
                act.wait_ge(s_zero_wk, 2)
                for i in range(4):
                    ps, done = wait_filled(act, sl, f"wk{i}")
                    for e in range(2):
                        dst = wkT[e * E:(e + 1) * E, 4 * i:4 * i + 4, :] \
                            .rearrange("p (j e) d -> p j e d", e=2)[:, :, e, :]
                        last = act.activation(dst, ps[e * E:(e + 1) * E, :].rearrange("p (j d) -> p j d", j=2),
                                              ACT.Copy, scale=float(E) ** -0.5)
                    last.then_inc(done, 1)

            def context_copy(sl, t, b):
                ps, done = wait_filled(act, sl, f"ctxT{b}")
                act.copy(ctxT[b % 2][:, :, SK - 1], last_ctxT[:, :, t * TB + b])
                act.copy(ctxT[b % 2][:, :, 0:2 * P], ps[:].rearrange("p (c n) -> p c n", c=DC)).then_inc(done, 1)

            def query_keys_copy(sl, t, i):
                ps, done = wait_filled(act, sl, f"qk{i}")
                act.copy(qkT[:, :, i // 2, :, 2 * (i % 2) * L:2 * (i % 2 + 1) * L],
                         ps[:].rearrange("p (c b n) -> p c b n", c=DC, b=TB)) \
                    .then_inc(done, 1)

            def exponentials(sl, t, u):
                g = unit(t, u)
                act.wait_ge(s_negmax, g + 1)
                if not isinstance(g, int) or g >= 2:
                    act.wait_ge(s_tp, g - 1)
                for gi in range(2):
                    last = act.activation(probs[u % 2][:, gi, :], ps_s[:, u % 2, gi, 0:SK], ACT.Exp,
                                          bias=neg_max[:, u % 2, gi:gi + 1], accum_out=row_sum[:, u % 2, gi:gi + 1])
                last.then_inc(s_exp, 1)

            def sums_copy(sl, t, u):
                g, b, h0 = unit(t, u), u // 2, HU * (u % 2)
                act.wait_ge(s_z, g + 1)
                act.copy(zT[:, :, h0:h0 + HU, b * L:(b + 1) * L],
                         ps_z[:].rearrange("p c (h q) -> p c h q", h=HU)).then_inc(s_zT, 1)

            def chunk_decay(sl, v, c):
                act.wait_ge(s_arg, v * 4 + c + 1)
                act.activation(decay[:, c % 2], decay[:, c % 2], ACT.Exp, scale=-1.0).then_inc(s_decay, 1)

            def chunk_inverse(sl, v, c):
                act.wait_ge(s_decay, v * 4 + c + 1)
                if c >= 2:
                    act.wait_ge(s_scanned, v * 4 + c - 1)
                link(act.activation(inv_decay[:, c % 2], decay[:, c % 2], ACT.Ln, bias=eps_col[:, 1:2]))
                act.activation(inv_decay[:, c % 2], inv_decay[:, c % 2], ACT.Exp, scale=-1.0).then_inc(s_inv_decay, 1)

            def inverse_deviation(sl, v, _):
                act.wait_ge(s_mv2, v + 1)
                link(act.activation(lnv2[:], mv2[:, 1:2], ACT.Ln, bias=eps_col[:, 0:1]))
                act.activation(rstd2[:], lnv2[:], ACT.Exp, scale=-0.5).then_inc(s_rstd2, 1)

            def softplus(sl, v, _):
                act.wait_ge(s_negabs, v + 1)
                link(act.activation(sp_e[:], sp_e[:], ACT.Exp))
                act.activation(sp_e[:], sp_e[:], ACT.Ln, bias=1.0).then_inc(s_spl, 1)

            def later_copy(sl, v, _):
                ps, done = wait_filled(act, sl, "R")
                act.copy(later[:], ps[:, 0:D]).then_inc(done, 1)

            def y_copy(sl, v, _):
                ps, done = wait_filled(act, sl, "yT")
                act.copy(yT[:].rearrange("p c n -> p (c n)"), ps[:, 0:D]).then_inc(done, 1)

            def inverse_deviation3(sl, v, _):
                act.wait_ge(s_mv3, v + 1)
                link(act.activation(lnv2[:], mv2[:, 1:2], ACT.Ln, bias=eps_col[:, 0:1]))
                act.activation(rstd2[:], lnv2[:], ACT.Exp, scale=-0.5).then_inc(s_rstd3, 1)

            def convert_w1(sl, v, c):
                if c == 0:
                    act.wait_ge(s_mlp_in, 96)
                if c == FC // 2:
                    wait_copied(act, sl, "wo")
                act.activation(w1[:, c, :], k1[:, c, :], ACT.Copy, scale=2.0, bias=-1.0).then_inc(mlp.weights_ready, 1)

            def mlp_rows_hi(sl, v, j):
                if j == 1:
                    act.wait_ge(mlp.hidden_summed, HS // 2)
                if j == 2:
                    act.wait_ge(s_arg, T * 4)
                if j == BLOCKS - 1:
                    wait_copied(act, sl, "x3T")
                act.copy(block_tiles(0, j), rowsT[:, :, 2 * j:2 * j + 2, :]).then_inc(mlp.xT_hi_ready, 1)

            parts = {"mlpx": mlp_rows_hi, "high": lambda sl, v, k: mlp_high(act, mlp, k // HS, k % HS),
                     "mlpnorm": inverse_deviation3, "w1_": convert_w1, "ctxT": context_copy, "qk": query_keys_copy,
                     "exp": exponentials, "copyZ": sums_copy,
                     "layernorm": inverse_deviation, "dt": softplus, "R": later_copy, "decay": chunk_decay,
                     "invert": chunk_inverse, "yT": y_copy}
            setup()
            walk(parts, "first", 0, None)
            act.wait_ge(s_alog, 16)
            for c in range(4):
                last = act.activation(a_all[:, 4 * c:4 * c + 4, :], a_log[:, 4 * c:4 * c + 4, :], ACT.Exp)
            last.then_inc(s_a, 1)
            with act.Fori(1, T) as t:
                link.enter(t, 7)
                walk(parts, "body", t, t - 1)
            link.leave(T - 1)
            walk(parts, "last", None, T - 1)
            with act.Fori(2, BLOCKS) as i:
                for k in range(HS):
                    mlp_high(act, mlp, i, k)

        @block.vector
        def _(dve):
            link = Chain(s_dve, dve)

            def setup():
                sl = Slots("setup")
                dve.memset(wkT[:, 0:H // 2, :], 0.0).then_inc(s_zero_wk, 1)
                dve.wait_ge(s_x, 16)
                for t in range(T):
                    last = dve.bn_stats(stats1[:, t, :], x_all[:, t, :])
                link(last)
                for t in range(T):
                    last = dve.bn_aggr(mv1[:, t, :], stats1[:, t, :])
                last.then_inc(s_mv1, 1)
                dve.wait_ge(s_rstd1, 1)
                for t in range(T):
                    dve.tensor_scalar(xn1[:, t, :], x_all[:, t, :], mv1[:, t, 0:1], rstd1[:, t:t + 1],
                                      ALU.subtract, ALU.mult).then_inc(s_xn1, 1)
                for i in range(T // 2):
                    ps, done = wait_filled(dve, sl, f"x{i}")
                    dve.tensor_copy(xn1T[:, :, 2 * i:2 * i + 2, :],
                                    ps[:].rearrange("p (c t n) -> p c t n", c=DC, t=2)).then_inc(done, 1)
                ps, done = wait_filled(dve, sl, "lastc")
                dve.tensor_copy(last_ctxT[:], ps[:, 0:DC * B].rearrange("p (c n) -> p c n", c=DC)).then_inc(done, 1)
                ps, done = wait_filled(dve, sl, "vl")
                dve.wait_ge(s_zero, 1)
                for e in range(2):
                    half = slice(e * E, (e + 1) * E)
                    last = dve.tensor_copy(last_vT[half, :, e, :],
                                           ps[half, 0:IC * B].rearrange("p (c n) -> p c n", c=IC))
                last.then_inc(done, 1)
                for i in range(IC // 2):
                    ps, done = wait_filled(dve, sl, f"vo{i}")
                    dve.tensor_copy(vo_rows[:, 2 * i:2 * i + 2, :],
                                    ps[0:2 * B, :].rearrange("p (j d) -> p j d", j=2)).then_inc(done, 1)
                ps, done = wait_filled(dve, sl, "bias")
                dve.tensor_copy(bias[:], ps[:, 0:D]).then_inc(done, 1)
                wait_copied(dve, sl, "bias")
                link(dve.tensor_tensor(x_all[:], x_all[:], spread(bias[:], 1, T), ALU.add))

            def queries_copy(sl, t, i):
                ps, done = wait_filled(dve, sl, f"q{i}")
                dve.tensor_tensor(qT[:, 4 * i:4 * i + 4, :], ps[:].rearrange("p (j n) -> p j n", j=4),
                                  spread(bqT[:, 4 * i:4 * i + 4], 2, P), ALU.add).then_inc(done, 1)

            def maxima(sl, t, u):
                g = unit(t, u)
                dve.wait_ge(s_scores, g + 1)
                dve.tensor_reduce(neg_max[:, u % 2, :], ps_s[:, u % 2, :, 0:SK], AX.X, ALU.max, negate=True) \
                    .then_inc(s_negmax, 1)

            def inverse_sums(sl, t, u):
                dve.wait_ge(s_exp, unit(t, u) + 1)
                dve.reciprocal(inv_sum[:, u % 2, :], row_sum[:, u % 2, :]).then_inc(s_inv, 1)

            def probs_copy(sl, t, u):
                dve.wait_ge(s_tp, unit(t, u) + 1)
                dve.tensor_copy(pT[u % 2][:], ps_t[:]).then_inc(s_pT, 1)

            def heads_copy(sl, v, i):
                ps, done = wait_filled(dve, sl, f"oT{i}")
                dve.tensor_copy(oT[:, 4 * i:4 * i + 4, :], ps[:].rearrange("p (j n) -> p j n", j=4)) \
                    .then_inc(done, 1)

            def last_rows_own(sl, v, _):
                ps, done = wait_filled(dve, sl, "last")
                dve.tensor_tensor(last_pm[:].rearrange("p b g q -> p (b g) q"),
                                  ps[0:TB * H, :].rearrange("p (k q) -> p k q", q=L),
                                  spread(own[0:TB * H, :], 2, L), ALU.mult).then_inc(done, 1)
                wait_copied(dve, sl, "last")
                dve.tensor_reduce(last_pT[:], last_pm[:].rearrange("p b g q -> p b q g"), AX.X, ALU.add) \
                    .then_inc(s_lastT, 1)

            def attended(sl, v, _):
                ps, done = wait_filled(dve, sl, "wo")
                dve.tensor_tensor(x1[:], ps[:, 0:D], x_all[:, v, :], ALU.add).then_inc(done, 1)

            def layernorm(sl, v, _):
                wait_copied(dve, sl, "wo")
                link(dve.bn_stats(stats2[:], x1[:]))
                dve.tensor_tensor(x1b[:], x1[:], bout[:], ALU.add).then_inc(s_x1b, 1)
                dve.bn_aggr(mv2[:], stats2[:]).then_inc(s_mv2, 1)
                dve.wait_ge(s_mv2, v + 1)
                dve.wait_ge(s_rstd2, v + 1)
                dve.tensor_scalar(xn2[:], x1[:], mv2[:, 0:1], rstd2[:, 0:1], ALU.subtract, ALU.mult) \
                    .then_inc(s_xn2, 1)

            def xn2_copy(sl, v, _):
                ps, done = wait_filled(dve, sl, "xnT")
                dve.tensor_copy(xn2T[:].rearrange("p c n -> p (c n)"), ps[:, 0:D]).then_inc(done, 1)

            def delta_rows_copy(sl, v, _):
                ps, done = wait_filled(dve, sl, "dT")
                dve.tensor_copy(dT[0:RANK, :], ps[0:RANK, 0:P]).then_inc(done, 1)

            def b_and_c_copy(sl, v, _):
                ps, done = wait_filled(dve, sl, "BC")
                dve.tensor_copy(bc[:], ps[:, 0:2 * NS]).then_inc(done, 1)

            def softplus(sl, v, _):
                ps, done = wait_filled(dve, sl, "dt")
                dve.tensor_copy(sp_x[:], ps[:, 0:D]).then_inc(done, 1)
                wait_copied(dve, sl, "dt")
                dve.scalar_tensor_tensor(sp_e[:], sp_x[:], -1.0, sp_x[:], ALU.mult, ALU.min).then_inc(s_negabs, 1)
                dve.wait_ge(s_spl, v + 1)
                dve.scalar_tensor_tensor(delta[:], sp_x[:], 0.0, sp_e[:], ALU.max, ALU.add).then_inc(s_delta, 1)

            def drive(sl, v, c):
                if c == 0:
                    dve.wait_ge(s_du, v + 1)
                else:
                    wait_filled(dve, sl, f"num{2 * c - 1}")
                dve.wait_ge(s_decay, v * 4 + c + 1)
                dve.tensor_tensor(driven, decay[:, c % 2], spread(du[:], 1, 4), ALU.mult).then_inc(s_driven, 1)

            def newton(sl, v, c):
                dve.wait_ge(s_inv_decay, v * 4 + c + 1)
                dve.scalar_tensor_tensor(error, decay[:, c % 2], SCAN_EPS, inv_decay[:, c % 2],
                                         ALU.add, ALU.mult).then_inc(s_error, 1)
                dve.wait_ge(s_error, v * 4 + c + 1)
                link(dve.scalar_tensor_tensor(inv_decay[:, c % 2], error, 2.0, inv_decay[:, c % 2],
                                              ALU.subtract, ALU.mult))

            def numerators(sl, v, i):
                ps, done = wait_filled(dve, sl, f"num{i}")
                c = i // 2
                for j in range(2):
                    n = 2 * (i % 2) + j
                    last = dve.scalar_tensor_tensor(inv_decay[:, c % 2, n, :], ps[:, j * D:(j + 1) * D],
                                                    bc[:, NS + 4 * c + n:NS + 4 * c + n + 1],
                                                    inv_decay[:, c % 2, n, :], ALU.mult, ALU.mult)
                last.then_inc(done, 1)

            def part_of_y(sl, v, c):
                wait_copied(dve, sl, f"num{2 * c + 1}")
                link(dve.tensor_reduce(y_part[:], inv_decay[:, c % 2].rearrange("p n d -> p d n"), AX.X, ALU.add))
                if c == 0:
                    dve.wait_ge(s_y0, v + 1)
                else:
                    dve.wait_ge(s_scanned, v * 4 + c)
                dve.tensor_tensor(y[:], y[:], y_part[:], ALU.subtract).then_inc(s_scanned, 1)

            def scanned(sl, v, _):
                ps, done = wait_filled(dve, sl, "out")
                dve.wait_ge(s_x1b, v + 1)
                link(dve.tensor_tensor(x2[:], ps[:, 0:D], x1b[:], ALU.add))
                link(dve.bn_stats(stats2[:], x2[:]))
                dve.tensor_tensor(x_all[:, v, :], ps[:, 0:D], x1b[:], ALU.add).then_inc(done, 1)

            def layernorm3(sl, v, _):
                dve.bn_aggr(mv2[:], stats2[:]).then_inc(s_mv3, 1)
                dve.wait_ge(s_mv3, v + 1)
                dve.wait_ge(s_rstd3, v + 1)
                dve.tensor_scalar(xn2[:], x2[:], mv2[:, 0:1], rstd2[:, 0:1], ALU.subtract, ALU.mult) \
                    .then_inc(s_xn3, 1)

            def xn3_copy(sl, v, _):
                ps, done = wait_filled(dve, sl, "x3T")
                dve.tensor_copy(xn3T[:, :, v, :], ps[:, 0:D].rearrange("p (c n) -> p c n", c=DC)).then_inc(done, 1)

            def convert_w0(sl, v, _):
                dve.wait_ge(s_mlp_in, 96)
                dve.tensor_tensor(w0[:], k0[:, 0:DC, :], k0[:, DC:2 * DC, :], ALU.subtract) \
                    .then_inc(mlp.weights_ready, 1)
                dve.tensor_scalar(mlp.s_two[:, 0:1], s_cols[:, 0:1], 4.0, None, ALU.mult).then_inc(mlp.scales_ready, 1)
                dve.tensor_scalar(mlp.s_two[:, 1:2], s_cols[:, 1:2], 2.0, None, ALU.mult).then_inc(mlp.scales_ready, 1)
                dve.wait_ge(mlp.scales_ready, 2)

            def mlp_rows_lo(sl, v, j):
                dve.wait_ge(mlp.xT_hi_ready, j + 1)
                if j == BLOCKS - 1:
                    wait_copied(dve, sl, "x3T")
                dve.tensor_tensor(block_tiles(1, j), rowsT[:, :, 2 * j:2 * j + 2, :],
                                  block_tiles(0, j).bitcast(F32), ALU.subtract).then_inc(mlp.xT_lo_ready, 1)

            parts = {"mlpx": mlp_rows_lo, "relu": lambda sl, v, k: mlp_relu(dve, mlp, k // HS, k % HS),
                     "mlpsum": lambda sl, v, k: mlp_results(dve, mlp, 0), "mlpnorm": layernorm3, "x3T": xn3_copy,
                     "w": convert_w0, "q": queries_copy, "max": maxima, "copyP": probs_copy, "inv": inverse_sums,
                     "oT": heads_copy,
                     "last": last_rows_own, "wo": attended, "layernorm": layernorm, "xnT": xn2_copy,
                     "dT": delta_rows_copy, "BC": b_and_c_copy, "dt": softplus, "drive": drive, "newton": newton,
                     "num": numerators, "part": part_of_y, "out": scanned}
            setup()
            walk(parts, "first", 0, None)
            dve.wait_ge(s_rows, 32)
            with dve.Fori(1, T) as t:
                link.enter(t, 11)
                walk(parts, "body", t, t - 1)
            link.leave(T - 1)
            walk(parts, "last", None, T - 1)
            with dve.Fori(2, BLOCKS) as i:
                for k in range(HS // 2):
                    mlp_relu(dve, mlp, i, k)
                mlp_results(dve, mlp, i - 1)
                for k in range(HS // 2, HS):
                    mlp_relu(dve, mlp, i, k)
            mlp_results(dve, mlp, BLOCKS - 1)


NB = 2 * P
BLOCKS = T // 2
HB = 4
HS = FC




def past_first(i):
    return not isinstance(i, int) or i >= 1


def mlp_layer(pe, m, i, k):
    if k >= HB or past_first(i):
        pe.wait_ge(m.hidden_whole, i * HS + k - HB + 1)
    first_layer = k < HS // 2
    for j in range(2):
        f = 2 * (k % (HS // 2)) + j
        n = 0
        if first_layer:
            for lo in range(2):
                for c in range(DC):
                    last = pe.matmul(m.banks[k % HB][:, j, :], m.w0[:, c, f * P:(f + 1) * P], m.x_rows(lo, c, i),
                                     start=(n == 0), stop=(n == 2 * DC - 1))
                    n += 1
        else:
            for c in range(FC):
                if c % 2 == 0 and k == HS // 2 and j == 0:
                    pe.wait_ge(m.hidden_lo_ready, i * HS + c // 2 + 1)
                for part in (m.h1_hi, m.h1_lo):
                    last = pe.matmul(m.banks[k % HB][:, j, :], m.w1[:, c, f * P:(f + 1) * P], part[:, c, :],
                                     start=(n == 0), stop=(n == 2 * FC - 1))
                    n += 1
    last.then_inc(m.hidden_summed, 1)


def mlp_last_layer(pe, m, i):
    for c in range(FC):
        if c % 2 == 0:
            pe.wait_ge(m.hidden_lo_ready, i * HS + HS // 2 + c // 2 + 1)
        for j in range(2):
            if c == 0 and past_first(i):
                pe.wait_ge(m.outputs0_ready if j == 0 else m.outputs1_ready, i)
            for part in (m.h2_hi, m.h2_lo):
                last = pe.matmul(m.out_banks[j], part[:, c, j * P:(j + 1) * P], m.w2[:, c, :],
                                 start=(c == 0 and part is m.h2_hi), stop=(c == FC - 1 and part is m.h2_lo))
            if c == FC - 1:
                last.then_inc(m.outputs_summed, 1)


def mlp_relu(dve, m, i, k):
    dve.wait_ge(m.hidden_summed, i * HS + k + 1)
    if k >= 2 or past_first(i):
        dve.wait_ge(m.hidden_lo_ready, i * HS + k - 1)
    layer = 0 if k < HS // 2 else 1
    dve.tensor_scalar(m.whole[k % 2], m.banks[k % HB], m.s_two[:, layer:layer + 1], 0.0,
                      ALU.mult, ALU.max).then_inc(m.hidden_whole, 1)


def hidden_halves(m, k):
    hi, lo = (m.h1_hi, m.h1_lo) if k < HS // 2 else (m.h2_hi, m.h2_lo)
    j = 2 * (k % (HS // 2))
    return hi[:, j:j + 2, :], lo[:, j:j + 2, :]


def mlp_high(act, m, i, k):
    act.wait_ge(m.hidden_whole, i * HS + k + 1)
    act.copy(hidden_halves(m, k)[0], m.whole[k % 2]).then_inc(m.hidden_hi_ready, 1)


def mlp_low(pool, m, i, k):
    pool.wait_ge(m.hidden_hi_ready, i * HS + k + 1)
    hi, lo = hidden_halves(m, k)
    pool.tensor_tensor(lo, m.whole[k % 2], hi.bitcast(F32), ALU.subtract).then_inc(m.hidden_lo_ready, 1)


def mlp_results(dve, m, i):
    for j in range(2):
        dve.wait_ge(m.outputs_summed, 2 * i + j + 1)
        if past_first(i):
            dve.wait_ge(m.stored0 if j == 0 else m.stored1, 16 * i)
        dve.scalar_tensor_tensor(m.y_out[:, j, :], m.out_banks[j], m.s_cols[:, 2:3], m.x_all[:, 2 * i + j, :],
                                 ALU.mult, ALU.add).then_inc(m.outputs0_ready if j == 0 else m.outputs1_ready, 1)


def mlp_stores(sp, m, out, i):
    out_rows = out.rearrange("(t b) l d -> (b l) t d", b=TB)
    for j in range(2):
        sp.wait_ge(m.outputs0_ready if j == 0 else m.outputs1_ready, i + 1)
        sp.dma_start(out_rows[:, 2 * i + j, :], m.y_out[:, j, :]).then_inc(m.stored0 if j == 0 else m.stored1, 16)


_INS = ["x", "ctx_1024", "L0_xattn_Wq", "L0_xattn_bq", "L0_xattn_Wk", "L0_xattn_bk", "L0_xattn_Wv", "L0_xattn_bv",
        "L0_xattn_Wo", "L0_xattn_bo", "L0_attn_W_x", "L0_attn_W_dt", "L0_attn_b_dt", "L0_attn_A_log", "L0_attn_D",
        "L0_attn_W_out", "L0_attn_b_out", "L0_ffn_k0", "L0_ffn_k1", "L0_ffn_k2", "L0_ffn_s0", "L0_ffn_s1",
        "L0_ffn_s2"]


def kernel(**inputs):
    import numpy as _np
    import concourse.bacc as _bacc
    from concourse import mybir as _mybir
    from concourse.bass_utils import run_bass_kernel_spmd as _run

    nc = _bacc.Bacc("TRN2", target_bir_lowering=False, num_devices=1)
    arrays = {"in_masks": host_constants()}
    for name in _INS:
        a = _np.ascontiguousarray(inputs[name])
        arrays[f"in_{name}"] = a.reshape(1) if a.ndim == 0 else a
    args = [nc.dram_tensor(n, a.shape, _mybir.dt.from_np(a.dtype), kind="ExternalInput").ap()
            for n, a in arrays.items()]
    args.append(nc.dram_tensor("out_x", (B, L, D), F32, kind="ExternalOutput").ap())
    perceiver_block(nc, *args)
    r = _run(nc, [arrays], core_ids=[0])
    return r.results[0]["out_x"]
```
